# Optimizing a Trainium2 kernel written in Bass

```python
import numpy as np
import jax
import jax.numpy as jnp

def _softmax(x, axis=-1):
    return jax.nn.softmax(x, axis=axis)

def _gelu(x):
    return jax.nn.gelu(x, approximate=True)

def _silu(x):
    return jax.nn.silu(x)

def _sigmoid(x):
    return jax.nn.sigmoid(x)

def _layernorm(x, axis=-1, eps=1e-05):
    m = jnp.mean(x, axis=axis, keepdims=True)
    v = jnp.var(x, axis=axis, keepdims=True)
    return (x - m) / jnp.sqrt(v + eps)

def _scatter_add(tgt, idx, src, axis=0):
    return tgt.at[idx].add(src)

def _segment_sum(src, seg, n):
    return jax.ops.segment_sum(src, seg, n)
kernel_name = 'mk_gnn_resnorm_d4_gnn_r8_0bbd6f'

def setup_inputs(seed: int=0):
    np.random.seed(seed)
    _w = jnp.asarray

    def _rec_inputs():
        import jax
        import jax.numpy as jnp
        _gk = jax.random.key(seed)
        x = -0.0008691 + 1 * jax.random.normal(jax.random.fold_in(_gk, 1), (12500, 128), jnp.float32)
        src = jax.random.randint(jax.random.fold_in(_gk, 2), (200000,), 0, 12500, jnp.int32)
        dst = jax.random.randint(jax.random.fold_in(_gk, 3), (200000,), 0, 12500, jnp.int32)
        _o = jnp.argsort(dst, stable=True)
        src = src[_o]
        dst = dst[_o]
        return (x, src, dst)
    x, src, dst = _rec_inputs()

    def _L0_gnn_setup():
        import jax, jax.numpy as jnp
        import numpy as np
        N_NODES = 1250
        N_EDGES = 80000
        D = 128

        def _mean_aggregate(x, src, dst, num_nodes):
            msg = x[src]
            summed = jax.ops.segment_sum(msg, dst, num_segments=num_nodes)
            cnt = jax.ops.segment_sum(jnp.ones_like(dst, dtype=x.dtype), dst, num_segments=num_nodes)
            return summed / jnp.maximum(cnt, 1.0)[:, None]

        def _sage_conv(x, src, dst, W_l, b, W_r, num_nodes):
            aggr = _mean_aggregate(x, src, dst, num_nodes)
            return aggr @ W_l + b + x @ W_r
        key = jax.random.key(seed)
        ks = jax.random.split(key, 8)
        s = 1.0 / np.sqrt(D)
        return {'node_fts': jax.random.normal(ks[0], (N_NODES, D), dtype=jnp.float32), 'edge_index': jax.random.randint(ks[1], (2, N_EDGES), 0, N_NODES, dtype=jnp.int64), 'W1_l': jax.random.normal(ks[2], (D, D), dtype=jnp.float32) * s, 'b1': jnp.zeros((D,), dtype=jnp.float32), 'W1_r': jax.random.normal(ks[3], (D, D), dtype=jnp.float32) * s, 'W2_l': jax.random.normal(ks[4], (D, D), dtype=jnp.float32) * s, 'b2': jnp.zeros((D,), dtype=jnp.float32), 'W2_r': jax.random.normal(ks[5], (D, D), dtype=jnp.float32) * s}
    _L0_gnn_all = _L0_gnn_setup()
    _L0_gnn_in = {k: v for k, v in _L0_gnn_all.items() if k in ('W1_l', 'b1', 'W1_r', 'W2_l', 'b2', 'W2_r')}
    del _L0_gnn_all

    def _L1_gnn_setup():
        import jax, jax.numpy as jnp
        import numpy as np
        N, E, D = (12500, 80000, 128)
        BN_EPS = 1e-05

        def _batchnorm(h, gamma, beta):
            mean = jnp.mean(h, axis=0)
            var = jnp.var(h, axis=0)
            return gamma * (h - mean) * jax.lax.rsqrt(var + BN_EPS) + beta
        key = jax.random.key(seed)
        ks = jax.random.split(key, 8)
        x = jax.random.normal(ks[0], (N, D), dtype=jnp.float32)
        edge_index = jax.random.randint(ks[1], (2, E), 0, N, dtype=jnp.int64)
        s = 1.0 / np.sqrt(D)
        W1 = jax.random.uniform(ks[2], (D, D), jnp.float32, -s, s)
        b1 = jax.random.uniform(ks[3], (D,), jnp.float32, -s, s)
        W2 = jax.random.uniform(ks[4], (D, D), jnp.float32, -s, s)
        b2 = jax.random.uniform(ks[5], (D,), jnp.float32, -s, s)
        return {'x': x, 'edge_index': edge_index, 'eps': jnp.array([0.1], dtype=jnp.float32), 'W1': W1, 'b1': b1, 'g1': jnp.ones((D,), jnp.float32), 'beta1': jnp.zeros((D,), jnp.float32), 'W2': W2, 'b2': b2, 'g2': jnp.ones((D,), jnp.float32), 'beta2': jnp.zeros((D,), jnp.float32)}
    _L1_gnn_all = _L1_gnn_setup()
    _L1_gnn_in = {k: v for k, v in _L1_gnn_all.items() if k in ('eps', 'W1', 'b1', 'g1', 'beta1', 'W2', 'b2', 'g2', 'beta2')}
    del _L1_gnn_all

    def _L2_gnn_setup():
        import jax, jax.numpy as jnp
        import numpy as np
        N_NODES = 1250
        N_EDGES = 80000
        IN_CH = 128
        OUT_CH = 128
        key = jax.random.key(seed)
        k1, k2, k3, k4 = jax.random.split(key, 4)
        x = jax.random.normal(k1, (N_NODES, IN_CH), dtype=jnp.float32)
        edge_index = jax.random.randint(k2, (2, N_EDGES), 0, N_NODES, dtype=jnp.int64)
        bound = 1.0 / np.sqrt(2 * IN_CH)
        W = jax.random.uniform(k3, (OUT_CH, 2 * IN_CH), dtype=jnp.float32, minval=-bound, maxval=bound)
        b = jax.random.uniform(k4, (OUT_CH,), dtype=jnp.float32, minval=-bound, maxval=bound)
        return {'x': x, 'W': W, 'b': b, 'edge_index': edge_index}
    _L2_gnn_all = _L2_gnn_setup()
    _L2_gnn_in = {k: v for k, v in _L2_gnn_all.items() if k in ('W', 'b')}
    del _L2_gnn_all

    def _L3_gnn_setup():
        import jax, jax.numpy as jnp
        import numpy as np
        N, E, F_IN, F_OUT = (6250, 200000, 128, 128)
        ALPHA = 0.2
        key = jax.random.key(seed)
        k1, k2, k3, k4 = jax.random.split(key, 4)
        h = jax.random.normal(k1, (N, F_IN), dtype=jnp.float32)
        edge_index = jax.random.randint(k2, (2, E), 0, N, dtype=jnp.int32)
        gain = 1.414
        std_W = gain * np.sqrt(2.0 / (F_IN + F_OUT))
        std_a = gain * np.sqrt(2.0 / (1 + 2 * F_OUT))
        W = std_W * jax.random.normal(k3, (F_IN, F_OUT), dtype=jnp.float32)
        a = std_a * jax.random.normal(k4, (1, 2 * F_OUT), dtype=jnp.float32)
        return {'h': h, 'edge_index': edge_index, 'W': W, 'a': a}
    _L3_gnn_all = _L3_gnn_setup()
    _L3_gnn_in = {k: v for k, v in _L3_gnn_all.items() if k in ('W', 'a')}
    del _L3_gnn_all
    return {'x': x, 'src': src, 'dst': dst, 'L0_gnn_W1_l': _L0_gnn_in['W1_l'], 'L0_gnn_b1': _L0_gnn_in['b1'], 'L0_gnn_W1_r': _L0_gnn_in['W1_r'], 'L0_gnn_W2_l': _L0_gnn_in['W2_l'], 'L0_gnn_b2': _L0_gnn_in['b2'], 'L0_gnn_W2_r': _L0_gnn_in['W2_r'], 'L1_gnn_eps': _L1_gnn_in['eps'], 'L1_gnn_W1': _L1_gnn_in['W1'], 'L1_gnn_b1': _L1_gnn_in['b1'], 'L1_gnn_g1': _L1_gnn_in['g1'], 'L1_gnn_beta1': _L1_gnn_in['beta1'], 'L1_gnn_W2': _L1_gnn_in['W2'], 'L1_gnn_b2': _L1_gnn_in['b2'], 'L1_gnn_g2': _L1_gnn_in['g2'], 'L1_gnn_beta2': _L1_gnn_in['beta2'], 'L2_gnn_W': _L2_gnn_in['W'], 'L2_gnn_b': _L2_gnn_in['b'], 'L3_gnn_W': _L3_gnn_in['W'], 'L3_gnn_a': _L3_gnn_in['a']}

def reference(x, src, dst, L0_gnn_W1_l, L0_gnn_b1, L0_gnn_W1_r, L0_gnn_W2_l, L0_gnn_b2, L0_gnn_W2_r, L1_gnn_eps, L1_gnn_W1, L1_gnn_b1, L1_gnn_g1, L1_gnn_beta1, L1_gnn_W2, L1_gnn_b2, L1_gnn_g2, L1_gnn_beta2, L2_gnn_W, L2_gnn_b, L3_gnn_W, L3_gnn_a):
    import jax
    import jax.numpy as jnp

    def _L0_gnn_ref(node_fts, edge_index, W1_l, b1, W1_r, W2_l, b2, W2_r):
        import jax, jax.numpy as jnp
        import numpy as np
        N_NODES = 1250
        N_EDGES = 80000
        D = 128

        def _mean_aggregate(x, src, dst, num_nodes):
            msg = x[src]
            summed = jax.ops.segment_sum(msg, dst, num_segments=num_nodes)
            cnt = jax.ops.segment_sum(jnp.ones_like(dst, dtype=x.dtype), dst, num_segments=num_nodes)
            return summed / jnp.maximum(cnt, 1.0)[:, None]

        def _sage_conv(x, src, dst, W_l, b, W_r, num_nodes):
            aggr = _mean_aggregate(x, src, dst, num_nodes)
            return aggr @ W_l + b + x @ W_r
        src, dst = (edge_index[0], edge_index[1])
        n = node_fts.shape[0]
        x = jax.nn.relu(_sage_conv(node_fts, src, dst, W1_l, b1, W1_r, n))
        x = jax.nn.relu(_sage_conv(x, src, dst, W2_l, b2, W2_r, n))
        return x

    def _L1_gnn_ref(x, edge_index, eps, W1, b1, g1, beta1, W2, b2, g2, beta2):
        import jax, jax.numpy as jnp
        import numpy as np
        N, E, D = (12500, 80000, 128)
        BN_EPS = 1e-05

        def _batchnorm(h, gamma, beta):
            mean = jnp.mean(h, axis=0)
            var = jnp.var(h, axis=0)
            return gamma * (h - mean) * jax.lax.rsqrt(var + BN_EPS) + beta
        src, dst = (edge_index[0], edge_index[1])
        aggr = jax.ops.segment_sum(x[src], dst, num_segments=x.shape[0])
        h = (1.0 + eps) * x + aggr
        h = jax.nn.relu(_batchnorm(h @ W1.T + b1, g1, beta1))
        h = jax.nn.relu(_batchnorm(h @ W2.T + b2, g2, beta2))
        return h

    def _L2_gnn_ref(x, W, b, edge_index):
        import jax, jax.numpy as jnp
        import numpy as np
        N_NODES = 1250
        N_EDGES = 80000
        IN_CH = 128
        OUT_CH = 128
        src, dst = (edge_index[0], edge_index[1])
        x_i = x[dst]
        x_j = x[src]
        feat = jnp.concatenate([x_i, x_j - x_i], axis=-1)
        msg = feat @ W.T + b
        out = jax.ops.segment_max(msg, dst, num_segments=x.shape[0])
        return jnp.where(jnp.isfinite(out), out, 0.0)

    def _L3_gnn_ref(h, edge_index, W, a):
        import jax, jax.numpy as jnp
        import numpy as np
        N, E, F_IN, F_OUT = (6250, 200000, 128, 128)
        ALPHA = 0.2
        n = h.shape[0]
        row, col = (edge_index[0], edge_index[1])
        Wh = h @ W
        a_src, a_dst = (a[0, :F_OUT], a[0, F_OUT:])
        score = Wh[row] @ a_src + Wh[col] @ a_dst
        edge_e = jnp.exp(-jax.nn.leaky_relu(score, negative_slope=ALPHA))
        e_rowsum = jax.ops.segment_sum(edge_e, row, num_segments=n)
        h_prime = jax.ops.segment_sum(edge_e[:, None] * Wh[col], row, num_segments=n)
        h_prime = h_prime / e_rowsum[:, None]
        return jax.nn.elu(h_prime)
    edge_index = jnp.stack([src, dst])
    x = _layernorm(x + _L0_gnn_ref(x, edge_index, L0_gnn_W1_l, L0_gnn_b1, L0_gnn_W1_r, L0_gnn_W2_l, L0_gnn_b2, L0_gnn_W2_r), axis=-1)
    x = _layernorm(x + _L1_gnn_ref(x, edge_index, L1_gnn_eps, L1_gnn_W1, L1_gnn_b1, L1_gnn_g1, L1_gnn_beta1, L1_gnn_W2, L1_gnn_b2, L1_gnn_g2, L1_gnn_beta2), axis=-1)
    x = _layernorm(x + _L2_gnn_ref(x, L2_gnn_W, L2_gnn_b, edge_index), axis=-1)
    x = _layernorm(x + _L3_gnn_ref(x, edge_index, L3_gnn_W, L3_gnn_a), axis=-1)
    return x

_drawn_inputs = setup_inputs


def setup_inputs(seed=0):
    import zlib

    import numpy as np

    out = dict(_drawn_inputs(seed))
    spreads = {'L0_gnn_b1': (0.0, 0.1),
     'L0_gnn_b2': (0.0, 0.1),
     'L1_gnn_g1': (1.0, 0.2),
     'L1_gnn_beta1': (0.0, 0.1),
     'L1_gnn_g2': (1.0, 0.2),
     'L1_gnn_beta2': (0.0, 0.1)}
    factors = {}
    for name, (base, spread) in spreads.items():
        noise = np.random.default_rng([zlib.crc32(name.encode()), seed]).standard_normal(out[name].shape)
        drawn = base * np.exp(spread * noise) if base else spread * noise
        out[name] = jnp.asarray(drawn.astype(out[name].dtype))
    for name, factor in factors.items():
        out[name] = (out[name] * factor).astype(out[name].dtype)
    return out
```

```python
import concourse.bass as bass
from concourse import mybir
from contextlib import ExitStack

P = 128
D = 128
N_NODES = 12500
N_EDGES = 200000
J = 8
CHUNK = P * J
CHUNKS = -(-N_EDGES // CHUNK)
EDGES = CHUNKS * CHUNK
COLS = CHUNKS * J
BLOCKS = -(-N_NODES // P)
NODES = BLOCKS * P
PAD_NODE = NODES - 1
STEPS = 3 * BLOCKS + 1
EMPTY = STEPS - (CHUNKS + BLOCKS - 1)
ACC_BLOCKS = BLOCKS + EMPTY
TURNS = CHUNKS - 1
RING = 4
LAPS = CHUNKS // RING
ROW = D + 2
G = 2
GROUPS = BLOCKS // G
W = G * P
LOT = 7
LOTS = BLOCKS // LOT
DST_SHIFT = 14
BLOCK_SHIFT = 7
BIG = 3.0e38
LN_EPS = 1e-5
BN_EPS = 1e-5
LRELU_SLOPE = 0.2

SAGE1, SAGE2, GIN, EDGE, GAT = range(5)
WALKS_BEFORE = {SAGE1: 0, SAGE2: 1, GIN: 2, GAT: 3}
SCATTER_AFTER = {SAGE1: 3, SAGE2: 13, GIN: 30, EDGE: 3}
assert CHUNKS % RING == 0 and BLOCKS % G == 0 and GROUPS % 2 == 1 and EMPTY >= 0
assert NODES <= 1 << DST_SHIFT and 1 << BLOCK_SHIFT == P


class Tally:

    def __init__(self, engine, sem):
        self.engine, self.sem, self.n, self.offset = engine, sem, 0, 0

    def up(self, instruction):
        self.n += 1
        instruction.then_inc(self.sem, 1)

    def done(self):
        self.engine.wait_ge(self.sem, self.offset + self.n)

    def link(self, instruction):
        self.up(instruction)
        self.done()

    def enter(self, i, per):
        self.at, self.per, self.offset = self.n, per, i * per

    def leave(self, times):
        assert self.n - self.at == self.per, (self.n - self.at, self.per)
        self.n = self.at + self.per * times
        self.offset = 0


def gnn(nc, A, out):
    fp32, bf16, i32 = mybir.dt.float32, mybir.dt.bfloat16, mybir.dt.int32
    ALU, ACT = mybir.AluOpType, mybir.ActivationFunctionType
    ds = bass.ds

    with ExitStack() as ctx:
        def sb(name, shape, dt=fp32):
            return ctx.enter_context(nc.sbuf_tensor(name, shape, dt))

        def sem(name):
            return ctx.enter_context(nc.semaphore(name))

        def dram(name, shape, dt=fp32):
            return nc.dram_tensor(name, shape, dt, kind="Internal").ap()

        h1_rows = dram("h1_rows", (NODES, D))
        x1_rows = dram("x1_rows", (NODES, D))
        z_rows = dram("z_rows", (NODES, D))
        wh_rows = dram("wh_rows", (NODES, ROW))
        max_rows = dram("max_rows", (EDGES, D))
        starts_dram = dram("starts_dram", (EDGES,), bf16)
        place_dram = dram("place_dram", (EDGES,), i32)
        pair_dram = dram("pair_dram", (EDGES,), i32)
        sorted_dram = dram("sorted_dram", (EDGES, 1), i32)
        col_dram = dram("col_dram", (EDGES,), i32)
        p_dram = dram("p_dram", (NODES,))

        acc = sb("acc", [P, ACC_BLOCKS, D + 1])
        X = sb("X", [P, BLOCKS, D])
        Y = sb("Y", [P, ACC_BLOCKS * D])
        key = sb("key", [P, COLS], mybir.dt.int16)
        ring = sb("ring", [P, RING * J, ROW])
        onehot = sb("onehot", [P, 3, J, P])
        work = sb("work", [P, 2, J * P])
        idx_ring = sb("idx_ring", [P, RING, J], i32)
        pair_ring = sb("pair_ring", [P, RING, J], i32)
        wts = {n: sb("w_" + n, [P, D]) for n in ("l1", "r1", "l2", "r2", "g1", "g2")}
        w_edge = sb("w_edge", [P, 2 * D])
        w_gat = sb("w_gat", [P, D + 2])
        a_cols = sb("a_cols", [P, 2])
        vecs = sb("vecs", [P, 6])
        sage_bias = sb("sage_bias", [1, 2, D])
        edge_bias = sb("edge_bias", [1, D])
        eps1 = sb("eps1", [P, 1])
        ident = sb("ident", [P, P])
        below = sb("below", [P, P])
        ones = sb("ones", [P, P])
        ones_bf = sb("ones_bf", [P, 1], bf16)
        part_i = sb("part_i", [P, 1], i32)
        iota_f = sb("iota_f", [P, STEPS])
        part_f = sb("part_f", [P, 1])
        first_node = sb("first_node", [P, ACC_BLOCKS])
        samp = sb("samp", [P, 2], i32)
        sampf = sb("sampf", [P, 2])
        srow = sb("srow", [1, CHUNKS], i32)
        chunk_at = sb("chunk_at", [1, 2, STEPS], i32)
        steps_to = sb("steps_to", [1, 2, CHUNKS], i32)
        count = sb("count", [P, BLOCKS])
        offs = sb("offs", [P, BLOCKS])
        inv = sb("inv", [P, BLOCKS])
        deg = sb("deg", [P, BLOCKS])
        lone = sb("lone", [P, BLOCKS])
        last_i = sb("last_i", [P, BLOCKS], i32)
        pick_idx = sb("pick_idx", [P, 2, LOT], i32)
        mv = sb("mv", [P, BLOCKS, 2])
        rstd = sb("rstd", [P, BLOCKS])
        lmv = sb("lmv", [P, LOT, 2])
        lstat = sb("lstat", [P, LOT, 6])
        bn = sb("bn", [P, 2, 4])
        ps = ctx.enter_context(nc.psum_tensor("ps", [P, 8, 512], fp32))

        Yn = Y[:, 0:NODES].rearrange("p (b f) -> p b f", f=D)
        acc_flat = acc[:, :, :].rearrange("p b f -> p (b f)")
        acc_z = acc[:, 0:BLOCKS, 0:D]
        acc_wh = acc_flat[:, 0:BLOCKS * ROW].rearrange("p (b r) -> p b r", r=ROW)
        iota_i = acc_flat[:, 0:STEPS].bitcast(i32)
        wts["at"] = Y[:, NODES:NODES + D]
        scan_b = mv[:, :, :].rearrange("p b t -> p (b t)")[:, 0:BLOCKS]
        hot = onehot[:, :, :, :].rearrange("p a j n -> p a (j n)")
        ring_flat = ring[:, :, :].rearrange("p a r -> p (a r)")
        FREE = 2 * J * ROW
        words = ring_flat[:, FREE:FREE + COLS].bitcast(i32)
        words_dst = ring_flat[:, 0:COLS].bitcast(i32)
        words_src = onehot[:, :, :, :].rearrange("p a j n -> p (a j n)")[:, 0:COLS].bitcast(i32)
        work4 = work[:, :, :].rearrange("p a (q f) -> p a q f", f=P)
        fed_b = work4[:, :, 0:2 * G, :]
        turned_b = work4[:, :, 2 * G:4 * G, :]
        rowsT = hot[:, 0:2, :]
        products = work[:, 0, :].rearrange("p (j n) -> p j n", n=P)
        score = work[:, 1, 0:3 * J].rearrange("p (a j) -> p a j", j=J)
        maxT = work[:, :, :]
        starts_b = hot[:, 2, :].bitcast(bf16).rearrange("p (a n) -> p a n", a=2)
        lot_a = hot[:, 0, 0:LOT * D].rearrange("p (b f) -> p b f", f=D)
        lot_b = hot[:, 1, 0:LOT * D].rearrange("p (b f) -> p b f", f=D)
        lot_c = hot[:, 2, 0:LOT * D].rearrange("p (b f) -> p b f", f=D)
        stats = hot[:, 2, 0:GROUPS * 6].rearrange("p (g t) -> p g t", t=6)
        before = work[:, 0, 0:STEPS].bitcast(bf16).rearrange("p (a k) -> p a k", a=2)
        SORT = NODES - 4 * COLS
        spare, place, place_i, _ = (Y[:, SORT + i * COLS:SORT + (i + 1) * COLS] for i in range(4))
        bucket, mine = spare.bitcast(bf16)[:, 0:COLS], spare.bitcast(bf16)[:, COLS:2 * COLS]
        is_start = Y[:, SORT + 3 * COLS:SORT + 4 * COLS]
        raw_dst, raw_prev, raw_src, raw_key = (Y[:, i * COLS:(i + 1) * COLS].bitcast(i32) for i in range(4))
        rank = ps[:, 3:7, :].rearrange("p a n -> p (a n)")[:, 0:COLS]
        OWN_BANK, TURN_BANK, MIX_BANK, SIDE_BANK = 0, 3, 5, 7

        def by_chunk(v):
            return v.rearrange("(c p j) -> p c j", p=P, j=J)

        def as_chunks(v):
            return v.rearrange("p (c j) -> p c j", j=J)

        S = {n: sem(n) for n in """
            consts_loaded keys_loaded iotas ready_consts counted counted_mm tables_mm tabled src_tables_mm
            src_tabled chunks_here onehot_ready steps_done acc_done dve_chain act_chain pool_turn
            degrees_ready last_mm last_ready place_ready place_out starts_ready starts_out
            pair_ready pair_out h1_loaded acc_clear words_loaded words_ready col_out src_loaded
            sqrt_in sqrt_out settled normed x1_out gin_ready rows_turned rows_copied scanned back_turned
            back_copied pick_ready scores_ready weights_ready p_ready
            p_turned p_row p_out p_loaded wa_mm wa_ready h_ready e_ready out_stored
            """.split()}
        idx_here, gathered, scattered, place_here, row_stored = (
            [sem(f"{n}{r}") for r in range(RING)]
            for n in ("idx_here", "gathered", "scattered", "place_here", "row_stored"))
        picked = [sem(f"picked{a}") for a in range(2)]
        starts_here = [sem(f"starts_here{a}") for a in range(2)]
        fed, turned, copied, mixed, used, stored = (
            {n: sem(f"{w}_{n}") for n in ("sage1", "sage2", "gin1", "gin2", "gin3", "edge", "gat")}
            for w in ("fed", "turned", "copied", "mixed", "used", "stored"))

        idx_src = {q: by_chunk(A["src"]) for q in (SAGE1, SAGE2, GIN, EDGE)}
        idx_src[GAT] = by_chunk(col_dram)
        table = {SAGE1: A["x"], SAGE2: h1_rows, GIN: x1_rows, EDGE: z_rows, GAT: wh_rows}
        scatter_from = {q: sum(n for r, n in SCATTER_AFTER.items() if r < q) for q in SCATTER_AFTER}

        def settle(engine):
            engine.sem_inc(S["settled"], 1)

        def grouped(engine, body, first=None, last=None):
            (first or body)(0, 0)
            with engine.Fori(0, (GROUPS - 1) // 2) as i:
                for half in (1, 0):
                    body(2 * i + 2 - half, half)
            if last:
                last(GROUPS - 1, 0)

        block = ctx.enter_context(nc.Block())

        @block.sync
        def _(sp):
            def load(dst, src, s):
                sp.dma_start(dst, src).then_inc(S[s], 16)

            def stage_idx(q, r, c):
                sp.dma_start(idx_ring[:, r, :], idx_src[q][:, ds(c, 1), :].rearrange("p o j -> p (o j)")
                             ).then_inc(idx_here[r], 16)

            def stage_place(r, c):
                for to, frm in ((idx_ring, place_dram), (pair_ring, pair_dram)):
                    sp.dma_start(to[:, r, :], by_chunk(frm)[:, ds(c, 1), :].rearrange("p o j -> p (o j)")
                                 ).then_inc(place_here[r], 16)

            def announce(q, r, lap):
                sp.wait_ge(gathered[r], 16 * J * (q * LAPS + lap + 1))
                sp.sem_inc(S["chunks_here"], 1)

            def feed_gathers(q):
                with sp.Fori(0, LAPS - 1) as lap:
                    for r in range(RING):
                        announce(q, r, lap)
                        stage_idx(q, r, (lap + 1) * RING + r)
                for r in range(RING):
                    announce(q, r, LAPS - 1)

            def first_idx(q):
                for r in range(RING):
                    stage_idx(q, r, r)

            def feed_scatter(q):
                lap0, n = scatter_from[q], SCATTER_AFTER[q]
                for r in range(RING):
                    stage_place(r, lap0 * RING + r)
                with sp.Fori(lap0, lap0 + n - 1) as lap:
                    for r in range(RING):
                        sp.wait_ge(scattered[r], 16 * J * (lap + 1))
                        settle(sp)
                        stage_place(r, (lap + 1) * RING + r)
                for r in range(RING):
                    sp.wait_ge(scattered[r], 16 * J * (lap0 + n))

            first_idx(SAGE1)
            dst = A["dst_before"][1:EDGES + 1]
            firsts = dst.rearrange("(c e) -> c e", e=CHUNK)
            with nc.allow_non_contiguous_dma(reason="one word per chunk"):
                load(samp[:, 0:1], firsts[1:P + 1, 0:1], "keys_loaded")
                load(samp[0:TURNS - P, 1:2], firsts[P + 1:CHUNKS, 0:1], "keys_loaded")
                load(srow[0:1, 0:TURNS], firsts[1:CHUNKS, 0:1].rearrange("c o -> o c"), "keys_loaded")
            load(as_chunks(raw_key), by_chunk(dst), "keys_loaded")
            load(as_chunks(raw_src), by_chunk(A["src"]), "keys_loaded")
            load(raw_dst, dst.rearrange("(p t) -> p t", p=P), "keys_loaded")
            load(raw_prev, A["dst_before"][0:EDGES].rearrange("(p t) -> p t", p=P), "keys_loaded")
            for n, a in (("l1", "W1_l"), ("r1", "W1_r"), ("l2", "W2_l"), ("r2", "W2_r"),
                         ("g1", "gin_W1t"), ("g2", "gin_W2t"), ("at", "gat_Wt")):
                load(wts[n][:, :], A[a], "consts_loaded")
            load(w_edge[:, D:2 * D], A["edge_Wt"][0:P, :], "consts_loaded")
            load(w_edge[:, 0:D], A["edge_Wt"][P:2 * P, :], "consts_loaded")
            load(w_gat[:, 0:D], A["gat_W"], "consts_loaded")
            load(a_cols[:, :], A["gat_a"], "consts_loaded")
            load(vecs[:, :], A["vecs"], "consts_loaded")
            load(sage_bias[:, :, :], A["biases"][0:2, :].rearrange("(o r) f -> o r f", o=1), "consts_loaded")
            load(edge_bias[:, :], A["biases"][2:3, :], "consts_loaded")
            load(eps1[:, :], A["eps"].partition_broadcast(P), "consts_loaded")
            load(X[:, :, :], A["x"].rearrange("(b p) f -> p b f", p=P), "consts_loaded")
            sp.wait_ge(S["pair_ready"], 1)
            load(by_chunk(pair_dram), as_chunks(raw_key), "pair_out")
            sp.wait_ge(S["starts_ready"], 1)
            load(starts_dram.rearrange("(p t) -> p t", p=P),
                 Y[:, COLS:COLS + COLS // 2].bitcast(bf16), "starts_out")
            feed_gathers(SAGE1)
            sp.wait_ge(S["place_ready"], 1)
            load(by_chunk(place_dram), as_chunks(place_i.bitcast(i32)), "place_out")
            sp.wait_ge(S["pair_out"], 16)
            sp.wait_ge(S["starts_out"], 16)
            sp.wait_ge(S["place_out"], 16)
            feed_scatter(SAGE1)

            first_idx(SAGE2)
            sp.wait_ge(stored["sage1"], 16 * GROUPS)
            load(Yn[:, :, :], h1_rows.rearrange("(b p) f -> p b f", p=P), "h1_loaded")
            feed_gathers(SAGE2)
            feed_scatter(SAGE2)

            first_idx(GIN)
            feed_gathers(GIN)
            feed_scatter(GIN)

            first_idx(EDGE)
            def load_starts(a, c):
                sp.dma_start(starts_b[:, a, :], starts_dram.rearrange("(c e) -> c e", e=CHUNK)
                             [ds(c, 1), :].rearrange("o e -> (o e)").partition_broadcast(P)
                             ).then_inc(starts_here[a], 16)

            def store_max(r, c):
                sp.dma_start(max_rows.rearrange("(c p j) f -> c p j f", p=P, j=J)[ds(c, 1), :, :, :]
                             .rearrange("o p j f -> p (o j) f"),
                             ring[:, r * J:(r + 1) * J, 0:D]).then_inc(row_stored[r], 16)

            def edge_chunk(c, lap, r, first=False, refill=True):
                announce(EDGE, r, lap)
                if refill:
                    stage_idx(EDGE, r, c + RING)
                if not first or r >= 1:
                    sp.wait_ge(S["scanned"], c)
                    settle(sp)
                if refill or r < RING - 1:
                    load_starts((r + 1) % 2, c + 1)
                if not first or r >= 2:
                    sp.wait_ge(S["back_copied"], c - 1)
                    settle(sp)
                    store_max((r - 2) % RING, c - 2)

            sp.wait_ge(used["edge"], 1)
            load_starts(0, 0)
            for r in range(RING):
                edge_chunk(r, 0, r, first=True)
            with sp.Fori(1, LAPS - 1) as lap:
                for r in range(RING):
                    edge_chunk(lap * RING + r, lap, r)
            for r in range(RING):
                edge_chunk(CHUNKS - RING + r, LAPS - 1, r, refill=False)
            for c in (CHUNKS - 2, CHUNKS - 1):
                sp.wait_ge(S["back_copied"], c + 1)
                store_max(c % RING, c)

            for r in range(RING):
                sp.wait_ge(row_stored[r], 16 * LAPS)
            feed_scatter(EDGE)
            load(as_chunks(words), by_chunk(sorted_dram.rearrange("e o -> (e o)")), "words_loaded")
            firsts = sorted_dram.rearrange("(c e) o -> c (e o)", e=CHUNK)
            with nc.allow_non_contiguous_dma(reason="one word per chunk"):
                load(samp[:, 0:1], firsts[1:P + 1, 0:1], "words_loaded")
                load(samp[0:TURNS - P, 1:2], firsts[P + 1:CHUNKS, 0:1], "words_loaded")
                load(srow[0:1, 0:TURNS], firsts[1:CHUNKS, 0:1].rearrange("c o -> o c"), "words_loaded")
            sp.wait_ge(S["words_ready"], 1)
            load(by_chunk(col_dram), as_chunks(words_dst), "col_out")

            sp.wait_ge(S["col_out"], 16)
            first_idx(GAT)
            sp.wait_ge(S["p_row"], 1)
            load(p_dram.rearrange("(b p) -> b p", p=P), lot_a.rearrange("p b f -> p (b f)")[0:BLOCKS, 0:P], "p_out")
            sp.wait_ge(S["p_out"], 16)
            load(Y[:, 0:NODES], p_dram.partition_broadcast(P), "p_loaded")
            feed_gathers(GAT)

            full = N_NODES // P
            with sp.Fori(0, LOTS - 1) as m:
                sp.wait_ge(S["normed"], LOTS + m + 1)
                settle(sp)
                sp.dma_start(out[0:(LOTS - 1) * LOT * P, :].rearrange("(m b p) f -> m p b f", b=LOT, p=P)
                             [ds(m, 1), :, :, :].rearrange("o p b f -> p (o b) f"),
                             X[:, ds(m * LOT, LOT), :]).then_inc(S["out_stored"], 16)
            sp.wait_ge(S["normed"], 2 * LOTS)
            b0 = (LOTS - 1) * LOT
            sp.dma_start(out[b0 * P:full * P, :].rearrange("(b p) f -> p b f", p=P),
                         X[:, b0:full, :]).then_inc(S["out_stored"], 16)
            sp.dma_start(out[full * P:N_NODES, :], X[0:N_NODES - full * P, full, :]).then_inc(S["out_stored"], 16)
            sp.wait_ge(S["out_stored"], 16 * (LOTS + 1))

        @block.gpsimd
        def _(pool):
            pool.iota(iota_i[:, :], [[1, STEPS]], base=0, channel_multiplier=0).then_inc(S["iotas"], 1)
            pool.iota(part_i[:, :], [[1, 1]], base=0, channel_multiplier=1).then_inc(S["iotas"], 1)

            def gather_chunk(q, r):
                cols = ROW if q == GAT else D
                for j in range(J):
                    pool.indirect_dma_start(
                        ring[:, r * J + j, 0:cols], None, table[q],
                        bass.IndirectOffsetOnAxis(idx_ring[:, r, j:j + 1], 0)).then_inc(gathered[r], 16)

            def gathers(q):
                for r in range(RING):
                    pool.wait_ge(idx_here[r], 16 * (q * LAPS + 1))
                    gather_chunk(q, r)
                if q != EDGE:
                    pool.wait_ge(S["src_tabled" if q == GAT else "tabled"], 2)
                with pool.Fori(1, LAPS) as lap:
                    for r in range(RING):
                        pool.wait_ge(idx_here[r], 16 * (q * LAPS + lap + 1))
                        if q == EDGE:
                            pool.wait_ge(row_stored[r], 16 * lap)
                        else:
                            side = int(q == GAT)
                            n = pool.value_load(steps_to[0:1, side, ds((lap - 1) * RING + r, 1)],
                                                min_val=1, max_val=STEPS)
                            pool.wait_ge(S["steps_done"], n + WALKS_BEFORE[q] * STEPS)
                        pool.sem_inc(S["pool_turn"], 1)
                        gather_chunk(q, r)

            def scatters(q):
                with pool.Fori(scatter_from[q], scatter_from[q] + SCATTER_AFTER[q]) as lap:
                    for r in range(RING):
                        pool.wait_ge(place_here[r], 32 * (lap + 1))
                        pool.sem_inc(S["pool_turn"], 1)
                        for j in range(J):
                            pool.indirect_dma_start(
                                sorted_dram, bass.IndirectOffsetOnAxis(idx_ring[:, r, j:j + 1], 0),
                                pair_ring[:, r, j:j + 1], None).then_inc(scattered[r], 16)

            gathers(SAGE1)
            scatters(SAGE1)
            pool.wait_ge(stored["sage1"], 16 * GROUPS)
            gathers(SAGE2)
            scatters(SAGE2)
            pool.wait_ge(S["x1_out"], 16 * LOTS)
            gathers(GIN)
            scatters(GIN)
            pool.wait_ge(stored["edge"], 16 * GROUPS)
            gathers(EDGE)
            for r in range(RING):
                pool.wait_ge(row_stored[r], 16 * LAPS)
            with pool.Fori(0, LOTS // 2) as i:
                for half in range(2):
                    pool.wait_ge(S["pick_ready"], 2 * i + half + 1)
                    pool.sem_inc(S["pool_turn"], 1)
                    for b in range(LOT):
                        pool.indirect_dma_start(
                            ring[:, half * J + b, 0:D], None, max_rows,
                            bass.IndirectOffsetOnAxis(pick_idx[:, half, b:b + 1], 0)
                        ).then_inc(picked[half], 16)
            scatters(EDGE)
            pool.wait_ge(stored["gat"], 16 * GROUPS)
            gathers(GAT)

        @block.tensor
        def _(pe):
            def mm(o, lhsT, rhs, start=True, stop=True):
                return nc.tensor.matmul(o, lhsT, rhs, start=start, stop=stop)

            def turn(o, a):
                return nc.tensor.transpose(o, a, ident[:, :])

            def path_sum(done):
                mm(ps[0:1, SIDE_BANK, 0:STEPS], ones_bf[:, :], before[:, 0, :], stop=False)
                mm(ps[0:1, SIDE_BANK, 0:STEPS], ones_bf[0:TURNS - P, :], before[0:TURNS - P, 1, :],
                   start=False).then_inc(done, 1)

            def walk(q, between=None):
                side = int(q == GAT)
                base = WALKS_BEFORE[q] * STEPS

                def step(k, buf):
                    c = pe.value_load(chunk_at[0:1, side, ds(k, 1)], min_val=0, max_val=CHUNKS - 1)
                    pe.wait_ge(S["chunks_here"], c + (q * CHUNKS + 1))
                    if q == GAT:
                        pe.wait_ge(S["weights_ready"], k + 1)
                    else:
                        pe.wait_ge(S["onehot_ready"], k + (base + 1))
                    for j in range(J):
                        last = mm(ps[:, buf, 0:D + 1], onehot[:, buf, j, :],
                                  ring[:, ds((c & (RING - 1)) * J + j, 1), 0:D + 1]
                                  .rearrange("p o f -> p (o f)"),
                                  start=j == 0, stop=j == J - 1)
                    last.then_inc(S["steps_done"], 1)

                step(0, 0)
                for start, turns in ((0, BLOCKS // 2), (BLOCKS // 2, BLOCKS // 2)) if between else ((0, BLOCKS),):
                    if start:
                        between()
                    with pe.Fori(0, turns) as i:
                        for n in (1, 2, 3):
                            step(3 * i + (3 * start + n), n % 3)

            def dense(n, turn_of, mix_of):
                def both(g, half):
                    turn_of(g, half)
                    mix_of(g - 1, 1 - half)
                grouped(pe, both, first=turn_of, last=mix_of)

            def bank(which, half):
                return ps[:, which + half, :]

            def turn_sage(n):
                def f(g, half):
                    pe.wait_ge(fed[n], g + 1)
                    o = bank(TURN_BANK, half)
                    for i in range(2 * G):
                        last = turn(o[:, i * P:(i + 1) * P], fed_b[:, half, i, :])
                    last.then_inc(turned[n], 1)
                return f

            def mix_sage(n, layer):
                def f(g, half):
                    pe.wait_ge(copied[n], g + 1)
                    o = bank(MIX_BANK, half)
                    for i in range(G):
                        at = o[:, i * D:(i + 1) * D]
                        mm(at, ones[0:1, :], sage_bias[0:1, layer, :], stop=False)
                        mm(at, turned_b[:, half, i, :], wts[f"l{layer + 1}"][:, :], start=False, stop=False)
                        last = mm(at, turned_b[:, half, G + i, :], wts[f"r{layer + 1}"][:, :], start=False)
                    last.then_inc(mixed[n], 1)
                return f

            def turn_nodes(n):
                def f(g, half):
                    pe.wait_ge(fed[n], g + 1)
                    for i in range(G):
                        last = turn(bank(TURN_BANK, half)[:, i * P:(i + 1) * P], fed_b[:, half, i, :])
                    last.then_inc(turned[n], 1)
                return f

            def mix_gin(n, w):
                def f(g, half):
                    pe.wait_ge(copied[n], g + 1)
                    mm(bank(MIX_BANK, half)[:, 0:W], w[:, :],
                       turned_b[:, half, 0:G, :].rearrange("p i n -> p (i n)")).then_inc(mixed[n], 1)
                return f

            def mix_nodes(n, w, w_own, bias=None):
                def f(g, half):
                    pe.wait_ge(copied[n], g + 1)
                    pe.wait_ge(used[n], g + 1)
                    cols, own = w.shape[1], w_own.shape[1]
                    for i in range(G):
                        mm(bank(MIX_BANK, half)[:, i * W:i * W + cols], turned_b[:, half, i, :], w)
                    for i in range(G):
                        at = bank(OWN_BANK, half)[:, i * D:i * D + own]
                        if bias is not None:
                            mm(at, ones[0:1, :], bias, stop=False)
                        last = mm(at, turned_b[:, half, i, :], w_own, start=bias is None)
                    last.then_inc(mixed[n], 1)
                return f

            pe.wait_ge(S["ready_consts"], 1)
            pe.wait_ge(S["tabled"], 1)
            path_sum(S["tables_mm"])
            pe.wait_ge(S["consts_loaded"], 16 * 16)
            mm(ps[:, SIDE_BANK - 1, 0:2], wts["at"][:, :], a_cols[:, :]).then_inc(S["wa_mm"], 1)
            pe.wait_ge(S["tabled"], 2)

            def sum_counts():
                pe.wait_ge(S["counted"], 1)
                mm(ps[:, SIDE_BANK, 0:BLOCKS], below[:, :], count[:, :])
                mm(ps[:, SIDE_BANK, P:P + BLOCKS], ones[:, :], count[:, :]).then_inc(S["counted_mm"], 1)
            walk(SAGE1, sum_counts)

            pe.wait_ge(S["degrees_ready"], 1)
            mm(ps[:, SIDE_BANK, 2 * P:2 * P + BLOCKS], below[:, :], deg[:, :])
            mm(ps[:, SIDE_BANK, 3 * P:3 * P + BLOCKS], ones[:, :], deg[:, :]).then_inc(S["counted_mm"], 1)
            dense("sage1", turn_sage("sage1"), mix_sage("sage1", 0))
            walk(SAGE2)
            dense("sage2", turn_sage("sage2"), mix_sage("sage2", 1))
            walk(GIN)
            dense("gin1", turn_nodes("gin1"), mix_gin("gin1", wts["g1"]))
            grouped(pe, mix_gin("gin2", wts["g2"]))

            def turn_back(g, half):
                pe.wait_ge(copied["gin3"], g + 1)
                for i in range(G):
                    last = turn(bank(MIX_BANK, half)[:, i * P:(i + 1) * P], turned_b[:, half, i, :])
                last.then_inc(mixed["gin3"], 1)
            grouped(pe, turn_back)
            dense("edge", turn_nodes("edge"), mix_nodes("edge", w_edge[:, 0:D], w_edge[:, D:2 * D], edge_bias[:, :]))

            def rows_turn(c, r):
                pe.wait_ge(S["chunks_here"], c + (EDGE * CHUNKS + 1))
                for j in range(J):
                    last = turn(ps[:, 2 * (r % 2) + j // 4, (j % 4) * P:(j % 4 + 1) * P],
                                ring[:, r * J + j, 0:D])
                last.then_inc(S["rows_turned"], 1)

            def back_turn(c, r):
                pe.wait_ge(S["scanned"], c + 1)
                for j in range(J):
                    last = turn(ps[:, 4 + 2 * (r % 2) + j // 4, (j % 4) * P:(j % 4 + 1) * P],
                                maxT[:, r % 2, :].rearrange("f (p j) -> f j p", j=J)[:, j, :])
                last.then_inc(S["back_turned"], 1)

            pe.wait_ge(used["edge"], GROUPS + 1)
            rows_turn(0, 0)
            for r in range(1, RING):
                rows_turn(r, r)
                back_turn(r - 1, r - 1)
            with pe.Fori(1, LAPS) as lap:
                for r in range(RING):
                    rows_turn(lap * RING + r, r)
                    back_turn(lap * RING + r - 1, (r - 1) % RING)
            back_turn(CHUNKS - 1, RING - 1)

            dense("gat", turn_nodes("gat"), mix_nodes("gat", w_gat[:, :], w_gat[:, D:D + 1]))
            pe.wait_ge(S["src_tabled"], 1)
            path_sum(S["src_tables_mm"])
            pe.wait_ge(S["src_tabled"], 2)
            pe.wait_ge(S["p_ready"], 1)
            turn(ps[0:BLOCKS, SIDE_BANK, 0:P], inv[:, :]).then_inc(S["p_turned"], 1)
            walk(GAT)

        @block.scalar
        def _(act):
            chain = Tally(act, S["act_chain"])
            roots = [0]

            def root():
                roots[0] += 1
                act.wait_ge(S["sqrt_in"], roots[0])
                what = bn[:, 0, 1:2] if roots[0] == 2 else bn[:, 1, 1:2] if roots[0] == 3 else rstd[:, :]
                nc.scalar.activation(what, what, ACT.Sqrt).then_inc(S["sqrt_out"], 1)

            def copy_turned(n, width):
                def f(g, half):
                    act.wait_ge(turned[n], g + 1)
                    nc.scalar.copy(turned_b[:, half, 0:width, :].rearrange("p q n -> p (q n)"),
                                   ps[:, TURN_BANK + half, 0:width * P]).then_inc(copied[n], 1)
                return f

            def dense(first, use):
                def both(g, half):
                    first(g, half)
                    use(g - 1, 1 - half)
                grouped(act, both, first=first, last=use)

            def store_group(n, rows, src, cols):
                act.dma_start(rows.rearrange("(g b p) f -> g p b f", p=P, b=G)[ds(cols, 1), :, :, :]
                              .rearrange("o p b f -> p (o b) f"), src).then_inc(stored[n], 16)

            def use_sage1(g, half):
                act.wait_ge(mixed["sage1"], g + 1)
                to = acc[:, ds(g * G, G), 0:D]
                nc.scalar.activation(to, ps[:, MIX_BANK + half, 0:W].rearrange("p (i f) -> p i f", i=G),
                                     ACT.Relu).then_inc(used["sage1"], 1)
                act.wait_ge(used["sage1"], g + 1)
                store_group("sage1", h1_rows, to, g)

            dense(copy_turned("sage1", 2 * G), use_sage1)
            grouped(act, copy_turned("sage2", 2 * G))
            root()
            with act.Fori(0, LOTS) as m:
                act.wait_ge(S["normed"], m + 1)
                act.dma_start(x1_rows.rearrange("(m b p) f -> m p b f", b=LOT, p=P)[ds(m, 1), :, :, :]
                              .rearrange("o p b f -> p (o b) f"),
                              X[:, ds(m * LOT, LOT), :]).then_inc(S["x1_out"], 16)
            grouped(act, copy_turned("gin1", G))
            root()

            def normed_relu(n, layer):
                def f(g, half):
                    act.wait_ge(used[n], g + 1)
                    nc.scalar.activation(turned_b[:, half, 0:G, :].rearrange("p q n -> p (q n)"),
                                         Y[:, ds(g * W, W)], ACT.Relu, bias=bn[:, layer, 3:4],
                                         scale=bn[:, layer, 2:3]).then_inc(copied[n], 1)
                return f

            act.wait_ge(S["gin_ready"], 1)
            grouped(act, normed_relu("gin2", 0))
            root()
            act.wait_ge(S["gin_ready"], 2)
            grouped(act, normed_relu("gin3", 1))
            root()

            def use_edge(g, half):
                act.wait_ge(mixed["edge"], g + 1)
                to = acc[:, ds(g * G, G), 0:D]
                frm = ps[:, MIX_BANK + half, :].rearrange("p (i f) -> p i f", i=G)
                chain.link(nc.scalar.copy(to, frm[:, :, 0:D]))
                store_group("edge", z_rows, to, g)

            def looped_dense(first, use, per):
                first(0, 0)
                with act.Fori(0, (GROUPS - 1) // 2) as i:
                    chain.enter(i, 2 * per)
                    for half in (1, 0):
                        first(2 * i + 2 - half, half)
                        use(2 * i + 1 - half, 1 - half)
                    chain.leave((GROUPS - 1) // 2)
                use(GROUPS - 1, 0)

            looped_dense(copy_turned("edge", G), use_edge, 1)

            def rows_copy(c, r):
                act.wait_ge(S["rows_turned"], c + 1)
                nc.scalar.copy(rowsT[:, r % 2, :].rearrange("f (p j) -> f j p", j=J),
                               ps[:, 2 * (r % 2):2 * (r % 2) + 2, :].rearrange("f a (j p) -> f (a j) p", p=P)
                               ).then_inc(S["rows_copied"], 1)

            def back_copy(c, r):
                act.wait_ge(S["back_turned"], c + 1)
                a = 4 + 2 * (r % 2)
                nc.scalar.copy(ring[:, r * J:(r + 1) * J, 0:D],
                               ps[:, a:a + 2, :].rearrange("p a (j f) -> p (a j) f", f=D)
                               ).then_inc(S["back_copied"], 1)

            rows_copy(0, 0)
            for r in range(1, RING):
                rows_copy(r, r)
                back_copy(r - 1, r - 1)
            with act.Fori(1, LAPS) as lap:
                for r in range(RING):
                    rows_copy(lap * RING + r, r)
                    back_copy(lap * RING + r - 1, (r - 1) % RING)
            back_copy(CHUNKS - 1, RING - 1)
            root()

            def use_gat(g, half):
                act.wait_ge(mixed["gat"], g + 1)
                frm = ps[:, MIX_BANK + half, :].rearrange("p (i f) -> p i f", i=G)
                chain.up(nc.scalar.copy(acc_wh[:, ds(g * G, G), 0:D], frm[:, :, 0:D]))
                chain.link(nc.scalar.copy(acc_wh[:, ds(g * G, G), D + 1:D + 2], frm[:, :, D + 1:D + 2]))
                store_group("gat", wh_rows, acc_wh[:, ds(g * G, G), :], g)

            looped_dense(copy_turned("gat", G), use_gat, 2)

            def weigh(k, n):
                act.wait_ge(S["scores_ready"], k + 1)
                chain.link(nc.scalar.activation(score[:, n % 3, :], score[:, n % 3, :], ACT.Exp, scale=-1.0))
                for j in range(J):
                    at = onehot[:, n % 3, j, :]
                    last = nc.scalar.mul(at, at, score[:, n % 3, j:j + 1])
                last.then_inc(S["weights_ready"], 1)
            weigh(0, 0)
            with act.Fori(0, BLOCKS // 2) as i:
                chain.enter(i, 6)
                for n in range(1, 7):
                    weigh(6 * i + n, n)
                chain.leave(BLOCKS // 2)
            with act.Fori(0, LOTS) as m:
                act.wait_ge(S["h_ready"], m + 1)
                nc.scalar.activation(lot_b, lot_b, ACT.Exp).then_inc(S["e_ready"], 1)
            root()

        @block.vector
        def _(dve):
            v = nc.vector
            chain = Tally(dve, S["dve_chain"])
            up, link = chain.up, chain.link
            roots = [0]

            def wide(t, n):
                return t.unsqueeze(2).to_broadcast([P, t.shape[1], n])

            def path_tables(side, mask, tabled, mm_done):
                for a, n in ((0, P), (1, TURNS - P)):
                    if mask:
                        up(v.tensor_scalar(samp[0:n, a:a + 1], samp[0:n, a:a + 1], mask, BLOCK_SHIFT,
                                           ALU.bitwise_and, ALU.logical_shift_right))
                    else:
                        up(v.tensor_scalar(samp[0:n, a:a + 1], samp[0:n, a:a + 1], BLOCK_SHIFT, None,
                                           ALU.logical_shift_right))
                if mask:
                    link(v.tensor_scalar(srow[:, 0:TURNS], srow[:, 0:TURNS], mask, BLOCK_SHIFT,
                                         ALU.bitwise_and, ALU.logical_shift_right))
                else:
                    link(v.tensor_scalar(srow[:, 0:TURNS], srow[:, 0:TURNS], BLOCK_SHIFT, None,
                                         ALU.logical_shift_right))
                up(v.scalar_tensor_tensor(out=sampf[:, 0:1], in0=samp[:, 0:1], scalar=0.0, in1=part_f[:, :],
                                          op0=ALU.add, op1=ALU.add))
                up(v.scalar_tensor_tensor(out=sampf[0:TURNS - P, 1:2], in0=samp[0:TURNS - P, 1:2],
                                          scalar=float(P), in1=part_f[0:TURNS - P, :], op0=ALU.add, op1=ALU.add))
                link(v.scalar_tensor_tensor(out=steps_to[:, side, 0:TURNS], in0=srow[:, 0:TURNS], scalar=1.0,
                                            in1=iota_f[0:1, 0:TURNS], op0=ALU.add, op1=ALU.add))
                up(v.tensor_scalar(before[:, 0, :], iota_f[:, :], sampf[:, 0:1], None, ALU.is_gt))
                v.tensor_scalar(before[0:TURNS - P, 1, :], iota_f[0:TURNS - P, :], sampf[0:TURNS - P, 1:2],
                                None, ALU.is_gt).then_inc(tabled, 1)
                dve.wait_ge(mm_done, 1)
                v.tensor_copy(chunk_at[:, side, :], ps[0:1, SIDE_BANK, 0:STEPS]).then_inc(tabled, 1)
                dve.wait_ge(tabled, 2)

            def one_hot(side, k, buf):
                c = dve.value_load(chunk_at[0:1, side, ds(k, 1)], min_val=0, max_val=CHUNKS - 1)
                b = (k - c).with_bounds(min_val=0, max_val=ACC_BLOCKS - 1)
                ins = v.scalar_tensor_tensor(
                    out=onehot[:, buf, :, :], in0=wide(key[:, ds(c * J, J)], P), scalar=first_node[:, ds(b, 1)],
                    in1=iota_f[:, 0:P].unsqueeze(1).to_broadcast([P, J, P]), op0=ALU.subtract, op1=ALU.is_equal)
                return c, b, ins

            def add_step(q, k, buf):
                side, base = int(q == GAT), WALKS_BEFORE[q] * STEPS
                c = dve.value_load(chunk_at[0:1, side, ds(k, 1)], min_val=0, max_val=CHUNKS - 1)
                b = (k - c).with_bounds(min_val=0, max_val=ACC_BLOCKS - 1)
                to = acc[:, ds(b, 1), :].rearrange("p o f -> p (o f)")
                dve.wait_ge(S["acc_done"], k + (base + WALKS_BEFORE[q] + 1))
                dve.wait_ge(S["steps_done"], k + (base + 1))
                v.tensor_tensor(to, to, ps[:, buf, 0:D + 1], ALU.add).then_inc(S["acc_done"], 1)

            def clear_acc():
                v.memset(acc[:, :, :], 0.0).then_inc(S["acc_done"], 1)

            def walk(q, hooks=((BLOCKS, None, 0),), between=None):
                clear_acc()
                _, _, ins = one_hot(0, 0, 0)
                ins.then_inc(S["onehot_ready"], 1)
                start = 0
                for turns, hook, per in hooks:
                    if start:
                        between()
                    with dve.Fori(0, turns) as i:
                        chain.enter(i, per)
                        for n in (1, 2, 3):
                            k = 3 * i + (3 * start + n)
                            _, _, ins = one_hot(0, k, n % 3)
                            ins.then_inc(S["onehot_ready"], 1)
                            add_step(q, k - 1, (n - 1) % 3)
                        if hook:
                            hook(i)
                        chain.leave(turns)
                    start += turns
                add_step(q, STEPS - 1, (STEPS - 1) % 3)
                dve.wait_ge(S["acc_done"], (WALKS_BEFORE[q] + 1) * (STEPS + 1))

            def walk_gat():
                def step(k, n, first=0):
                    a = buf = n % 3
                    c, b, ins = one_hot(1, k, buf)
                    link(ins)
                    link(v.tensor_tensor(products, onehot[:, buf, :, :],
                                         Y[:, ds(b * P, P)].unsqueeze(1).to_broadcast([P, J, P]), ALU.mult))
                    link(v.tensor_reduce(score[:, a, :], products, mybir.AxisListType.X, ALU.add))
                    dve.wait_ge(S["chunks_here"], c + (GAT * CHUNKS + 1))
                    link(v.tensor_tensor(score[:, a, :], score[:, a, :],
                                         ring[:, ds((c & (RING - 1)) * J, J), D + 1], ALU.add))
                    v.scalar_tensor_tensor(out=score[:, a, :], in0=score[:, a, :], scalar=LRELU_SLOPE,
                                           in1=score[:, a, :], op0=ALU.mult, op1=ALU.max
                                           ).then_inc(S["scores_ready"], 1)
                    if not first:
                        add_step(GAT, k - 2, (n - 2) % 3)

                clear_acc()
                step(0, 0, first=1)
                step(1, 1, first=1)
                with dve.Fori(0, (STEPS - 7) // 6) as i:
                    chain.enter(i, 6 * 4)
                    for n in range(2, 8):
                        step(6 * i + n, n)
                    chain.leave((STEPS - 7) // 6)
                for k in range(6 * ((STEPS - 7) // 6) + 2, STEPS):
                    step(k, k % 6)
                add_step(GAT, STEPS - 2, (STEPS - 2) % 3)
                add_step(GAT, STEPS - 1, (STEPS - 1) % 3)
                dve.wait_ge(S["acc_done"], 4 * (STEPS + 1))

            def norm_stats(at, n, first_block):
                settle(dve)
                for i in range(n):
                    up(v.bn_stats(lstat[:, i, :], at(i)))
                chain.done()
                settle(dve)
                for i in range(n):
                    up(v.bn_aggr(lmv[:, i, :], lstat[:, i, :]))
                chain.done()
                up(v.tensor_copy(mv[:, ds(first_block, n), :], lmv[:, 0:n, :]))

            def norm_scale():
                chain.done()
                v.tensor_scalar(rstd[:, :], mv[:, :, 1], LN_EPS, None, ALU.add).then_inc(S["sqrt_in"], 1)
                roots[0] += 1
                dve.wait_ge(S["sqrt_out"], roots[0])
                link(v.reciprocal(rstd[:, :], rstd[:, :]))

            def norm_block(b, to=None):
                at = X[:, ds(b, 1), :].rearrange("p o f -> p (o f)")
                return v.tensor_scalar(at if to is None else to, at, mv[:, ds(b, 1), 0:1].rearrange("p o t -> p (o t)"),
                                       rstd[:, ds(b, 1)], ALU.subtract, ALU.mult)

            def norm_lots():
                with dve.Fori(0, LOTS) as m:
                    for i in range(LOT):
                        last = norm_block(m * LOT + i)
                    last.then_inc(S["normed"], 1)

            def norm_groups(n, out_of):
                norm_scale()

                def make(g, half):
                    for i in range(G):
                        last = norm_block(g * G + i, fed_b[:, half, i, :])
                    return last

                def norm(g, half):
                    feed(n, make)(g, half)
                    for i in range(G):
                        norm_block(g * G + i)

                def both(g, half):
                    norm(g, half)
                    out_of(g - 1, 1 - half)
                grouped(dve, both, first=norm, last=out_of)

            def chained_groups(body, per, first=None, last=None):
                (first or body)(0, 0)
                with dve.Fori(0, (GROUPS - 1) // 2) as i:
                    chain.enter(i, 2 * per)
                    for half in (1, 0):
                        body(2 * i + 2 - half, half)
                    chain.leave((GROUPS - 1) // 2)
                if last:
                    last(GROUPS - 1, 0)

            def feed(n, make):
                def f(g, half):
                    if not isinstance(g, int) or g:
                        dve.wait_ge(turned[n], g)
                    make(g, half).then_inc(fed[n], 1)
                return f

            def mean(g, half, other):
                v.tensor_copy(fed_b[:, half, G:2 * G, :], other[:, ds(g * G, G), :])
                return v.tensor_tensor(fed_b[:, half, 0:G, :], acc[:, ds(g * G, G), 0:D],
                                       wide(inv[:, ds(g * G, G)], D), ALU.mult)

            def x_group(g):
                return X[:, ds(g * G, G), :]

            def mix_out(half, which=MIX_BANK):
                return ps[:, which + half, 0:W].rearrange("p (i f) -> p i f", i=G)

            dve.wait_ge(S["iotas"], 2)
            up(v.tensor_copy(iota_f[:, :], iota_i[:, :]))
            up(v.tensor_copy(part_f[:, :], part_i[:, :]))
            up(v.memset(ones[:, :], 1.0))
            up(v.memset(ones_bf[:, :], 1.0))
            up(v.memset(ring[:, :, D:ROW], 1.0))
            chain.done()
            up(v.tensor_scalar(first_node[:, :], iota_f[:, 0:ACC_BLOCKS], float(P), None, ALU.mult))
            up(v.tensor_scalar(below[:, :], iota_f[:, 0:P], part_f[:, :], None, ALU.is_gt))
            up(v.tensor_scalar(ident[:, :], iota_f[:, 0:P], part_f[:, :], None, ALU.is_equal))
            chain.done()
            dve.wait_ge(S["keys_loaded"], 16 * 7)
            up(v.tensor_copy(key[:, :], raw_key))
            dve.sem_inc(S["ready_consts"], 1)
            path_tables(0, 0, S["tabled"], S["tables_mm"])
            up(v.tensor_scalar(place_i.bitcast(i32), raw_src, BLOCK_SHIFT, None, ALU.logical_shift_right))
            link(v.tensor_scalar(raw_key, raw_key, DST_SHIFT, None, ALU.logical_shift_left))
            up(v.tensor_copy(bucket, place_i.bitcast(i32)))
            up(v.memset(place, 0.0))
            v.tensor_tensor(raw_key, raw_key, raw_src, ALU.bitwise_or).then_inc(S["pair_ready"], 1)
            link(v.tensor_tensor(is_start, raw_dst, raw_prev, ALU.is_equal))
            link(v.tensor_scalar(is_start, is_start, 2.0, -1.0, ALU.mult, ALU.add))
            v.tensor_scalar(Y[:, COLS:COLS + COLS // 2].bitcast(bf16), is_start, BIG, None, ALU.mult
                            ).then_inc(S["starts_ready"], 1)
            dve.wait_ge(S["consts_loaded"], 16 * 16)
            up(v.tensor_tensor(w_edge[:, D:2 * D], w_edge[:, D:2 * D], w_edge[:, 0:D], ALU.subtract))
            up(v.tensor_scalar(eps1[:, :], eps1[:, :], 1.0, None, ALU.add))
            dve.wait_ge(S["wa_mm"], 1)
            link(v.tensor_copy(w_gat[:, D:D + 2], ps[:, SIDE_BANK - 1, 0:2]))

            def count_bucket(h):
                link(v.tensor_scalar(mine, bucket, iota_f[:, ds(h, 1)], 0.0, ALU.is_equal, ALU.add,
                                   accum_out=count[:, ds(h, 1)]))

            def count_two(i):
                count_bucket(2 * i)
                count_bucket(2 * i + 1)

            def bucket_starts():
                dve.sem_inc(S["counted"], 1)
                dve.wait_ge(S["counted_mm"], 1)
                link(v.tensor_copy(offs[:, :], side[:, P:P + BLOCKS]))
                link(v.tensor_tensor_scan(out=count[:, :], data0=offs[:, :], data1=offs[:, :], initial=0.0,
                                          op0=ALU.add, op1=ALU.max))
                link(v.tensor_tensor(offs[:, :], count[:, :], offs[:, :], ALU.subtract))
                link(v.tensor_tensor(offs[:, :], offs[:, :], side[:, 0:BLOCKS], ALU.add))

            def rank_bucket(h):
                link(v.tensor_scalar(mine, bucket, iota_f[:, ds(h, 1)], None, ALU.is_equal))
                link(v.tensor_tensor_scan(out=rank, data0=mine, data1=mine, initial=offs[:, ds(h, 1)],
                                          op0=ALU.add, op1=ALU.max))
                settle(dve)
                link(v.copy_predicated(place, mine.bitcast(mybir.dt.int16), rank))

            def rank_two(i):
                rank_bucket(2 * i)
                rank_bucket(2 * i + 1)

            side = ps[:, SIDE_BANK, :]
            walk(SAGE1, ((BLOCKS // 2, count_two, 2), (BLOCKS // 2, rank_two, 6)), bucket_starts)
            v.tensor_scalar(place_i.bitcast(i32), place, -1.0, None, ALU.add).then_inc(S["place_ready"], 1)
            link(v.tensor_copy(deg[:, :], acc[:, 0:BLOCKS, D]))
            up(v.tensor_scalar(inv[:, :], deg[:, :], 1.0, None, ALU.max))
            v.tensor_scalar(lone[:, :], deg[:, :], 1.0, None, ALU.min).then_inc(S["degrees_ready"], 1)
            dve.wait_ge(S["degrees_ready"], 1)
            link(v.reciprocal(inv[:, :], inv[:, :]))
            link(v.tensor_scalar(lone[:, :], lone[:, :], -1.0, 1.0, ALU.mult, ALU.add))
            grouped(dve, feed("sage1", lambda g, half: mean(g, half, X)))
            dve.wait_ge(S["counted_mm"], 2)
            link(v.tensor_copy(scan_b[:, :], side[:, 3 * P:3 * P + BLOCKS]))
            link(v.tensor_tensor_scan(out=rstd[:, :], data0=scan_b[:, :], data1=scan_b[:, :], initial=0.0,
                                      op0=ALU.add, op1=ALU.max))
            link(v.tensor_tensor(scan_b[:, :], rstd[:, :], scan_b[:, :], ALU.subtract))
            link(v.tensor_tensor(scan_b[:, :], scan_b[:, :], side[:, 2 * P:2 * P + BLOCKS], ALU.add))
            link(v.scalar_tensor_tensor(out=scan_b[:, :], in0=scan_b[:, :], scalar=-1.0, in1=deg[:, :],
                                        op0=ALU.add, op1=ALU.add))
            link(v.tensor_scalar(last_i[:, :], scan_b[:, :], 0.0, None, ALU.max))
            dve.wait_ge(stored["sage1"], 16 * GROUPS)
            walk(SAGE2)

            def sage2_out(g, half):
                dve.wait_ge(mixed["sage2"], g + 1)
                link(v.scalar_tensor_tensor(out=x_group(g), in0=mix_out(half), scalar=0.0, in1=x_group(g),
                                            op0=ALU.max, op1=ALU.add))
                norm_stats(lambda i: X[:, ds(g * G + i, 1), :].rearrange("p o f -> p (o f)"), G, g * G)

            sage2_feed = feed("sage2", lambda g, half: mean(g, half, Yn))

            def sage2_both(g, half):
                sage2_feed(g, half)
                sage2_out(g - 1, 1 - half)
            dve.wait_ge(S["h1_loaded"], 16)
            chained_groups(sage2_both, 2 + 2 * G, first=sage2_feed, last=sage2_out)
            norm_scale()
            norm_lots()

            walk(GIN)

            def gin_in(g, half):
                return v.scalar_tensor_tensor(out=fed_b[:, half, 0:G, :], in0=x_group(g), scalar=eps1[:, :],
                                              in1=acc[:, ds(g * G, G), 0:D], op0=ALU.mult, op1=ALU.add)

            def gin_stats(g):
                if isinstance(g, int) and g == GROUPS - 1:
                    up(v.bn_stats(stats[:, g, :], Y[:, g * W:N_NODES]))
                else:
                    up(v.bn_stats(stats[:, ds(g, 1), :].rearrange("p o t -> p (o t)"), Y[:, ds(g * W, W)]))

            def gin_out(n, layer):
                def f(g, half):
                    dve.wait_ge(mixed[n], g + 1)
                    ins = v.tensor_scalar(Y[:, ds(g * W, W)], ps[:, MIX_BANK + half, 0:W],
                                          vecs[:, 3 * layer:3 * layer + 1], None, ALU.add)
                    ins.then_inc(used[n], 1)
                    dve.wait_ge(used[n], g + (1 if n == "gin1" else 2))
                    settle(dve)
                    gin_stats(g)
                return f

            def gin_scale(layer):
                chain.done()
                link(v.bn_aggr(bn[:, layer, 0:2], stats[:, :, :].rearrange("p g t -> p (g t)")))
                v.tensor_scalar(bn[:, layer, 1:2], bn[:, layer, 1:2], BN_EPS, None, ALU.add).then_inc(S["sqrt_in"], 1)
                roots[0] += 1
                dve.wait_ge(S["sqrt_out"], roots[0])
                link(v.reciprocal(bn[:, layer, 2:3], bn[:, layer, 1:2]))
                link(v.tensor_tensor(bn[:, layer, 2:3], bn[:, layer, 2:3], vecs[:, 3 * layer + 1:3 * layer + 2], ALU.mult))
                link(v.tensor_tensor(bn[:, layer, 3:4], bn[:, layer, 0:1], bn[:, layer, 2:3], ALU.mult))
                v.tensor_tensor(bn[:, layer, 3:4], vecs[:, 3 * layer + 2:3 * layer + 3], bn[:, layer, 3:4],
                                ALU.subtract).then_inc(S["gin_ready"], 1)

            def gin1_both(g, half):
                feed("gin1", gin_in)(g, half)
                gin_out("gin1", 0)(g - 1, 1 - half)
            chained_groups(gin1_both, 1, first=feed("gin1", gin_in), last=gin_out("gin1", 0))
            gin_scale(0)
            dve.sem_inc(used["gin2"], 1)
            gin_out("gin2", 1)(0, 0)
            with dve.Fori(0, (GROUPS - 1) // 2 - 1) as i:
                chain.enter(i, 2)
                for half in (1, 0):
                    gin_out("gin2", 1)(2 * i + 2 - half, half)
                chain.leave((GROUPS - 1) // 2 - 1)
            gin_out("gin2", 1)(GROUPS - 2, 1)
            gin_out("gin2", 1)(GROUPS - 1, 0)
            gin_scale(1)
            dve.sem_inc(used["gin3"], 1)

            def gin3_out(g, half):
                dve.wait_ge(mixed["gin3"], g + 1)
                v.tensor_tensor(x_group(g), x_group(g), mix_out(half), ALU.add).then_inc(used["gin3"], 1)
                dve.wait_ge(used["gin3"], g + 2)
                settle(dve)
                norm_stats(lambda i: X[:, ds(g * G + i, 1), :].rearrange("p o f -> p (o f)"), G, g * G)
            chained_groups(gin3_out, 2 * G + 1)

            dve.sem_inc(used["edge"], 1)

            def edge_own(g, half):
                dve.wait_ge(mixed["edge"], g + 1)
                v.tensor_copy(Yn[:, ds(g * G, G), :], mix_out(half, OWN_BANK)).then_inc(used["edge"], 1)
            norm_groups("edge", edge_own)

            def scan_max(c, r, lap, first=False):
                a = r % 2
                dve.wait_ge(starts_here[a], 16 * (2 * lap + r // 2 + 1))
                if not first:
                    dve.wait_ge(S["scanned"], c)
                    if not isinstance(c, int) or c >= 2:
                        dve.wait_ge(S["back_turned"], c - 1)
                dve.wait_ge(S["rows_copied"], c + 1)
                v.tensor_tensor_scan(out=maxT[:, a, :], data0=starts_b[:, a, :], data1=rowsT[:, a, :],
                                     initial=-BIG if first else maxT[:, 1 - a, J * P - 1:J * P],
                                     op0=ALU.min, op1=ALU.max).then_inc(S["scanned"], 1)

            for r in range(RING):
                scan_max(r, r, 0, first=r == 0)
            with dve.Fori(1, LAPS) as lap:
                for r in range(RING):
                    scan_max(lap * RING + r, r, lap)

            def pick(m, half):
                v.tensor_copy(pick_idx[:, half, :], last_i[:, ds(m * LOT, LOT)]).then_inc(S["pick_ready"], 1)

            def edge_out(m, half, turn):
                dve.wait_ge(picked[half], 16 * LOT * (turn + 1))
                xs = X[:, ds(m * LOT, LOT), :]
                up(v.memset(lot_c, 0.0))
                link(v.tensor_tensor(lot_a, ring[:, half * J:half * J + LOT, 0:D], Yn[:, ds(m * LOT, LOT), :], ALU.add))
                link(v.scalar_tensor_tensor(out=lot_b, in0=lot_a, scalar=0.0,
                                            in1=wide(lone[:, ds(m * LOT, LOT)], D),
                                            op0=ALU.mult, op1=ALU.is_equal))
                settle(dve)
                link(v.copy_predicated(lot_c, lot_b.bitcast(i32), lot_a))
                link(v.tensor_tensor(xs, xs, lot_c, ALU.add))
                norm_stats(lambda i: X[:, ds(m * LOT + i, 1), :].rearrange("p o f -> p (o f)"), LOT, m * LOT)

            dve.wait_ge(S["back_copied"], CHUNKS)
            pick(0, 0)
            with dve.Fori(0, LOTS // 2 - 1) as i:
                chain.enter(i, 2 * (6 + 2 * LOT))
                pick(2 * i + 1, 1)
                edge_out(2 * i, 0, i)
                pick(2 * i + 2, 0)
                edge_out(2 * i + 1, 1, i)
                chain.leave(LOTS // 2 - 1)
            pick(LOTS - 1, 1)
            edge_out(LOTS - 2, 0, LOTS // 2 - 1)
            edge_out(LOTS - 1, 1, LOTS // 2 - 1)

            up(v.memset(acc_wh[:, :, D:D + 1], 1.0))
            dve.sem_inc(used["gat"], 1)

            def gat_own(g, half):
                dve.wait_ge(mixed["gat"], g + 1)
                v.tensor_copy(inv[:, ds(g * G, G)], mix_out(half, OWN_BANK)[:, :, 0]).then_inc(used["gat"], 1)
            norm_groups("gat", gat_own)

            dve.wait_ge(S["words_loaded"], 16 * 4)
            up(v.tensor_scalar(words_src, words, (1 << DST_SHIFT) - 1, None, ALU.bitwise_and))
            v.tensor_scalar(words_dst, words, DST_SHIFT, None, ALU.logical_shift_right).then_inc(S["words_ready"], 1)
            path_tables(1, (1 << DST_SHIFT) - 1, S["src_tabled"], S["src_tables_mm"])
            link(v.tensor_copy(key[:, :], words_src))

            dve.wait_ge(used["gat"], GROUPS + 1)
            up(v.memset(Y[:, NODES:ACC_BLOCKS * D], 0.0))
            dve.sem_inc(S["p_ready"], 1)
            dve.wait_ge(S["p_turned"], 1)
            v.tensor_copy(lot_a.rearrange("p b f -> p (b f)")[0:BLOCKS, 0:P], ps[0:BLOCKS, SIDE_BANK, 0:P]
                          ).then_inc(S["p_row"], 1)
            dve.wait_ge(S["p_loaded"], 16)
            dve.wait_ge(stored["gat"], 16 * GROUPS)
            walk_gat()

            pad_at = acc[:, BLOCKS - 1, D:D + 1]
            link(v.scalar_tensor_tensor(out=pad_at, in0=part_f[:, :], scalar=float(N_NODES % P), in1=pad_at,
                                        op0=ALU.is_ge, op1=ALU.add))
            link(v.reciprocal(inv[:, :], acc[:, 0:BLOCKS, D]))
            with dve.Fori(0, LOTS) as m:
                chain.enter(m, 5 + 2 * LOT)
                xs = X[:, ds(m * LOT, LOT), :]
                link(v.tensor_tensor(lot_a, acc[:, ds(m * LOT, LOT), 0:D], wide(inv[:, ds(m * LOT, LOT)], D), ALU.mult))
                v.tensor_scalar(lot_b, lot_a, 0.0, None, ALU.min).then_inc(S["h_ready"], 1)
                link(v.scalar_tensor_tensor(out=xs, in0=lot_a, scalar=0.0, in1=xs, op0=ALU.mult, op1=ALU.add))
                dve.wait_ge(S["e_ready"], m + 1)
                link(v.scalar_tensor_tensor(out=lot_b, in0=lot_a, scalar=0.0, in1=lot_b, op0=ALU.max, op1=ALU.add))
                link(v.scalar_tensor_tensor(out=xs, in0=lot_b, scalar=-1.0, in1=xs, op0=ALU.add, op1=ALU.add))
                norm_stats(lambda i: X[:, ds(m * LOT + i, 1), :].rearrange("p o f -> p (o f)"), LOT, m * LOT)
                chain.leave(LOTS)
            norm_scale()
            norm_lots()


def kernel(x, src, dst, L0_gnn_W1_l, L0_gnn_b1, L0_gnn_W1_r, L0_gnn_W2_l, L0_gnn_b2, L0_gnn_W2_r,
           L1_gnn_eps, L1_gnn_W1, L1_gnn_b1, L1_gnn_g1, L1_gnn_beta1, L1_gnn_W2, L1_gnn_b2, L1_gnn_g2,
           L1_gnn_beta2, L2_gnn_W, L2_gnn_b, L3_gnn_W, L3_gnn_a):
    import numpy as np
    import concourse.bacc as bacc
    from concourse.bass_utils import run_bass_kernel_spmd as run

    def flat(a):
        return np.ascontiguousarray(np.asarray(a))

    x, src, dst = flat(x), flat(src), flat(dst)
    pad = np.full(EDGES - N_EDGES, PAD_NODE, src.dtype)
    arrays = {
        "x": np.concatenate([x, np.zeros((NODES - N_NODES, D), x.dtype)]),
        "src": np.concatenate([src, pad]),
        "dst_before": np.concatenate([np.full(1, -1, dst.dtype), dst, pad]),
        "W1_l": flat(L0_gnn_W1_l), "W1_r": flat(L0_gnn_W1_r),
        "W2_l": flat(L0_gnn_W2_l), "W2_r": flat(L0_gnn_W2_r),
        "gin_W1t": flat(np.asarray(L1_gnn_W1).T), "gin_W2t": flat(np.asarray(L1_gnn_W2).T),
        "edge_Wt": flat(np.asarray(L2_gnn_W).T),
        "gat_W": flat(L3_gnn_W), "gat_Wt": flat(np.asarray(L3_gnn_W).T),
        "gat_a": flat(np.asarray(L3_gnn_a).reshape(2, D).T),
        "vecs": flat(np.stack([np.asarray(a) for a in (L1_gnn_b1, L1_gnn_g1, L1_gnn_beta1,
                                                       L1_gnn_b2, L1_gnn_g2, L1_gnn_beta2)], axis=1)),
        "biases": flat(np.stack([np.asarray(a) for a in (L0_gnn_b1, L0_gnn_b2, L2_gnn_b)])),
        "eps": flat(L1_gnn_eps),
    }
    nc = bacc.Bacc("TRN2", target_bir_lowering=False, num_devices=1)
    A = {n: nc.dram_tensor("in_" + n, a.shape, mybir.dt.from_np(a.dtype), kind="ExternalInput").ap()
         for n, a in arrays.items()}
    out = nc.dram_tensor("out", (N_NODES, D), mybir.dt.float32, kind="ExternalOutput").ap()
    gnn(nc, A, out)
    r = run(nc, [{"in_" + n: a for n, a in arrays.items()}], core_ids=[0])
    return r.results[0]["out"]
```

```python
import concourse.bass as bass
from concourse import mybir
from contextlib import ExitStack

P = 128
D = 128
N_NODES = 12500
N_EDGES = 200000
J = 8
CHUNK = P * J
CHUNKS = -(-N_EDGES // CHUNK)
EDGES = CHUNKS * CHUNK
COLS = CHUNKS * J
BLOCKS = -(-N_NODES // P)
NODES = BLOCKS * P
PAD_NODE = NODES - 1
STEPS = 3 * BLOCKS + 1
EMPTY = STEPS - (CHUNKS + BLOCKS - 1)
ACC_BLOCKS = BLOCKS + EMPTY
TURNS = CHUNKS - 1
RING = 4
LAPS = CHUNKS // RING
ROW = D + 2
G = 2
GROUPS = BLOCKS // G
W = G * P
LOT = 7
LOTS = BLOCKS // LOT
DST_SHIFT = 14
BLOCK_SHIFT = 7
BIG = 3.0e38
LN_EPS = 1e-5
BN_EPS = 1e-5
LRELU_SLOPE = 0.2

SAGE1, SAGE2, GIN, EDGE, GAT = range(5)
WALKS_BEFORE = {SAGE1: 0, SAGE2: 1, GIN: 2, GAT: 3}
SCATTER_AFTER = {SAGE1: 3, SAGE2: 13, GIN: 30, EDGE: 3}
COUNT_TURNS = -(-BLOCKS // 3)
assert (BLOCKS - COUNT_TURNS) % 2 == 1 and 3 * ((BLOCKS - COUNT_TURNS) // 2) <= BLOCKS
assert CHUNKS % RING == 0 and BLOCKS % G == 0 and GROUPS % 2 == 1 and EMPTY >= 0
assert NODES <= 1 << DST_SHIFT and 1 << BLOCK_SHIFT == P


class Tally:

    def __init__(self, engine, sem):
        self.engine, self.sem, self.n, self.offset = engine, sem, 0, 0

    def up(self, instruction):
        self.n += 1
        instruction.then_inc(self.sem, 1)

    def done(self):
        self.engine.wait_ge(self.sem, self.offset + self.n)

    def link(self, instruction):
        self.up(instruction)
        self.done()

    def enter(self, i, per):
        self.at, self.per, self.offset = self.n, per, i * per

    def leave(self, times):
        assert self.n - self.at == self.per, (self.n - self.at, self.per)
        self.n = self.at + self.per * times
        self.offset = 0


def gnn(nc, A, out):
    fp32, bf16, i32 = mybir.dt.float32, mybir.dt.bfloat16, mybir.dt.int32
    ALU, ACT = mybir.AluOpType, mybir.ActivationFunctionType
    ds = bass.ds

    with ExitStack() as ctx:
        def sb(name, shape, dt=fp32):
            return ctx.enter_context(nc.sbuf_tensor(name, shape, dt))

        def sem(name):
            return ctx.enter_context(nc.semaphore(name))

        def dram(name, shape, dt=fp32):
            return nc.dram_tensor(name, shape, dt, kind="Internal").ap()

        h1_rows = dram("h1_rows", (NODES, D))
        x1_rows = dram("x1_rows", (NODES, D))
        z_rows = dram("z_rows", (NODES, D))
        wh_rows = dram("wh_rows", (NODES, ROW))
        max_rows = dram("max_rows", (EDGES, D))
        starts_dram = dram("starts_dram", (EDGES,), bf16)
        place_dram = dram("place_dram", (EDGES,), i32)
        pair_dram = dram("pair_dram", (EDGES,), i32)
        sorted_dram = dram("sorted_dram", (EDGES, 1), i32)
        col_dram = dram("col_dram", (EDGES,), i32)
        p_dram = dram("p_dram", (NODES,))

        acc = sb("acc", [P, ACC_BLOCKS, D + 1])
        X = sb("X", [P, BLOCKS, D])
        Y = sb("Y", [P, ACC_BLOCKS * D])
        key = sb("key", [P, COLS], mybir.dt.int16)
        ring = sb("ring", [P, RING * J, ROW])
        onehot = sb("onehot", [P, 3, J, P])
        work = sb("work", [P, 2, J * P])
        idx_ring = sb("idx_ring", [P, RING, J], i32)
        pair_ring = sb("pair_ring", [P, RING, J], i32)
        wts = {n: sb("w_" + n, [P, D]) for n in ("l1", "r1", "l2", "r2", "g1", "g2")}
        w_edge = sb("w_edge", [P, 2 * D])
        w_gat = sb("w_gat", [P, D + 2])
        a_cols = sb("a_cols", [P, 2])
        vecs = sb("vecs", [P, 6])
        sage_bias = sb("sage_bias", [1, 2, D])
        edge_bias = sb("edge_bias", [1, D])
        eps1 = sb("eps1", [P, 1])
        ident = sb("ident", [P, P])
        below = sb("below", [P, P])
        ones = sb("ones", [P, P])
        ones_bf = sb("ones_bf", [P, 1], bf16)
        part_i = sb("part_i", [P, 1], i32)
        iota_f = sb("iota_f", [P, STEPS])
        part_f = sb("part_f", [P, 1])
        first_node = sb("first_node", [P, ACC_BLOCKS])
        samp = sb("samp", [P, 2], i32)
        sampf = sb("sampf", [P, 2])
        srow = sb("srow", [1, CHUNKS], i32)
        chunk_at = sb("chunk_at", [1, 2, STEPS], i32)
        steps_to = sb("steps_to", [1, 2, CHUNKS], i32)
        count = sb("count", [P, 3 * COUNT_TURNS])
        offs = sb("offs", [P, BLOCKS])
        inv = sb("inv", [P, BLOCKS])
        deg = sb("deg", [P, BLOCKS])
        lone = sb("lone", [P, BLOCKS])
        last_i = sb("last_i", [P, BLOCKS], i32)
        pick_idx = sb("pick_idx", [P, 2, LOT], i32)
        mv = sb("mv", [P, BLOCKS, 2])
        rstd = sb("rstd", [P, BLOCKS])
        lmv = sb("lmv", [P, LOT, 2])
        lstat = sb("lstat", [P, LOT, 6])
        bn = sb("bn", [P, 2, 4])
        ps = ctx.enter_context(nc.psum_tensor("ps", [P, 8, 512], fp32))

        Yn = Y[:, 0:NODES].rearrange("p (b f) -> p b f", f=D)
        acc_flat = acc[:, :, :].rearrange("p b f -> p (b f)")
        acc_z = acc[:, 0:BLOCKS, 0:D]
        acc_wh = acc_flat[:, 0:BLOCKS * ROW].rearrange("p (b r) -> p b r", r=ROW)
        iota_i = acc_flat[:, 0:STEPS].bitcast(i32)
        wts["at"] = Y[:, NODES:NODES + D]
        scan_b = mv[:, :, :].rearrange("p b t -> p (b t)")[:, 0:BLOCKS]
        hot = onehot[:, :, :, :].rearrange("p a j n -> p a (j n)")
        ring_flat = ring[:, :, :].rearrange("p a r -> p (a r)")
        FREE = 2 * J * ROW
        words = ring_flat[:, FREE:FREE + COLS].bitcast(i32)
        words_dst = ring_flat[:, 0:COLS].bitcast(i32)
        words_src = onehot[:, :, :, :].rearrange("p a j n -> p (a j n)")[:, 0:COLS].bitcast(i32)
        work4 = work[:, :, :].rearrange("p a (q f) -> p a q f", f=P)
        fed_b = work4[:, :, 0:2 * G, :]
        turned_b = work4[:, :, 2 * G:4 * G, :]
        rowsT = hot[:, 0:2, :]
        products = work[:, 0, :].rearrange("p (j n) -> p j n", n=P)
        score = work[:, 1, 0:3 * J].rearrange("p (a j) -> p a j", j=J)
        maxT = work[:, :, :]
        starts_b = hot[:, 2, :].bitcast(bf16).rearrange("p (a n) -> p a n", a=2)
        lot_a = hot[:, 0, 0:LOT * D].rearrange("p (b f) -> p b f", f=D)
        lot_ps = ps[:, 0:2, :].rearrange("p a n -> p (a n)")[:, 0:LOT * D].rearrange("p (b f) -> p b f", f=D)
        lot_b = hot[:, 1, 0:LOT * D].rearrange("p (b f) -> p b f", f=D)
        lot_c = hot[:, 2, 0:LOT * D].rearrange("p (b f) -> p b f", f=D)
        stats = hot[:, 2, 0:GROUPS * 6].rearrange("p (g t) -> p g t", t=6)
        before = work[:, 0, 0:STEPS].bitcast(bf16).rearrange("p (a k) -> p a k", a=2)
        SORT = NODES - 4 * COLS
        spare, place, place_i, _ = (Y[:, SORT + i * COLS:SORT + (i + 1) * COLS] for i in range(4))
        h_lot = (lot_a, lot_c)
        e_lot = (lot_b, work[:, 0, 0:LOT * D].rearrange("p (b f) -> p b f", f=D))
        bucket, mine = spare.bitcast(bf16)[:, 0:COLS], spare.bitcast(bf16)[:, COLS:2 * COLS]
        is_start = Y[:, SORT + 3 * COLS:SORT + 4 * COLS]
        raw_dst, raw_prev, raw_src, raw_key = (Y[:, i * COLS:(i + 1) * COLS].bitcast(i32) for i in range(4))
        rank = ps[:, 3:7, :].rearrange("p a n -> p (a n)")[:, 0:COLS]
        OWN_BANK, TURN_BANK, MIX_BANK, SIDE_BANK = 0, 3, 5, 7

        def by_chunk(v):
            return v.rearrange("(c p j) -> p c j", p=P, j=J)

        def as_chunks(v):
            return v.rearrange("p (c j) -> p c j", j=J)

        S = {n: sem(n) for n in """
            consts_loaded keys_loaded iotas ready_consts counted counted_mm tables_mm tabled src_tables_mm
            src_tabled chunks_here onehot_ready steps_done acc_done dve_chain act_chain pool_turn
            degrees_ready last_mm last_ready place_ready place_out starts_ready starts_out
            pair_ready pair_out h1_loaded acc_clear words_loaded words_ready col_out src_loaded
            sqrt_in sqrt_out settled normed x1_out gin_ready rows_turned rows_copied scanned back_turned
            back_copied pick_ready scores_ready weights_ready p_ready
            p_turned p_row p_out p_loaded wa_mm wa_ready h_ready e_ready out_stored
            """.split()}
        idx_here, gathered, scattered, place_here, row_stored = (
            [sem(f"{n}{r}") for r in range(RING)]
            for n in ("idx_here", "gathered", "scattered", "place_here", "row_stored"))
        picked = [sem(f"picked{a}") for a in range(2)]
        starts_here = [sem(f"starts_here{a}") for a in range(2)]
        fed, turned, copied, mixed, used, stored = (
            {n: sem(f"{w}_{n}") for n in ("sage1", "sage2", "gin1", "gin2", "gin3", "edge", "gat")}
            for w in ("fed", "turned", "copied", "mixed", "used", "stored"))

        idx_src = {q: by_chunk(A["src"]) for q in (SAGE1, SAGE2, GIN, EDGE)}
        idx_src[GAT] = by_chunk(col_dram)
        table = {SAGE1: A["x"], SAGE2: h1_rows, GIN: x1_rows, EDGE: z_rows, GAT: wh_rows}
        scatter_from = {q: sum(n for r, n in SCATTER_AFTER.items() if r < q) for q in SCATTER_AFTER}

        def settle(engine):
            engine.sem_inc(S["settled"], 1)

        def grouped(engine, body, first=None, last=None):
            (first or body)(0, 0)
            with engine.Fori(0, (GROUPS - 1) // 2) as i:
                for half in (1, 0):
                    body(2 * i + 2 - half, half)
            if last:
                last(GROUPS - 1, 0)

        def staged(engine, make, use, chain=None, per=0):
            make(0, 0)
            make(1, 1)
            make(2, 0)
            use(0, 0)
            with engine.Fori(0, (GROUPS - 3) // 2) as i:
                if chain:
                    chain.enter(i, 2 * per)
                for n in (3, 4):
                    make(2 * i + n, n % 2)
                    use(2 * i + n - 2, n % 2)
                if chain:
                    chain.leave((GROUPS - 3) // 2)
            use(GROUPS - 2, 1)
            use(GROUPS - 1, 0)

        block = ctx.enter_context(nc.Block())

        @block.sync
        def _(sp):
            def load(dst, src, s):
                sp.dma_start(dst, src).then_inc(S[s], 16)

            def stage_idx(q, r, c):
                sp.dma_start(idx_ring[:, r, :], idx_src[q][:, ds(c, 1), :].rearrange("p o j -> p (o j)")
                             ).then_inc(idx_here[r], 16)

            def stage_place(r, c):
                for to, frm in ((idx_ring, place_dram), (pair_ring, pair_dram)):
                    sp.dma_start(to[:, r, :], by_chunk(frm)[:, ds(c, 1), :].rearrange("p o j -> p (o j)")
                                 ).then_inc(place_here[r], 16)

            def announce(q, r, lap):
                sp.wait_ge(gathered[r], 16 * J * (q * LAPS + lap + 1))
                sp.sem_inc(S["chunks_here"], 1)

            def feed_gathers(q):
                with sp.Fori(0, LAPS - 1) as lap:
                    for r in range(RING):
                        announce(q, r, lap)
                        stage_idx(q, r, (lap + 1) * RING + r)
                for r in range(RING):
                    announce(q, r, LAPS - 1)

            def first_idx(q):
                for r in range(RING):
                    stage_idx(q, r, r)

            def feed_scatter(q):
                lap0, n = scatter_from[q], SCATTER_AFTER[q]
                for r in range(RING):
                    stage_place(r, lap0 * RING + r)
                with sp.Fori(lap0, lap0 + n - 1) as lap:
                    for r in range(RING):
                        sp.wait_ge(scattered[r], 16 * J * (lap + 1))
                        settle(sp)
                        stage_place(r, (lap + 1) * RING + r)
                for r in range(RING):
                    sp.wait_ge(scattered[r], 16 * J * (lap0 + n))

            first_idx(SAGE1)
            dst = A["dst_before"][1:EDGES + 1]
            firsts = dst.rearrange("(c e) -> c e", e=CHUNK)
            with nc.allow_non_contiguous_dma(reason="one word per chunk"):
                load(samp[:, 0:1], firsts[1:P + 1, 0:1], "keys_loaded")
                load(samp[0:TURNS - P, 1:2], firsts[P + 1:CHUNKS, 0:1], "keys_loaded")
                load(srow[0:1, 0:TURNS], firsts[1:CHUNKS, 0:1].rearrange("c o -> o c"), "keys_loaded")
            load(as_chunks(raw_key), by_chunk(dst), "keys_loaded")
            load(as_chunks(raw_src), by_chunk(A["src"]), "keys_loaded")
            load(raw_dst, dst.rearrange("(p t) -> p t", p=P), "keys_loaded")
            load(raw_prev, A["dst_before"][0:EDGES].rearrange("(p t) -> p t", p=P), "keys_loaded")
            for n, a in (("l1", "W1_l"), ("r1", "W1_r"), ("l2", "W2_l"), ("r2", "W2_r"),
                         ("g1", "gin_W1t"), ("g2", "gin_W2t"), ("at", "gat_Wt")):
                load(wts[n][:, :], A[a], "consts_loaded")
            load(w_edge[:, D:2 * D], A["edge_Wt"][0:P, :], "consts_loaded")
            load(w_edge[:, 0:D], A["edge_Wt"][P:2 * P, :], "consts_loaded")
            load(w_gat[:, 0:D], A["gat_W"], "consts_loaded")
            load(a_cols[:, :], A["gat_a"], "consts_loaded")
            load(vecs[:, :], A["vecs"], "consts_loaded")
            load(sage_bias[:, :, :], A["biases"][0:2, :].rearrange("(o r) f -> o r f", o=1), "consts_loaded")
            load(edge_bias[:, :], A["biases"][2:3, :], "consts_loaded")
            load(eps1[:, :], A["eps"].partition_broadcast(P), "consts_loaded")
            load(X[:, :, :], A["x"].rearrange("(b p) f -> p b f", p=P), "consts_loaded")
            sp.wait_ge(S["pair_ready"], 1)
            load(by_chunk(pair_dram), as_chunks(raw_key), "pair_out")
            sp.wait_ge(S["starts_ready"], 1)
            load(starts_dram.rearrange("(p t) -> p t", p=P),
                 Y[:, COLS:COLS + COLS // 2].bitcast(bf16), "starts_out")
            feed_gathers(SAGE1)
            sp.wait_ge(S["place_ready"], 1)
            load(by_chunk(place_dram), as_chunks(place_i.bitcast(i32)), "place_out")
            sp.wait_ge(S["pair_out"], 16)
            sp.wait_ge(S["starts_out"], 16)
            sp.wait_ge(S["place_out"], 16)
            feed_scatter(SAGE1)

            first_idx(SAGE2)
            sp.wait_ge(stored["sage1"], 16 * GROUPS)
            load(Yn[:, :, :], h1_rows.rearrange("(b p) f -> p b f", p=P), "h1_loaded")
            feed_gathers(SAGE2)
            feed_scatter(SAGE2)

            first_idx(GIN)
            feed_gathers(GIN)
            feed_scatter(GIN)

            first_idx(EDGE)
            def load_starts(a, c):
                sp.dma_start(starts_b[:, a, :], starts_dram.rearrange("(c e) -> c e", e=CHUNK)
                             [ds(c, 1), :].rearrange("o e -> (o e)").partition_broadcast(P)
                             ).then_inc(starts_here[a], 16)

            def store_max(r, c):
                sp.dma_start(max_rows.rearrange("(c p j) f -> c p j f", p=P, j=J)[ds(c, 1), :, :, :]
                             .rearrange("o p j f -> p (o j) f"),
                             ring[:, r * J:(r + 1) * J, 0:D]).then_inc(row_stored[r], 16)

            def edge_chunk(c, lap, r, first=False, refill=True):
                announce(EDGE, r, lap)
                if refill:
                    stage_idx(EDGE, r, c + RING)
                if not first or r >= 1:
                    sp.wait_ge(S["scanned"], c)
                    settle(sp)
                if refill or r < RING - 1:
                    load_starts((r + 1) % 2, c + 1)
                if not first or r >= 2:
                    sp.wait_ge(S["back_copied"], c - 1)
                    settle(sp)
                    store_max((r - 2) % RING, c - 2)

            sp.wait_ge(used["edge"], 1)
            load_starts(0, 0)
            for r in range(RING):
                edge_chunk(r, 0, r, first=True)
            with sp.Fori(1, LAPS - 1) as lap:
                for r in range(RING):
                    edge_chunk(lap * RING + r, lap, r)
            for r in range(RING):
                edge_chunk(CHUNKS - RING + r, LAPS - 1, r, refill=False)
            for c in (CHUNKS - 2, CHUNKS - 1):
                sp.wait_ge(S["back_copied"], c + 1)
                store_max(c % RING, c)

            for r in range(RING):
                sp.wait_ge(row_stored[r], 16 * LAPS)
            feed_scatter(EDGE)
            load(as_chunks(words), by_chunk(sorted_dram.rearrange("e o -> (e o)")), "words_loaded")
            firsts = sorted_dram.rearrange("(c e) o -> c (e o)", e=CHUNK)
            with nc.allow_non_contiguous_dma(reason="one word per chunk"):
                load(samp[:, 0:1], firsts[1:P + 1, 0:1], "words_loaded")
                load(samp[0:TURNS - P, 1:2], firsts[P + 1:CHUNKS, 0:1], "words_loaded")
                load(srow[0:1, 0:TURNS], firsts[1:CHUNKS, 0:1].rearrange("c o -> o c"), "words_loaded")
            sp.wait_ge(S["words_ready"], 1)
            load(by_chunk(col_dram), as_chunks(words_dst), "col_out")

            sp.wait_ge(S["col_out"], 16)
            first_idx(GAT)
            sp.wait_ge(S["p_row"], 1)
            load(p_dram.rearrange("(b p) -> b p", p=P), lot_a.rearrange("p b f -> p (b f)")[0:BLOCKS, 0:P], "p_out")
            sp.wait_ge(S["p_out"], 16)
            load(Y[:, 0:NODES], p_dram.partition_broadcast(P), "p_loaded")
            feed_gathers(GAT)

            full = N_NODES // P
            with sp.Fori(0, LOTS - 1) as m:
                sp.wait_ge(S["normed"], LOTS + m + 1)
                settle(sp)
                sp.dma_start(out[0:(LOTS - 1) * LOT * P, :].rearrange("(m b p) f -> m p b f", b=LOT, p=P)
                             [ds(m, 1), :, :, :].rearrange("o p b f -> p (o b) f"),
                             X[:, ds(m * LOT, LOT), :]).then_inc(S["out_stored"], 16)
            sp.wait_ge(S["normed"], 2 * LOTS)
            b0 = (LOTS - 1) * LOT
            sp.dma_start(out[b0 * P:full * P, :].rearrange("(b p) f -> p b f", p=P),
                         X[:, b0:full, :]).then_inc(S["out_stored"], 16)
            sp.dma_start(out[full * P:N_NODES, :], X[0:N_NODES - full * P, full, :]).then_inc(S["out_stored"], 16)
            sp.wait_ge(S["out_stored"], 16 * (LOTS + 1))

        @block.gpsimd
        def _(pool):
            pool.iota(iota_i[:, :], [[1, STEPS]], base=0, channel_multiplier=0).then_inc(S["iotas"], 1)
            pool.iota(part_i[:, :], [[1, 1]], base=0, channel_multiplier=1).then_inc(S["iotas"], 1)

            def gather_chunk(q, r):
                cols = ROW if q == GAT else D
                for j in range(J):
                    pool.indirect_dma_start(
                        ring[:, r * J + j, 0:cols], None, table[q],
                        bass.IndirectOffsetOnAxis(idx_ring[:, r, j:j + 1], 0)).then_inc(gathered[r], 16)

            def gathers(q):
                for r in range(RING):
                    pool.wait_ge(idx_here[r], 16 * (q * LAPS + 1))
                    gather_chunk(q, r)
                if q != EDGE:
                    pool.wait_ge(S["src_tabled" if q == GAT else "tabled"], 2)
                with pool.Fori(1, LAPS) as lap:
                    for r in range(RING):
                        pool.wait_ge(idx_here[r], 16 * (q * LAPS + lap + 1))
                        if q == EDGE:
                            pool.wait_ge(row_stored[r], 16 * lap)
                        else:
                            side = int(q == GAT)
                            n = pool.value_load(steps_to[0:1, side, ds((lap - 1) * RING + r, 1)],
                                                min_val=1, max_val=STEPS)
                            pool.wait_ge(S["steps_done"], n + WALKS_BEFORE[q] * STEPS)
                        pool.sem_inc(S["pool_turn"], 1)
                        gather_chunk(q, r)

            def scatters(q):
                with pool.Fori(scatter_from[q], scatter_from[q] + SCATTER_AFTER[q]) as lap:
                    for r in range(RING):
                        pool.wait_ge(place_here[r], 32 * (lap + 1))
                        pool.sem_inc(S["pool_turn"], 1)
                        for j in range(J):
                            pool.indirect_dma_start(
                                sorted_dram, bass.IndirectOffsetOnAxis(idx_ring[:, r, j:j + 1], 0),
                                pair_ring[:, r, j:j + 1], None).then_inc(scattered[r], 16)

            gathers(SAGE1)
            scatters(SAGE1)
            pool.wait_ge(stored["sage1"], 16 * GROUPS)
            gathers(SAGE2)
            scatters(SAGE2)
            pool.wait_ge(S["x1_out"], 16 * LOTS)
            gathers(GIN)
            scatters(GIN)
            pool.wait_ge(stored["edge"], 16 * GROUPS)
            gathers(EDGE)
            for r in range(RING):
                pool.wait_ge(row_stored[r], 16 * LAPS)
            with pool.Fori(0, LOTS // 2) as i:
                for half in range(2):
                    pool.wait_ge(S["pick_ready"], 2 * i + half + 1)
                    pool.sem_inc(S["pool_turn"], 1)
                    for b in range(LOT):
                        pool.indirect_dma_start(
                            ring[:, half * J + b, 0:D], None, max_rows,
                            bass.IndirectOffsetOnAxis(pick_idx[:, half, b:b + 1], 0)
                        ).then_inc(picked[half], 16)
            scatters(EDGE)
            pool.wait_ge(stored["gat"], 16 * GROUPS)
            gathers(GAT)

        @block.tensor
        def _(pe):
            def mm(o, lhsT, rhs, start=True, stop=True):
                return nc.tensor.matmul(o, lhsT, rhs, start=start, stop=stop)

            def turn(o, a):
                return nc.tensor.transpose(o, a, ident[:, :])

            def path_sum(done):
                mm(ps[0:1, SIDE_BANK, 0:STEPS], ones_bf[:, :], before[:, 0, :], stop=False)
                mm(ps[0:1, SIDE_BANK, 0:STEPS], ones_bf[0:TURNS - P, :], before[0:TURNS - P, 1, :],
                   start=False).then_inc(done, 1)

            def walk(q, between=None):
                side = int(q == GAT)
                base = WALKS_BEFORE[q] * STEPS

                def step(k, buf):
                    c = pe.value_load(chunk_at[0:1, side, ds(k, 1)], min_val=0, max_val=CHUNKS - 1)
                    pe.wait_ge(S["chunks_here"], c + (q * CHUNKS + 1))
                    if q == GAT:
                        pe.wait_ge(S["weights_ready"], k + 1)
                    else:
                        pe.wait_ge(S["onehot_ready"], k + (base + 1))
                    for j in range(J):
                        last = mm(ps[:, buf, 0:D + 1], onehot[:, buf, j, :],
                                  ring[:, ds((c & (RING - 1)) * J + j, 1), 0:D + 1]
                                  .rearrange("p o f -> p (o f)"),
                                  start=j == 0, stop=j == J - 1)
                    last.then_inc(S["steps_done"], 1)

                step(0, 0)
                parts = ((0, COUNT_TURNS), (COUNT_TURNS, BLOCKS - COUNT_TURNS)) if between else ((0, BLOCKS),)
                for start, turns in parts:
                    if start:
                        between()
                    with pe.Fori(0, turns) as i:
                        for n in (1, 2, 3):
                            step(3 * i + (3 * start + n), n % 3)

            def dense(n, turn_of, mix_of):
                def both(g, half):
                    turn_of(g, half)
                    mix_of(g - 1, 1 - half)

                def last(g, half):
                    if n in ("sage2", "gin1"):
                        pe.wait_ge(used[n], GROUPS - 2)
                    mix_of(g, half)
                grouped(pe, both, first=turn_of, last=last)

            def bank(which, half):
                return ps[:, which + half, :]

            def turn_sage(n):
                def f(g, half):
                    pe.wait_ge(fed[n], g + 1)
                    o = bank(TURN_BANK, half)
                    for i in range(2 * G):
                        last = turn(o[:, i * P:(i + 1) * P], fed_b[:, half, i, :])
                    last.then_inc(turned[n], 1)
                return f

            def mix_sage(n, layer):
                def f(g, half):
                    pe.wait_ge(copied[n], g + 1)
                    o = bank(MIX_BANK, half)
                    for i in range(G):
                        at = o[:, i * D:(i + 1) * D]
                        mm(at, ones[0:1, :], sage_bias[0:1, layer, :], stop=False)
                        mm(at, turned_b[:, half, i, :], wts[f"l{layer + 1}"][:, :], start=False, stop=False)
                        last = mm(at, turned_b[:, half, G + i, :], wts[f"r{layer + 1}"][:, :], start=False)
                    last.then_inc(mixed[n], 1)
                return f

            def turn_nodes(n):
                def f(g, half):
                    pe.wait_ge(fed[n], g + 1)
                    for i in range(G):
                        last = turn(bank(TURN_BANK, half)[:, i * P:(i + 1) * P], fed_b[:, half, i, :])
                    last.then_inc(turned[n], 1)
                return f

            def mix_gin(n, w):
                def f(g, half):
                    pe.wait_ge(copied[n], g + 1)
                    mm(bank(MIX_BANK, half)[:, 0:W], w[:, :],
                       turned_b[:, half, 0:G, :].rearrange("p i n -> p (i n)")).then_inc(mixed[n], 1)
                return f

            def mix_nodes(n, w, w_own, bias=None):
                def f(g, half):
                    pe.wait_ge(copied[n], g + 1)
                    pe.wait_ge(used[n], g + 1)
                    cols, own = w.shape[1], w_own.shape[1]
                    for i in range(G):
                        mm(bank(MIX_BANK, half)[:, i * W:i * W + cols], turned_b[:, half, i, :], w)
                    for i in range(G):
                        at = bank(OWN_BANK, half)[:, i * D:i * D + own]
                        if bias is not None:
                            mm(at, ones[0:1, :], bias, stop=False)
                        last = mm(at, turned_b[:, half, i, :], w_own, start=bias is None)
                    last.then_inc(mixed[n], 1)
                return f

            pe.wait_ge(S["ready_consts"], 1)
            pe.wait_ge(S["tabled"], 1)
            path_sum(S["tables_mm"])
            pe.wait_ge(S["consts_loaded"], 16 * 16)
            mm(ps[:, SIDE_BANK - 1, 0:2], wts["at"][:, :], a_cols[:, :]).then_inc(S["wa_mm"], 1)
            pe.wait_ge(S["tabled"], 2)

            def sum_counts():
                pe.wait_ge(S["counted"], 1)
                mm(ps[:, SIDE_BANK, 0:BLOCKS], below[:, :], count[:, 0:BLOCKS])
                mm(ps[:, SIDE_BANK, P:P + BLOCKS], ones[:, :], count[:, 0:BLOCKS]).then_inc(S["counted_mm"], 1)
            walk(SAGE1, sum_counts)

            pe.wait_ge(S["degrees_ready"], 1)
            mm(ps[:, SIDE_BANK, 2 * P:2 * P + BLOCKS], below[:, :], deg[:, :])
            mm(ps[:, SIDE_BANK, 3 * P:3 * P + BLOCKS], ones[:, :], deg[:, :]).then_inc(S["counted_mm"], 1)
            dense("sage1", turn_sage("sage1"), mix_sage("sage1", 0))
            walk(SAGE2)
            dense("sage2", turn_sage("sage2"), mix_sage("sage2", 1))
            walk(GIN)
            dense("gin1", turn_nodes("gin1"), mix_gin("gin1", wts["g1"]))
            grouped(pe, mix_gin("gin2", wts["g2"]))

            def turn_back(g, half):
                pe.wait_ge(copied["gin3"], g + 1)
                for i in range(G):
                    last = turn(bank(MIX_BANK, half)[:, i * P:(i + 1) * P], turned_b[:, half, i, :])
                last.then_inc(mixed["gin3"], 1)
            grouped(pe, turn_back)
            dense("edge", turn_nodes("edge"), mix_nodes("edge", w_edge[:, 0:D], w_edge[:, D:2 * D], edge_bias[:, :]))

            def rows_turn(c, r):
                pe.wait_ge(S["chunks_here"], c + (EDGE * CHUNKS + 1))
                for j in range(J):
                    last = turn(ps[:, 2 * (r % 2) + j // 4, (j % 4) * P:(j % 4 + 1) * P],
                                ring[:, r * J + j, 0:D])
                last.then_inc(S["rows_turned"], 1)

            def back_turn(c, r):
                pe.wait_ge(S["scanned"], c + 1)
                for j in range(J):
                    last = turn(ps[:, 4 + 2 * (r % 2) + j // 4, (j % 4) * P:(j % 4 + 1) * P],
                                maxT[:, r % 2, :].rearrange("f (p j) -> f j p", j=J)[:, j, :])
                last.then_inc(S["back_turned"], 1)

            pe.wait_ge(used["edge"], GROUPS + 1)
            rows_turn(0, 0)
            for r in range(1, RING):
                rows_turn(r, r)
                back_turn(r - 1, r - 1)
            with pe.Fori(1, LAPS) as lap:
                for r in range(RING):
                    rows_turn(lap * RING + r, r)
                    back_turn(lap * RING + r - 1, (r - 1) % RING)
            back_turn(CHUNKS - 1, RING - 1)

            dense("gat", turn_nodes("gat"), mix_nodes("gat", w_gat[:, :], w_gat[:, D:D + 1]))
            pe.wait_ge(S["src_tabled"], 1)
            path_sum(S["src_tables_mm"])
            pe.wait_ge(S["src_tabled"], 2)
            pe.wait_ge(S["p_ready"], 1)
            turn(ps[0:BLOCKS, SIDE_BANK, 0:P], inv[:, :]).then_inc(S["p_turned"], 1)
            walk(GAT)

        @block.scalar
        def _(act):
            chain = Tally(act, S["act_chain"])
            roots = [0]

            def root():
                roots[0] += 1
                act.wait_ge(S["sqrt_in"], roots[0])
                what = bn[:, 0, 1:2] if roots[0] == 2 else bn[:, 1, 1:2] if roots[0] == 3 else rstd[:, :]
                nc.scalar.activation(what, what, ACT.Sqrt).then_inc(S["sqrt_out"], 1)

            def copy_turned(n, width):
                def f(g, half):
                    act.wait_ge(turned[n], g + 1)
                    nc.scalar.copy(turned_b[:, half, 0:width, :].rearrange("p q n -> p (q n)"),
                                   ps[:, TURN_BANK + half, 0:width * P]).then_inc(copied[n], 1)
                return f

            def dense(first, use):
                def both(g, half):
                    first(g, half)
                    use(g - 1, 1 - half)
                grouped(act, both, first=first, last=use)

            def store_group(n, rows, src, cols):
                act.dma_start(rows.rearrange("(g b p) f -> g p b f", p=P, b=G)[ds(cols, 1), :, :, :]
                              .rearrange("o p b f -> p (o b) f"), src).then_inc(stored[n], 16)

            def use_sage1(g, half):
                act.wait_ge(mixed["sage1"], g + 1)
                to = acc[:, ds(g * G, G), 0:D]
                nc.scalar.activation(to, ps[:, MIX_BANK + half, 0:W].rearrange("p (i f) -> p i f", i=G),
                                     ACT.Relu).then_inc(used["sage1"], 1)
                act.wait_ge(used["sage1"], g + 1)
                store_group("sage1", h1_rows, to, g)

            dense(copy_turned("sage1", 2 * G), use_sage1)
            grouped(act, copy_turned("sage2", 2 * G))
            root()
            with act.Fori(0, LOTS) as m:
                act.wait_ge(S["normed"], m + 1)
                act.dma_start(x1_rows.rearrange("(m b p) f -> m p b f", b=LOT, p=P)[ds(m, 1), :, :, :]
                              .rearrange("o p b f -> p (o b) f"),
                              X[:, ds(m * LOT, LOT), :]).then_inc(S["x1_out"], 16)
            grouped(act, copy_turned("gin1", G))
            root()

            def normed_relu(n, layer):
                def f(g, half):
                    act.wait_ge(used[n], g + 1)
                    nc.scalar.activation(turned_b[:, half, 0:G, :].rearrange("p q n -> p (q n)"),
                                         Y[:, ds(g * W, W)], ACT.Relu, bias=bn[:, layer, 3:4],
                                         scale=bn[:, layer, 2:3]).then_inc(copied[n], 1)
                return f

            act.wait_ge(S["gin_ready"], 1)
            grouped(act, normed_relu("gin2", 0))
            root()
            act.wait_ge(S["gin_ready"], 2)
            grouped(act, normed_relu("gin3", 1))
            root()

            def use_edge(g, half):
                act.wait_ge(mixed["edge"], g + 1)
                to = acc[:, ds(g * G, G), 0:D]
                frm = ps[:, MIX_BANK + half, :].rearrange("p (i f) -> p i f", i=G)
                chain.link(nc.scalar.copy(to, frm[:, :, 0:D]))
                store_group("edge", z_rows, to, g)

            def looped_dense(first, use, per):
                first(0, 0)
                with act.Fori(0, (GROUPS - 1) // 2) as i:
                    chain.enter(i, 2 * per)
                    for half in (1, 0):
                        first(2 * i + 2 - half, half)
                        use(2 * i + 1 - half, 1 - half)
                    chain.leave((GROUPS - 1) // 2)
                use(GROUPS - 1, 0)

            looped_dense(copy_turned("edge", G), use_edge, 1)

            def rows_copy(c, r):
                act.wait_ge(S["rows_turned"], c + 1)
                nc.scalar.copy(rowsT[:, r % 2, :].rearrange("f (p j) -> f j p", j=J),
                               ps[:, 2 * (r % 2):2 * (r % 2) + 2, :].rearrange("f a (j p) -> f (a j) p", p=P)
                               ).then_inc(S["rows_copied"], 1)

            def back_copy(c, r):
                act.wait_ge(S["back_turned"], c + 1)
                a = 4 + 2 * (r % 2)
                nc.scalar.copy(ring[:, r * J:(r + 1) * J, 0:D],
                               ps[:, a:a + 2, :].rearrange("p a (j f) -> p (a j) f", f=D)
                               ).then_inc(S["back_copied"], 1)

            rows_copy(0, 0)
            for r in range(1, RING):
                rows_copy(r, r)
                back_copy(r - 1, r - 1)
            with act.Fori(1, LAPS) as lap:
                for r in range(RING):
                    rows_copy(lap * RING + r, r)
                    back_copy(lap * RING + r - 1, (r - 1) % RING)
            back_copy(CHUNKS - 1, RING - 1)
            root()

            def use_gat(g, half):
                act.wait_ge(mixed["gat"], g + 1)
                frm = ps[:, MIX_BANK + half, :].rearrange("p (i f) -> p i f", i=G)
                chain.up(nc.scalar.copy(acc_wh[:, ds(g * G, G), 0:D], frm[:, :, 0:D]))
                chain.link(nc.scalar.copy(acc_wh[:, ds(g * G, G), D + 1:D + 2], frm[:, :, D + 1:D + 2]))
                store_group("gat", wh_rows, acc_wh[:, ds(g * G, G), :], g)

            looped_dense(copy_turned("gat", G), use_gat, 2)

            def weigh(k, n):
                act.wait_ge(S["scores_ready"], k + 1)
                chain.link(nc.scalar.activation(score[:, n % 3, :], score[:, n % 3, :], ACT.Exp, scale=-1.0))
                for j in range(J):
                    at = onehot[:, n % 3, j, :]
                    last = nc.scalar.mul(at, at, score[:, n % 3, j:j + 1])
                last.then_inc(S["weights_ready"], 1)
            weigh(0, 0)
            with act.Fori(0, BLOCKS // 2) as i:
                chain.enter(i, 6)
                for n in range(1, 7):
                    weigh(6 * i + n, n)
                chain.leave(BLOCKS // 2)
            with act.Fori(0, LOTS // 2) as i:
                chain.enter(i, 2)
                for n in range(2):
                    act.wait_ge(S["h_ready"], 2 * i + n + 1)
                    chain.link(nc.scalar.activation(e_lot[n], h_lot[n], ACT.Relu, scale=-1.0))
                    nc.scalar.activation(e_lot[n], e_lot[n], ACT.Exp, scale=-1.0).then_inc(S["e_ready"], 1)
                chain.leave(LOTS // 2)
            root()

        @block.vector
        def _(dve):
            v = nc.vector
            chain = Tally(dve, S["dve_chain"])
            up, link = chain.up, chain.link
            roots = [0]

            def wide(t, n):
                return t.unsqueeze(2).to_broadcast([P, t.shape[1], n])

            def path_tables(side, mask, tabled, mm_done):
                for a, n in ((0, P), (1, TURNS - P)):
                    if mask:
                        up(v.tensor_scalar(samp[0:n, a:a + 1], samp[0:n, a:a + 1], mask, BLOCK_SHIFT,
                                           ALU.bitwise_and, ALU.logical_shift_right))
                    else:
                        up(v.tensor_scalar(samp[0:n, a:a + 1], samp[0:n, a:a + 1], BLOCK_SHIFT, None,
                                           ALU.logical_shift_right))
                if mask:
                    link(v.tensor_scalar(srow[:, 0:TURNS], srow[:, 0:TURNS], mask, BLOCK_SHIFT,
                                         ALU.bitwise_and, ALU.logical_shift_right))
                else:
                    link(v.tensor_scalar(srow[:, 0:TURNS], srow[:, 0:TURNS], BLOCK_SHIFT, None,
                                         ALU.logical_shift_right))
                up(v.scalar_tensor_tensor(out=sampf[:, 0:1], in0=samp[:, 0:1], scalar=0.0, in1=part_f[:, :],
                                          op0=ALU.add, op1=ALU.add))
                up(v.scalar_tensor_tensor(out=sampf[0:TURNS - P, 1:2], in0=samp[0:TURNS - P, 1:2],
                                          scalar=float(P), in1=part_f[0:TURNS - P, :], op0=ALU.add, op1=ALU.add))
                link(v.scalar_tensor_tensor(out=steps_to[:, side, 0:TURNS], in0=srow[:, 0:TURNS], scalar=1.0,
                                            in1=iota_f[0:1, 0:TURNS], op0=ALU.add, op1=ALU.add))
                up(v.tensor_scalar(before[:, 0, :], iota_f[:, :], sampf[:, 0:1], None, ALU.is_gt))
                v.tensor_scalar(before[0:TURNS - P, 1, :], iota_f[0:TURNS - P, :], sampf[0:TURNS - P, 1:2],
                                None, ALU.is_gt).then_inc(tabled, 1)
                dve.wait_ge(mm_done, 1)
                v.tensor_copy(chunk_at[:, side, :], ps[0:1, SIDE_BANK, 0:STEPS]).then_inc(tabled, 1)
                dve.wait_ge(tabled, 2)

            def chunk_of(side, k):
                return dve.value_load(chunk_at[0:1, side, ds(k, 1)], min_val=0, max_val=CHUNKS - 1)

            def block_of(k, c):
                return (k - c).with_bounds(min_val=0, max_val=ACC_BLOCKS - 1)

            def one_hot(side, k, buf, c=None):
                c = chunk_of(side, k) if c is None else c
                return c, v.scalar_tensor_tensor(
                    out=onehot[:, buf, :, :], in0=wide(key[:, ds(c * J, J)], P),
                    scalar=first_node[:, ds(block_of(k, c), 1)],
                    in1=iota_f[:, 0:P].unsqueeze(1).to_broadcast([P, J, P]), op0=ALU.subtract, op1=ALU.is_equal)

            def add_step(q, k, buf, c=None):
                base = WALKS_BEFORE[q] * STEPS
                c = chunk_of(int(q == GAT), k) if c is None else c
                to = acc[:, ds(block_of(k, c), 1), :].rearrange("p o f -> p (o f)")
                dve.wait_ge(S["acc_done"], k + (base + WALKS_BEFORE[q] + 1))
                dve.wait_ge(S["steps_done"], k + (base + 1))
                v.tensor_tensor(to, to, ps[:, buf, 0:D + 1], ALU.add).then_inc(S["acc_done"], 1)

            def clear_acc():
                v.memset(acc[:, :, :], 0.0).then_inc(S["acc_done"], 1)

            def walk(q, parts=((BLOCKS, 1, None, 0),), between=None):
                clear_acc()
                _, ins = one_hot(0, 0, 0)
                ins.then_inc(S["onehot_ready"], 1)
                start = 0
                for turns, triples, hook, per in parts:
                    if start:
                        between(start)
                    with dve.Fori(0, turns) as i:
                        chain.enter(i, per)
                        c = chunk_of(0, 3 * triples * i + 3 * start)
                        for n in range(1, 3 * triples + 1):
                            k = 3 * triples * i + (3 * start + n)
                            c_next, ins = one_hot(0, k, n % 3)
                            ins.then_inc(S["onehot_ready"], 1)
                            add_step(q, k - 1, (n - 1) % 3, c)
                            c = c_next
                        if hook:
                            hook(i)
                        chain.leave(turns)
                    start += turns * triples
                assert start == BLOCKS
                add_step(q, STEPS - 1, (STEPS - 1) % 3)
                dve.wait_ge(S["acc_done"], (WALKS_BEFORE[q] + 1) * (STEPS + 1))

            def walk_gat():
                def step(k, n, c, c_next_at, c_before=None):
                    buf = n % 3
                    _, ins = one_hot(1, k, buf, c)
                    up(ins)
                    b = block_of(k, c) if not isinstance(k, int) or k else 0
                    c_next = c_next_at and chunk_of(1, k + 1)
                    chain.done()
                    up(v.tensor_tensor(products, onehot[:, buf, :, :],
                                       Y[:, ds(b * P, P)].unsqueeze(1).to_broadcast([P, J, P]), ALU.mult))
                    if c_before is not None:
                        add_step(GAT, k - 2, (n - 2) % 3, c_before)
                    chain.done()
                    link(v.tensor_reduce(score[:, buf, :], products, mybir.AxisListType.X, ALU.add))
                    dve.wait_ge(S["chunks_here"], c + (GAT * CHUNKS + 1))
                    link(v.tensor_tensor(score[:, buf, :], score[:, buf, :],
                                         ring[:, ds((c & (RING - 1)) * J, J), D + 1], ALU.add))
                    v.scalar_tensor_tensor(out=score[:, buf, :], in0=score[:, buf, :], scalar=LRELU_SLOPE,
                                           in1=score[:, buf, :], op0=ALU.mult, op1=ALU.max
                                           ).then_inc(S["scores_ready"], 1)
                    return c_next

                def run(ks, offset):
                    cs = {ks[0] - 2: chunk_of(1, offset + ks[0] - 2), ks[0] - 1: chunk_of(1, offset + ks[0] - 1),
                          ks[0]: chunk_of(1, offset + ks[0])}
                    for k in ks:
                        cs[k + 1] = step(offset + k, k, cs[k], k != ks[-1], cs[k - 2])

                clear_acc()
                c = step(0, 0, chunk_of(1, 0), True)
                step(1, 1, c, False)
                with dve.Fori(0, (STEPS - 7) // 6) as i:
                    chain.enter(i, 6 * 4)
                    run(range(2, 8), 6 * i)
                    chain.leave((STEPS - 7) // 6)
                run(range(6 * ((STEPS - 7) // 6) + 2, STEPS), 0)
                add_step(GAT, STEPS - 2, (STEPS - 2) % 3)
                add_step(GAT, STEPS - 1, (STEPS - 1) % 3)
                dve.wait_ge(S["acc_done"], 4 * (STEPS + 1))

            def norm_stats(at, n, first_block):
                settle(dve)
                for i in range(n):
                    up(v.bn_stats(lstat[:, i, :], at(i)))
                chain.done()
                settle(dve)
                for i in range(n):
                    up(v.bn_aggr(lmv[:, i, :], lstat[:, i, :]))
                chain.done()
                up(v.tensor_copy(mv[:, ds(first_block, n), :], lmv[:, 0:n, :]))

            def norm_scale():
                chain.done()
                v.tensor_scalar(rstd[:, :], mv[:, :, 1], LN_EPS, None, ALU.add).then_inc(S["sqrt_in"], 1)
                roots[0] += 1
                dve.wait_ge(S["sqrt_out"], roots[0])
                link(v.reciprocal(rstd[:, :], rstd[:, :]))

            def norm_block(b, to=None):
                at = X[:, ds(b, 1), :].rearrange("p o f -> p (o f)")
                return v.tensor_scalar(at if to is None else to, at, mv[:, ds(b, 1), 0:1].rearrange("p o t -> p (o t)"),
                                       rstd[:, ds(b, 1)], ALU.subtract, ALU.mult)

            def norm_lots():
                def less_mean(m):
                    xs = X[:, ds(m * LOT, LOT), :]
                    up(v.tensor_tensor(xs, xs, wide(mv[:, ds(m * LOT, LOT), 0], D), ALU.subtract))

                def scaled(m):
                    xs = X[:, ds(m * LOT, LOT), :]
                    v.tensor_tensor(xs, xs, wide(rstd[:, ds(m * LOT, LOT)], D), ALU.mult).then_inc(S["normed"], 1)

                less_mean(0)
                with dve.Fori(1, LOTS) as m:
                    chain.enter(m - 1, 1)
                    chain.done()
                    less_mean(m)
                    scaled(m - 1)
                    chain.leave(LOTS - 1)
                chain.done()
                scaled(LOTS - 1)

            def norm_groups(n, out_of):
                norm_scale()

                def make(g, half):
                    for i in range(G):
                        last = norm_block(g * G + i, fed_b[:, half, i, :])
                    return last

                def norm(g, half):
                    feed(n, make)(g, half)
                    for i in range(G):
                        norm_block(g * G + i)

                staged(dve, norm, out_of)

            def chained_groups(body, per, first=None, last=None):
                (first or body)(0, 0)
                with dve.Fori(0, (GROUPS - 1) // 2) as i:
                    chain.enter(i, 2 * per)
                    for half in (1, 0):
                        body(2 * i + 2 - half, half)
                    chain.leave((GROUPS - 1) // 2)
                if last:
                    last(GROUPS - 1, 0)

            def feed(n, make):
                def f(g, half):
                    if not isinstance(g, int) or g > 1:
                        dve.wait_ge(turned[n], g - 1)
                    make(g, half).then_inc(fed[n], 1)
                return f

            def mean(g, half, other):
                v.tensor_copy(fed_b[:, half, G:2 * G, :], other[:, ds(g * G, G), :])
                return v.tensor_tensor(fed_b[:, half, 0:G, :], acc[:, ds(g * G, G), 0:D],
                                       wide(inv[:, ds(g * G, G)], D), ALU.mult)

            def x_group(g):
                return X[:, ds(g * G, G), :]

            def mix_out(half, which=MIX_BANK):
                return ps[:, which + half, 0:W].rearrange("p (i f) -> p i f", i=G)

            dve.wait_ge(S["iotas"], 2)
            up(v.tensor_copy(iota_f[:, :], iota_i[:, :]))
            up(v.tensor_copy(part_f[:, :], part_i[:, :]))
            up(v.memset(ones[:, :], 1.0))
            up(v.memset(ones_bf[:, :], 1.0))
            up(v.memset(ring[:, :, D:ROW], 1.0))
            chain.done()
            up(v.tensor_scalar(first_node[:, :], iota_f[:, 0:ACC_BLOCKS], float(P), None, ALU.mult))
            up(v.tensor_scalar(below[:, :], iota_f[:, 0:P], part_f[:, :], None, ALU.is_gt))
            up(v.tensor_scalar(ident[:, :], iota_f[:, 0:P], part_f[:, :], None, ALU.is_equal))
            chain.done()
            dve.wait_ge(S["keys_loaded"], 16 * 7)
            up(v.tensor_copy(key[:, :], raw_key))
            dve.sem_inc(S["ready_consts"], 1)
            path_tables(0, 0, S["tabled"], S["tables_mm"])
            up(v.tensor_scalar(place_i.bitcast(i32), raw_src, BLOCK_SHIFT, None, ALU.logical_shift_right))
            link(v.tensor_scalar(raw_key, raw_key, DST_SHIFT, None, ALU.logical_shift_left))
            up(v.tensor_copy(bucket, place_i.bitcast(i32)))
            up(v.memset(place, 0.0))
            v.tensor_tensor(raw_key, raw_key, raw_src, ALU.bitwise_or).then_inc(S["pair_ready"], 1)
            link(v.tensor_tensor(is_start, raw_dst, raw_prev, ALU.is_equal))
            link(v.tensor_scalar(is_start, is_start, 2.0, -1.0, ALU.mult, ALU.add))
            v.tensor_scalar(Y[:, COLS:COLS + COLS // 2].bitcast(bf16), is_start, BIG, None, ALU.mult
                            ).then_inc(S["starts_ready"], 1)
            dve.wait_ge(S["consts_loaded"], 16 * 16)
            up(v.tensor_tensor(w_edge[:, D:2 * D], w_edge[:, D:2 * D], w_edge[:, 0:D], ALU.subtract))
            up(v.tensor_scalar(eps1[:, :], eps1[:, :], 1.0, None, ALU.add))
            dve.wait_ge(S["wa_mm"], 1)
            link(v.tensor_copy(w_gat[:, D:D + 2], ps[:, SIDE_BANK - 1, 0:2]))

            def count_bucket(h):
                link(v.tensor_scalar(mine, bucket, iota_f[:, ds(h, 1)], 0.0, ALU.is_equal, ALU.add,
                                   accum_out=count[:, ds(h, 1)]))

            def count_three(i):
                for n in range(3):
                    count_bucket(3 * i + n)

            def bucket_starts(start):
                if start > COUNT_TURNS:
                    return
                dve.sem_inc(S["counted"], 1)
                dve.wait_ge(S["counted_mm"], 1)
                link(v.tensor_copy(offs[:, :], side[:, P:P + BLOCKS]))
                link(v.tensor_tensor_scan(out=count[:, 0:BLOCKS], data0=offs[:, :], data1=offs[:, :], initial=0.0,
                                          op0=ALU.add, op1=ALU.max))
                link(v.tensor_tensor(offs[:, :], count[:, 0:BLOCKS], offs[:, :], ALU.subtract))
                link(v.tensor_tensor(offs[:, :], offs[:, :], side[:, 0:BLOCKS], ALU.add))

            def rank_bucket(h):
                link(v.tensor_scalar(mine, bucket, iota_f[:, ds(h, 1)], None, ALU.is_equal))
                link(v.tensor_tensor_scan(out=rank, data0=mine, data1=mine, initial=offs[:, ds(h, 1)],
                                          op0=ALU.add, op1=ALU.max))
                settle(dve)
                link(v.copy_predicated(place, mine.bitcast(mybir.dt.int16), rank))

            def rank_three(i):
                for n in range(3):
                    rank_bucket(3 * i + n)

            def rank_last(i):
                for h in range(3 * ((BLOCKS - COUNT_TURNS) // 2), BLOCKS):
                    rank_bucket(h)

            side = ps[:, SIDE_BANK, :]
            walk(SAGE1, ((COUNT_TURNS, 1, count_three, 3), ((BLOCKS - COUNT_TURNS) // 2, 2, rank_three, 9),
                         (1, 1, rank_last, 3 * (BLOCKS - 3 * ((BLOCKS - COUNT_TURNS) // 2)))), bucket_starts)
            v.tensor_scalar(place_i.bitcast(i32), place, -1.0, None, ALU.add).then_inc(S["place_ready"], 1)
            link(v.tensor_copy(deg[:, :], acc[:, 0:BLOCKS, D]))
            up(v.tensor_scalar(inv[:, :], deg[:, :], 1.0, None, ALU.max))
            v.tensor_scalar(lone[:, :], deg[:, :], 1.0, None, ALU.min).then_inc(S["degrees_ready"], 1)
            dve.wait_ge(S["degrees_ready"], 1)
            link(v.reciprocal(inv[:, :], inv[:, :]))
            link(v.tensor_scalar(lone[:, :], lone[:, :], -1.0, 1.0, ALU.mult, ALU.add))
            staged(dve, feed("sage1", lambda g, half: mean(g, half, X)), lambda g, half: None)
            dve.wait_ge(S["counted_mm"], 2)
            link(v.tensor_copy(scan_b[:, :], side[:, 3 * P:3 * P + BLOCKS]))
            link(v.tensor_tensor_scan(out=rstd[:, :], data0=scan_b[:, :], data1=scan_b[:, :], initial=0.0,
                                      op0=ALU.add, op1=ALU.max))
            link(v.tensor_tensor(scan_b[:, :], rstd[:, :], scan_b[:, :], ALU.subtract))
            link(v.tensor_tensor(scan_b[:, :], scan_b[:, :], side[:, 2 * P:2 * P + BLOCKS], ALU.add))
            link(v.scalar_tensor_tensor(out=scan_b[:, :], in0=scan_b[:, :], scalar=-1.0, in1=deg[:, :],
                                        op0=ALU.add, op1=ALU.add))
            link(v.tensor_scalar(last_i[:, :], scan_b[:, :], 0.0, None, ALU.max))
            dve.wait_ge(stored["sage1"], 16 * GROUPS)
            walk(SAGE2)

            def sage2_out(g, half):
                dve.wait_ge(mixed["sage2"], g + 1)
                v.scalar_tensor_tensor(out=x_group(g), in0=mix_out(half), scalar=0.0, in1=x_group(g),
                                       op0=ALU.max, op1=ALU.add).then_inc(used["sage2"], 1)
                dve.wait_ge(used["sage2"], g + 1)
                norm_stats(lambda i: X[:, ds(g * G + i, 1), :].rearrange("p o f -> p (o f)"), G, g * G)

            sage2_feed = feed("sage2", lambda g, half: mean(g, half, Yn))

            dve.wait_ge(S["h1_loaded"], 16)
            staged(dve, sage2_feed, sage2_out, chain, 1 + 2 * G)
            norm_scale()
            norm_lots()

            walk(GIN)

            def gin_in(g, half):
                return v.scalar_tensor_tensor(out=fed_b[:, half, 0:G, :], in0=x_group(g), scalar=eps1[:, :],
                                              in1=acc[:, ds(g * G, G), 0:D], op0=ALU.mult, op1=ALU.add)

            def gin_stats(g):
                if isinstance(g, int) and g == GROUPS - 1:
                    up(v.bn_stats(stats[:, g, :], Y[:, g * W:N_NODES]))
                else:
                    up(v.bn_stats(stats[:, ds(g, 1), :].rearrange("p o t -> p (o t)"), Y[:, ds(g * W, W)]))

            def gin_out(n, layer):
                def f(g, half):
                    dve.wait_ge(mixed[n], g + 1)
                    ins = v.tensor_scalar(Y[:, ds(g * W, W)], ps[:, MIX_BANK + half, 0:W],
                                          vecs[:, 3 * layer:3 * layer + 1], None, ALU.add)
                    ins.then_inc(used[n], 1)
                    dve.wait_ge(used[n], g + (1 if n == "gin1" else 2))
                    settle(dve)
                    gin_stats(g)
                return f

            def gin_scale(layer):
                chain.done()
                link(v.bn_aggr(bn[:, layer, 0:2], stats[:, :, :].rearrange("p g t -> p (g t)")))
                v.tensor_scalar(bn[:, layer, 1:2], bn[:, layer, 1:2], BN_EPS, None, ALU.add).then_inc(S["sqrt_in"], 1)
                roots[0] += 1
                dve.wait_ge(S["sqrt_out"], roots[0])
                link(v.reciprocal(bn[:, layer, 2:3], bn[:, layer, 1:2]))
                link(v.tensor_tensor(bn[:, layer, 2:3], bn[:, layer, 2:3], vecs[:, 3 * layer + 1:3 * layer + 2], ALU.mult))
                link(v.tensor_tensor(bn[:, layer, 3:4], bn[:, layer, 0:1], bn[:, layer, 2:3], ALU.mult))
                v.tensor_tensor(bn[:, layer, 3:4], vecs[:, 3 * layer + 2:3 * layer + 3], bn[:, layer, 3:4],
                                ALU.subtract).then_inc(S["gin_ready"], 1)

            staged(dve, feed("gin1", gin_in), gin_out("gin1", 0), chain, 1)
            gin_scale(0)
            dve.sem_inc(used["gin2"], 1)
            gin_out("gin2", 1)(0, 0)
            with dve.Fori(0, (GROUPS - 1) // 2 - 1) as i:
                chain.enter(i, 2)
                for half in (1, 0):
                    gin_out("gin2", 1)(2 * i + 2 - half, half)
                chain.leave((GROUPS - 1) // 2 - 1)
            gin_out("gin2", 1)(GROUPS - 2, 1)
            gin_out("gin2", 1)(GROUPS - 1, 0)
            gin_scale(1)
            dve.sem_inc(used["gin3"], 1)

            def gin3_out(g, half):
                dve.wait_ge(mixed["gin3"], g + 1)
                v.tensor_tensor(x_group(g), x_group(g), mix_out(half), ALU.add).then_inc(used["gin3"], 1)
                dve.wait_ge(used["gin3"], g + 2)
                settle(dve)
                norm_stats(lambda i: X[:, ds(g * G + i, 1), :].rearrange("p o f -> p (o f)"), G, g * G)
            chained_groups(gin3_out, 2 * G + 1)

            dve.sem_inc(used["edge"], 1)

            def edge_own(g, half):
                dve.wait_ge(mixed["edge"], g + 1)
                v.tensor_copy(Yn[:, ds(g * G, G), :], mix_out(half, OWN_BANK)).then_inc(used["edge"], 1)
            norm_groups("edge", edge_own)

            def scan_max(c, r, lap, first=False):
                a = r % 2
                dve.wait_ge(starts_here[a], 16 * (2 * lap + r // 2 + 1))
                if not first:
                    dve.wait_ge(S["scanned"], c)
                    if not isinstance(c, int) or c >= 2:
                        dve.wait_ge(S["back_turned"], c - 1)
                dve.wait_ge(S["rows_copied"], c + 1)
                v.tensor_tensor_scan(out=maxT[:, a, :], data0=starts_b[:, a, :], data1=rowsT[:, a, :],
                                     initial=-BIG if first else maxT[:, 1 - a, J * P - 1:J * P],
                                     op0=ALU.min, op1=ALU.max).then_inc(S["scanned"], 1)

            for r in range(RING):
                scan_max(r, r, 0, first=r == 0)
            with dve.Fori(1, LAPS) as lap:
                for r in range(RING):
                    scan_max(lap * RING + r, r, lap)

            def pick(m, half):
                v.tensor_copy(pick_idx[:, half, :], last_i[:, ds(m * LOT, LOT)]).then_inc(S["pick_ready"], 1)

            def edge_out(m, half, turn):
                dve.wait_ge(picked[half], 16 * LOT * (turn + 1))
                xs = X[:, ds(m * LOT, LOT), :]
                up(v.memset(lot_c, 0.0))
                link(v.tensor_tensor(lot_ps, ring[:, half * J:half * J + LOT, 0:D], Yn[:, ds(m * LOT, LOT), :], ALU.add))
                link(v.scalar_tensor_tensor(out=lot_b, in0=lot_ps, scalar=0.0,
                                            in1=wide(lone[:, ds(m * LOT, LOT)], D),
                                            op0=ALU.mult, op1=ALU.is_equal))
                settle(dve)
                link(v.copy_predicated(lot_c, lot_b.bitcast(i32), lot_ps))
                link(v.tensor_tensor(xs, xs, lot_c, ALU.add))
                norm_stats(lambda i: X[:, ds(m * LOT + i, 1), :].rearrange("p o f -> p (o f)"), LOT, m * LOT)

            dve.wait_ge(S["back_copied"], CHUNKS)
            pick(0, 0)
            with dve.Fori(0, LOTS // 2 - 1) as i:
                chain.enter(i, 2 * (6 + 2 * LOT))
                pick(2 * i + 1, 1)
                edge_out(2 * i, 0, i)
                pick(2 * i + 2, 0)
                edge_out(2 * i + 1, 1, i)
                chain.leave(LOTS // 2 - 1)
            pick(LOTS - 1, 1)
            edge_out(LOTS - 2, 0, LOTS // 2 - 1)
            edge_out(LOTS - 1, 1, LOTS // 2 - 1)

            up(v.memset(acc_wh[:, :, D:D + 1], 1.0))
            dve.sem_inc(used["gat"], 1)

            def gat_own(g, half):
                dve.wait_ge(mixed["gat"], g + 1)
                v.tensor_copy(inv[:, ds(g * G, G)], mix_out(half, OWN_BANK)[:, :, 0]).then_inc(used["gat"], 1)
            norm_groups("gat", gat_own)

            dve.wait_ge(S["words_loaded"], 16 * 4)
            up(v.tensor_scalar(words_src, words, (1 << DST_SHIFT) - 1, None, ALU.bitwise_and))
            v.tensor_scalar(words_dst, words, DST_SHIFT, None, ALU.logical_shift_right).then_inc(S["words_ready"], 1)
            path_tables(1, (1 << DST_SHIFT) - 1, S["src_tabled"], S["src_tables_mm"])
            link(v.tensor_copy(key[:, :], words_src))

            dve.wait_ge(used["gat"], GROUPS + 1)
            up(v.memset(Y[:, NODES:ACC_BLOCKS * D], 0.0))
            dve.sem_inc(S["p_ready"], 1)
            dve.wait_ge(S["p_turned"], 1)
            v.tensor_copy(lot_a.rearrange("p b f -> p (b f)")[0:BLOCKS, 0:P], ps[0:BLOCKS, SIDE_BANK, 0:P]
                          ).then_inc(S["p_row"], 1)
            dve.wait_ge(S["p_loaded"], 16)
            dve.wait_ge(stored["gat"], 16 * GROUPS)
            walk_gat()

            pad_at = acc[:, BLOCKS - 1, D:D + 1]
            link(v.scalar_tensor_tensor(out=pad_at, in0=part_f[:, :], scalar=float(N_NODES % P), in1=pad_at,
                                        op0=ALU.is_ge, op1=ALU.add))
            link(v.reciprocal(inv[:, :], acc[:, 0:BLOCKS, D]))
            up(v.tensor_scalar(deg[:, :], inv[:, :], 0.0, None, ALU.mult))

            def gat_mean(m, half):
                v.tensor_tensor(h_lot[half], acc[:, ds(m * LOT, LOT), 0:D], wide(inv[:, ds(m * LOT, LOT)], D),
                                ALU.mult).then_inc(S["h_ready"], 1)

            def gat_out(m, half):
                xs = X[:, ds(m * LOT, LOT), :]
                dve.wait_ge(S["e_ready"], m + 1)
                link(v.scalar_tensor_tensor(out=h_lot[half], in0=h_lot[half], scalar=0.0, in1=e_lot[half],
                                            op0=ALU.max, op1=ALU.add))
                link(v.scalar_tensor_tensor(out=xs, in0=h_lot[half], scalar=-1.0, in1=xs, op0=ALU.add, op1=ALU.add))
                norm_stats(lambda i: X[:, ds(m * LOT + i, 1), :].rearrange("p o f -> p (o f)"), LOT, m * LOT)

            chain.done()
            gat_mean(0, 0)
            with dve.Fori(0, LOTS // 2 - 1) as i:
                chain.enter(i, 2 * (3 + 2 * LOT))
                for n in range(2):
                    gat_mean(2 * i + n + 1, 1 - n)
                    gat_out(2 * i + n, n)
                chain.leave(LOTS // 2 - 1)
            gat_mean(LOTS - 1, 1)
            gat_out(LOTS - 2, 0)
            gat_out(LOTS - 1, 1)
            norm_scale()
            link(v.tensor_tensor(rstd[:, :], rstd[:, :], deg[:, :], ALU.add))
            norm_lots()


def kernel(x, src, dst, L0_gnn_W1_l, L0_gnn_b1, L0_gnn_W1_r, L0_gnn_W2_l, L0_gnn_b2, L0_gnn_W2_r,
           L1_gnn_eps, L1_gnn_W1, L1_gnn_b1, L1_gnn_g1, L1_gnn_beta1, L1_gnn_W2, L1_gnn_b2, L1_gnn_g2,
           L1_gnn_beta2, L2_gnn_W, L2_gnn_b, L3_gnn_W, L3_gnn_a):
    import numpy as np
    import concourse.bacc as bacc
    from concourse.bass_utils import run_bass_kernel_spmd as run

    def flat(a):
        return np.ascontiguousarray(np.asarray(a))

    x, src, dst = flat(x), flat(src), flat(dst)
    pad = np.full(EDGES - N_EDGES, PAD_NODE, src.dtype)
    arrays = {
        "x": np.concatenate([x, np.zeros((NODES - N_NODES, D), x.dtype)]),
        "src": np.concatenate([src, pad]),
        "dst_before": np.concatenate([np.full(1, -1, dst.dtype), dst, pad]),
        "W1_l": flat(L0_gnn_W1_l), "W1_r": flat(L0_gnn_W1_r),
        "W2_l": flat(L0_gnn_W2_l), "W2_r": flat(L0_gnn_W2_r),
        "gin_W1t": flat(np.asarray(L1_gnn_W1).T), "gin_W2t": flat(np.asarray(L1_gnn_W2).T),
        "edge_Wt": flat(np.asarray(L2_gnn_W).T),
        "gat_W": flat(L3_gnn_W), "gat_Wt": flat(np.asarray(L3_gnn_W).T),
        "gat_a": flat(np.asarray(L3_gnn_a).reshape(2, D).T),
        "vecs": flat(np.stack([np.asarray(a) for a in (L1_gnn_b1, L1_gnn_g1, L1_gnn_beta1,
                                                       L1_gnn_b2, L1_gnn_g2, L1_gnn_beta2)], axis=1)),
        "biases": flat(np.stack([np.asarray(a) for a in (L0_gnn_b1, L0_gnn_b2, L2_gnn_b)])),
        "eps": flat(L1_gnn_eps),
    }
    nc = bacc.Bacc("TRN2", target_bir_lowering=False, num_devices=1)
    A = {n: nc.dram_tensor("in_" + n, a.shape, mybir.dt.from_np(a.dtype), kind="ExternalInput").ap()
         for n, a in arrays.items()}
    out = nc.dram_tensor("out", (N_NODES, D), mybir.dt.float32, kind="ExternalOutput").ap()
    gnn(nc, A, out)
    r = run(nc, [{"in_" + n: a for n, a in arrays.items()}], core_ids=[0])
    return r.results[0]["out"]
```

```python
import concourse.bass as bass
from concourse import mybir
from contextlib import ExitStack

P = 128
D = 128
N_NODES = 12500
N_EDGES = 200000
J = 8
CHUNK = P * J
CHUNKS = -(-N_EDGES // CHUNK)
EDGES = CHUNKS * CHUNK
COLS = CHUNKS * J
BLOCKS = -(-N_NODES // P)
NODES = BLOCKS * P
PAD_NODE = NODES - 1
STEPS = 3 * BLOCKS + 1
EMPTY = STEPS - (CHUNKS + BLOCKS - 1)
ACC_BLOCKS = BLOCKS + EMPTY
TURNS = CHUNKS - 1
RING = 4
LAPS = CHUNKS // RING
ROW = D + 2
G = 2
GROUPS = BLOCKS // G
W = G * P
LOT = 7
LOTS = BLOCKS // LOT
DST_SHIFT = 14
BLOCK_SHIFT = 7
BIG = 3.0e38
LN_EPS = 1e-5
BN_EPS = 1e-5
LRELU_SLOPE = 0.2

SAGE1, SAGE2, GIN, EDGE, GAT = range(5)
WALKS_BEFORE = {SAGE1: 0, SAGE2: 1, GIN: 2, GAT: 3}
SCATTER_AFTER = {SAGE1: 3, SAGE2: 13, GIN: 30, EDGE: 3}
PLAIN_TURNS = 2
COUNT_TURNS = -(-BLOCKS // 4)
RANK_TURNS = BLOCKS // 3
LAST_RANKS = BLOCKS % 3
X_PARTS = LOTS // 2
HALF = LOTS // 2
DVE_LOTS = 4
CONSTS = 15 + X_PARTS
assert PLAIN_TURNS + COUNT_TURNS + 2 * RANK_TURNS + 1 < BLOCKS and LAST_RANKS
assert CHUNKS % RING == 0 and BLOCKS % G == 0 and GROUPS % 2 == 1 and EMPTY >= 0
assert NODES <= 1 << DST_SHIFT and 1 << BLOCK_SHIFT == P


class Tally:

    def __init__(self, engine, sem):
        self.engine, self.sem, self.n, self.offset = engine, sem, 0, 0

    def up(self, instruction):
        self.n += 1
        instruction.then_inc(self.sem, 1)

    def done(self):
        self.engine.wait_ge(self.sem, self.offset + self.n)

    def link(self, instruction):
        self.up(instruction)
        self.done()

    def enter(self, i, per):
        self.at, self.per, self.offset = self.n, per, i * per

    def leave(self, times):
        assert self.n - self.at == self.per, (self.n - self.at, self.per)
        self.n = self.at + self.per * times
        self.offset = 0


def gnn(nc, A, out):
    fp32, bf16, i32 = mybir.dt.float32, mybir.dt.bfloat16, mybir.dt.int32
    ALU, ACT = mybir.AluOpType, mybir.ActivationFunctionType
    ds = bass.ds

    with ExitStack() as ctx:
        def sb(name, shape, dt=fp32):
            return ctx.enter_context(nc.sbuf_tensor(name, shape, dt))

        def sem(name):
            return ctx.enter_context(nc.semaphore(name))

        def dram(name, shape, dt=fp32):
            return nc.dram_tensor(name, shape, dt, kind="Internal").ap()

        h1_rows = dram("h1_rows", (NODES, D))
        x1_rows = dram("x1_rows", (NODES, D))
        z_rows = dram("z_rows", (NODES, D))
        wh_rows = dram("wh_rows", (NODES, ROW))
        max_rows = dram("max_rows", (EDGES, D))
        starts_dram = dram("starts_dram", (EDGES,), bf16)
        place_dram = dram("place_dram", (EDGES,), i32)
        pair_dram = dram("pair_dram", (EDGES,), i32)
        sorted_dram = dram("sorted_dram", (EDGES, 1), i32)
        col_dram = dram("col_dram", (EDGES,), i32)
        p_dram = dram("p_dram", (NODES,))

        acc = sb("acc", [P, ACC_BLOCKS, D + 1])
        X = sb("X", [P, BLOCKS, D])
        Y = sb("Y", [P, ACC_BLOCKS * D])
        key = sb("key", [P, COLS], mybir.dt.int16)
        ring = sb("ring", [P, RING * J, ROW])
        onehot = sb("onehot", [P, 3, J, P])
        work = sb("work", [P, 2, J * P])
        idx_ring = sb("idx_ring", [P, RING, J], i32)
        pair_ring = sb("pair_ring", [P, RING, J], i32)
        wts = {n: sb("w_" + n, [P, D]) for n in ("l1", "r1", "l2", "r2", "g1", "g2")}
        w_edge = sb("w_edge", [P, 2 * D])
        w_gat = sb("w_gat", [P, D + 2])
        a_cols = sb("a_cols", [P, 2])
        vecs = sb("vecs", [P, 6])
        sage_bias = sb("sage_bias", [1, 2, D])
        edge_bias = sb("edge_bias", [1, D])
        eps1 = sb("eps1", [P, 1])
        ident = sb("ident", [P, P])
        below = sb("below", [P, P])
        ones = sb("ones", [P, P])
        ones_bf = sb("ones_bf", [P, 1], bf16)
        part_i = sb("part_i", [P, 1], i32)
        iota_f = sb("iota_f", [P, STEPS])
        part_f = sb("part_f", [P, 1])
        first_node = sb("first_node", [P, ACC_BLOCKS])
        samp = sb("samp", [P, 2], i32)
        sampf = sb("sampf", [P, 2])
        srow = sb("srow", [1, CHUNKS], i32)
        chunk_at = sb("chunk_at", [1, 2, STEPS], i32)
        steps_to = sb("steps_to", [1, 2, CHUNKS], i32)
        count = sb("count", [P, 4 * COUNT_TURNS])
        offs = sb("offs", [P, BLOCKS])
        inv = sb("inv", [P, BLOCKS])
        deg = sb("deg", [P, BLOCKS])
        lone = sb("lone", [P, BLOCKS])
        last_i = sb("last_i", [P, BLOCKS], i32)
        pick_idx = sb("pick_idx", [P, 2, LOT], i32)
        mv = sb("mv", [P, BLOCKS, 2])
        rstd = sb("rstd", [P, BLOCKS])
        lmv = sb("lmv", [P, LOT, 2])
        lstat = sb("lstat", [P, LOT, 6])
        bn = sb("bn", [P, 2, 4])
        ps = ctx.enter_context(nc.psum_tensor("ps", [P, 8, 512], fp32))

        Yn = Y[:, 0:NODES].rearrange("p (b f) -> p b f", f=D)
        acc_flat = acc[:, :, :].rearrange("p b f -> p (b f)")
        acc_wh = acc_flat[:, 0:BLOCKS * ROW].rearrange("p (b r) -> p b r", r=ROW)
        iota_i = acc_flat[:, 0:STEPS].bitcast(i32)
        wts["at"] = Y[:, NODES:NODES + D]
        scan_b = mv[:, :, :].rearrange("p b t -> p (b t)")[:, 0:BLOCKS]
        hot = onehot[:, :, :, :].rearrange("p a j n -> p a (j n)")
        words = (work[:, :, :].rearrange("p a n -> p (a n)")
                 [:, 2 * J * P - COLS:2 * J * P].bitcast(i32))
        words_dst = (onehot[:, :, :, :].rearrange("p a j n -> p (a j n)")
                     [:, 3 * J * P - COLS:3 * J * P].bitcast(i32))
        work4 = work[:, :, :].rearrange("p a (q f) -> p a q f", f=P)
        fed_b = work4[:, :, 0:2 * G, :]
        turned_b = work4[:, :, 2 * G:4 * G, :]
        rowsT = hot[:, 0:2, :]
        products = work[:, 0, :].rearrange("p (j n) -> p j n", n=P)
        score = work[:, 1, 0:3 * J].rearrange("p (a j) -> p a j", j=J)
        maxT = work[:, :, :]
        starts_b = hot[:, 2, :].bitcast(bf16).rearrange("p (a n) -> p a n", a=2)
        lot_a = hot[:, 0, 0:LOT * D].rearrange("p (b f) -> p b f", f=D)
        lot_ps = ps[:, 0:2, :].rearrange("p a n -> p (a n)")[:, 0:LOT * D].rearrange("p (b f) -> p b f", f=D)
        lot_b = hot[:, 1, 0:LOT * D].rearrange("p (b f) -> p b f", f=D)
        lot_c = hot[:, 2, 0:LOT * D].rearrange("p (b f) -> p b f", f=D)
        stats = hot[:, 2, 0:GROUPS * 6].rearrange("p (g t) -> p g t", t=6)
        before = work[:, 0, 0:STEPS].bitcast(bf16).rearrange("p (a k) -> p a k", a=2)
        SORT = NODES - 4 * COLS
        spare, place, place_i, is_start = (Y[:, SORT + i * COLS:SORT + (i + 1) * COLS] for i in range(4))
        h_lot = (lot_a, lot_c)
        e_lot = (lot_b, work[:, 0, 0:LOT * D].rearrange("p (b f) -> p b f", f=D))
        bucket, mine = spare.bitcast(bf16)[:, 0:COLS], spare.bitcast(bf16)[:, COLS:2 * COLS]
        raw_dst, raw_prev, raw_src, raw_key = (Y[:, i * COLS:(i + 1) * COLS].bitcast(i32) for i in range(4))
        rank = ps[:, 3:7, :].rearrange("p a n -> p (a n)")[:, 0:COLS]
        OWN_BANK, TURN_BANK, MIX_BANK, SIDE_BANK = 0, 3, 5, 7

        def by_chunk(v):
            return v.rearrange("(c p j) -> p c j", p=P, j=J)

        def as_chunks(v):
            return v.rearrange("p (c j) -> p c j", j=J)

        S = {n: sem(n) for n in """
            samples_loaded keys_loaded src_loaded marks_loaded consts_loaded iotas ready_consts counted
            counted_mm tables_mm tabled src_tables_mm src_tabled chunks_here onehot_ready steps_done acc_done
            dve_chain act_chain pool_turn degrees_ready place_ready place_out starts_ready starts_out pair_ready
            pair_out h1_loaded first_words first_idx_ready words_loaded words_ready sorted_samples
            col_out cols_out sqrt_in sqrt_out settled normed x1_out gin_ready rows_turned rows_copied scanned
            back_turned back_copied pick_ready scores_ready weights_ready p_turned p_row p_out p_loaded wa_mm h_ready
            e_ready out_stored inverses_ready lot_out scales_ready lot_centred pool_normed
            """.split()}
        idx_here, gathered, scattered, place_here, row_stored = (
            [sem(f"{n}{r}") for r in range(RING)]
            for n in ("idx_here", "gathered", "scattered", "place_here", "row_stored"))
        picked = [sem(f"picked{a}") for a in range(2)]
        starts_here = [sem(f"starts_here{a}") for a in range(2)]
        fed, turned, copied, mixed, used, stored = (
            {n: sem(f"{w}_{n}") for n in ("sage1", "sage2", "gin1", "gin2", "gin3", "edge", "gat")}
            for w in ("fed", "turned", "copied", "mixed", "used", "stored"))

        idx_src = {q: by_chunk(A["src"]) for q in (SAGE1, SAGE2, GIN, EDGE)}
        idx_src[GAT] = by_chunk(col_dram)
        table = {SAGE1: A["x"], SAGE2: h1_rows, GIN: x1_rows, EDGE: z_rows, GAT: wh_rows}
        scatter_from = {q: sum(n for r, n in SCATTER_AFTER.items() if r < q) for q in SCATTER_AFTER}

        def settle(engine):
            engine.sem_inc(S["settled"], 1)

        def wide(t, n):
            return t.unsqueeze(2).to_broadcast([P, t.shape[1], n])

        def grouped(engine, body, first=None, last=None):
            (first or body)(0, 0)
            with engine.Fori(0, (GROUPS - 1) // 2) as i:
                for half in (1, 0):
                    body(2 * i + 2 - half, half)
            if last:
                last(GROUPS - 1, 0)

        def staged(engine, make, use, chain=None, per=0):
            make(0, 0)
            make(1, 1)
            make(2, 0)
            use(0, 0)
            with engine.Fori(0, (GROUPS - 3) // 2) as i:
                if chain:
                    chain.enter(i, 2 * per)
                for n in (3, 4):
                    make(2 * i + n, n % 2)
                    use(2 * i + n - 2, n % 2)
                if chain:
                    chain.leave((GROUPS - 3) // 2)
            use(GROUPS - 2, 1)
            use(GROUPS - 1, 0)

        block = ctx.enter_context(nc.Block())

        @block.sync
        def _(sp):
            def load(dst, src, s):
                sp.dma_start(dst, src).then_inc(S[s], 16)

            def stage_idx(q, r, c):
                sp.dma_start(idx_ring[:, r, :], idx_src[q][:, ds(c, 1), :].rearrange("p o j -> p (o j)")
                             ).then_inc(idx_here[r], 16)

            def stage_place(r, c):
                for to, frm in ((idx_ring, place_dram), (pair_ring, pair_dram)):
                    sp.dma_start(to[:, r, :], by_chunk(frm)[:, ds(c, 1), :].rearrange("p o j -> p (o j)")
                                 ).then_inc(place_here[r], 16)

            def announce(q, r, lap):
                sp.wait_ge(gathered[r], 16 * J * (q * LAPS + lap + 1))
                sp.sem_inc(S["chunks_here"], 1)

            def feed_gathers(q):
                with sp.Fori(0, LAPS - 1) as lap:
                    for r in range(RING):
                        announce(q, r, lap)
                        stage_idx(q, r, (lap + 1) * RING + r)
                for r in range(RING):
                    announce(q, r, LAPS - 1)

            def first_idx(q):
                for r in range(RING):
                    stage_idx(q, r, r)

            def feed_scatter(q):
                lap0, n = scatter_from[q], SCATTER_AFTER[q]
                for r in range(RING):
                    stage_place(r, lap0 * RING + r)
                with sp.Fori(lap0, lap0 + n - 1) as lap:
                    for r in range(RING):
                        sp.wait_ge(scattered[r], 16 * J * (lap + 1))
                        settle(sp)
                        stage_place(r, (lap + 1) * RING + r)
                for r in range(RING):
                    sp.wait_ge(scattered[r], 16 * J * (lap0 + n))

            first_idx(SAGE1)
            dst = A["dst_before"][1:EDGES + 1]
            firsts = dst.rearrange("(c e) -> c e", e=CHUNK)
            with nc.allow_non_contiguous_dma(reason="one word per chunk"):
                load(samp[:, 0:1], firsts[1:P + 1, 0:1], "samples_loaded")
                load(samp[0:TURNS - P, 1:2], firsts[P + 1:CHUNKS, 0:1], "samples_loaded")
                load(srow[0:1, 0:TURNS], firsts[1:CHUNKS, 0:1].rearrange("c o -> o c"), "samples_loaded")
            for i in range(RING):
                at = slice(i * LAPS, (i + 1) * LAPS)
                load(as_chunks(raw_key)[:, at, :], by_chunk(dst)[:, at, :], "keys_loaded")
            for n, a in (("l1", "W1_l"), ("r1", "W1_r"), ("l2", "W2_l"), ("r2", "W2_r"),
                         ("g1", "gin_W1t"), ("g2", "gin_W2t"), ("at", "gat_Wt")):
                load(wts[n][:, :], A[a], "consts_loaded")
            load(w_edge[:, D:2 * D], A["edge_Wt"][0:P, :], "consts_loaded")
            load(w_edge[:, 0:D], A["edge_Wt"][P:2 * P, :], "consts_loaded")
            load(w_gat[:, 0:D], A["gat_W"], "consts_loaded")
            load(a_cols[:, :], A["gat_a"], "consts_loaded")
            load(vecs[:, :], A["vecs"], "consts_loaded")
            load(sage_bias[:, :, :], A["biases"][0:2, :].rearrange("(o r) f -> o r f", o=1), "consts_loaded")
            load(edge_bias[:, :], A["biases"][2:3, :], "consts_loaded")
            load(eps1[:, :], A["eps"].partition_broadcast(P), "consts_loaded")
            feed_gathers(SAGE1)
            sp.wait_ge(S["pair_out"], 16)
            sp.wait_ge(S["starts_out"], 16)
            sp.wait_ge(S["place_out"], 16)
            feed_scatter(SAGE1)

            first_idx(SAGE2)
            sp.wait_ge(stored["sage1"], 16 * GROUPS)
            load(Yn[:, :, :], h1_rows.rearrange("(b p) f -> p b f", p=P), "h1_loaded")
            feed_gathers(SAGE2)
            feed_scatter(SAGE2)

            first_idx(GIN)
            feed_gathers(GIN)
            feed_scatter(GIN)

            first_idx(EDGE)
            def load_starts(a, c):
                sp.dma_start(starts_b[:, a, :], starts_dram.rearrange("(c e) -> c e", e=CHUNK)
                             [ds(c, 1), :].rearrange("o e -> (o e)").partition_broadcast(P)
                             ).then_inc(starts_here[a], 16)

            def store_max(r, c):
                sp.dma_start(max_rows.rearrange("(c p j) f -> c p j f", p=P, j=J)[ds(c, 1), :, :, :]
                             .rearrange("o p j f -> p (o j) f"),
                             ring[:, r * J:(r + 1) * J, 0:D]).then_inc(row_stored[r], 16)

            def edge_chunk(c, lap, r, first=False, refill=True):
                announce(EDGE, r, lap)
                if refill:
                    stage_idx(EDGE, r, c + RING)
                if not first or r >= 1:
                    sp.wait_ge(S["scanned"], c)
                    settle(sp)
                if refill or r < RING - 1:
                    load_starts((r + 1) % 2, c + 1)
                if not first or r >= 2:
                    sp.wait_ge(S["back_copied"], c - 1)
                    settle(sp)
                    store_max((r - 2) % RING, c - 2)

            sp.wait_ge(used["edge"], 1)
            load_starts(0, 0)
            for r in range(RING):
                edge_chunk(r, 0, r, first=True)
            with sp.Fori(1, LAPS - 1) as lap:
                for r in range(RING):
                    edge_chunk(lap * RING + r, lap, r)
            for r in range(RING):
                edge_chunk(CHUNKS - RING + r, LAPS - 1, r, refill=False)
            for c in (CHUNKS - 2, CHUNKS - 1):
                sp.wait_ge(S["back_copied"], c + 1)
                store_max(c % RING, c)

            for r in range(RING):
                sp.wait_ge(row_stored[r], 16 * LAPS)
            feed_scatter(EDGE)
            by_place = by_chunk(sorted_dram.rearrange("e o -> (e o)"))
            load(pair_ring[:, :, :], by_place[:, 0:RING, :], "first_words")
            sp.wait_ge(mixed["gat"], GROUPS)
            load(as_chunks(words), by_place, "words_loaded")
            firsts = sorted_dram.rearrange("(c e) o -> c (e o)", e=CHUNK)
            with nc.allow_non_contiguous_dma(reason="one word per chunk"):
                load(samp[:, 0:1], firsts[1:P + 1, 0:1], "sorted_samples")
                load(samp[0:TURNS - P, 1:2], firsts[P + 1:CHUNKS, 0:1], "sorted_samples")
                load(srow[0:1, 0:TURNS], firsts[1:CHUNKS, 0:1].rearrange("c o -> o c"), "sorted_samples")
            sp.wait_ge(S["words_ready"], 1)
            load(by_chunk(col_dram)[:, 0:LAPS, :], as_chunks(words_dst)[:, 0:LAPS, :], "col_out")
            load(by_chunk(col_dram)[:, LAPS:CHUNKS, :], as_chunks(words_dst)[:, LAPS:CHUNKS, :], "cols_out")
            sp.wait_ge(S["col_out"], 16)
            feed_gathers(GAT)

            full = N_NODES // P
            def store_lots(first, n, sem, before):
                with sp.Fori(0, n) as m:
                    sp.wait_ge(S[sem], m + (before + 1))
                    settle(sp)
                    sp.dma_start(out[0:(LOTS - 1) * LOT * P, :].rearrange("(m b p) f -> m p b f", b=LOT, p=P)
                                 [ds(m + first, 1), :, :, :].rearrange("o p b f -> p (o b) f"),
                                 X[:, ds(m * LOT + first * LOT, LOT), :]).then_inc(S["out_stored"], 16)
            store_lots(0, HALF, "pool_normed", 0)
            store_lots(HALF, DVE_LOTS, "normed", LOTS)
            store_lots(HALF + DVE_LOTS, HALF - DVE_LOTS - 1, "pool_normed", HALF)
            sp.wait_ge(S["pool_normed"], LOTS - DVE_LOTS)
            b0 = (LOTS - 1) * LOT
            sp.dma_start(out[b0 * P:full * P, :].rearrange("(b p) f -> p b f", p=P),
                         X[:, b0:full, :]).then_inc(S["out_stored"], 16)
            sp.dma_start(out[full * P:N_NODES, :], X[0:N_NODES - full * P, full, :]).then_inc(S["out_stored"], 16)
            sp.wait_ge(S["out_stored"], 16 * (LOTS + 1))

        @block.gpsimd
        def _(pool):
            pool.iota(iota_i[:, :], [[1, STEPS]], base=0, channel_multiplier=0).then_inc(S["iotas"], 1)
            pool.iota(part_i[:, :], [[1, 1]], base=0, channel_multiplier=1).then_inc(S["iotas"], 1)

            def gather_chunk(q, r):
                cols = ROW if q == GAT else D
                for j in range(J):
                    pool.indirect_dma_start(
                        ring[:, r * J + j, 0:cols], None, table[q],
                        bass.IndirectOffsetOnAxis(idx_ring[:, r, j:j + 1], 0)).then_inc(gathered[r], 16)

            def gathers(q):
                for r in range(RING):
                    if q != GAT:
                        pool.wait_ge(idx_here[r], 16 * (q * LAPS + 1))
                    gather_chunk(q, r)
                if q != EDGE:
                    pool.wait_ge(S["src_tabled" if q == GAT else "tabled"], 2)
                with pool.Fori(1, LAPS) as lap:
                    for r in range(RING):
                        pool.wait_ge(idx_here[r], 16 * (q * LAPS + lap + int(q != GAT)))
                        if q == EDGE:
                            pool.wait_ge(row_stored[r], 16 * lap)
                        else:
                            side = int(q == GAT)
                            n = pool.value_load(steps_to[0:1, side, ds((lap - 1) * RING + r, 1)],
                                                min_val=1, max_val=STEPS)
                            pool.wait_ge(S["steps_done"], n + WALKS_BEFORE[q] * STEPS)
                        pool.sem_inc(S["pool_turn"], 1)
                        gather_chunk(q, r)

            def scatters(q):
                with pool.Fori(scatter_from[q], scatter_from[q] + SCATTER_AFTER[q]) as lap:
                    for r in range(RING):
                        pool.wait_ge(place_here[r], 32 * (lap + 1))
                        pool.sem_inc(S["pool_turn"], 1)
                        for j in range(J):
                            pool.indirect_dma_start(
                                sorted_dram, bass.IndirectOffsetOnAxis(idx_ring[:, r, j:j + 1], 0),
                                pair_ring[:, r, j:j + 1], None).then_inc(scattered[r], 16)

            gathers(SAGE1)
            scatters(SAGE1)
            pool.wait_ge(stored["sage1"], 16 * GROUPS)
            gathers(SAGE2)
            scatters(SAGE2)
            pool.wait_ge(S["x1_out"], 16 * LOTS)
            gathers(GIN)
            scatters(GIN)
            pool.wait_ge(stored["edge"], 16 * GROUPS)
            gathers(EDGE)
            for r in range(RING):
                pool.wait_ge(row_stored[r], 16 * LAPS)
            with pool.Fori(0, LOTS // 2) as i:
                for half in range(2):
                    pool.wait_ge(S["pick_ready"], 2 * i + half + 1)
                    pool.sem_inc(S["pool_turn"], 1)
                    for b in range(LOT):
                        pool.indirect_dma_start(
                            ring[:, half * J + b, 0:D], None, max_rows,
                            bass.IndirectOffsetOnAxis(pick_idx[:, half, b:b + 1], 0)
                        ).then_inc(picked[half], 16)
            scatters(EDGE)
            pool.wait_ge(S["first_idx_ready"], 1)
            pool.wait_ge(stored["gat"], 16 * GROUPS)
            gathers(GAT)

            def gat_mean(m):
                at = slice(m * LOT, (m + 1) * LOT)
                nc.gpsimd.tensor_tensor(h_lot[m % 2], acc[:, at, 0:D], wide(inv[:, at], D), ALU.mult
                                        ).then_inc(S["h_ready"], 1)

            def norm_lot(m, n, between=None):
                at = slice(m * LOT, (m + 1) * LOT)
                nc.gpsimd.tensor_tensor(X[:, at, :], X[:, at, :], wide(mv[:, at, 0], D), ALU.subtract
                                        ).then_inc(S["lot_centred"], 1)
                if between:
                    between()
                pool.wait_ge(S["lot_centred"], n + 1)
                nc.gpsimd.tensor_tensor(X[:, at, :], X[:, at, :], wide(rstd[:, at], D), ALU.mult
                                        ).then_inc(S["pool_normed"], 1)

            def next_mean(m):
                pool.wait_ge(S["lot_out"], m - 1)
                gat_mean(m)

            pool.wait_ge(S["inverses_ready"], 1)
            gat_mean(0)
            gat_mean(1)
            for m in range(2, HALF + 2):
                next_mean(m)
            pool.wait_ge(S["scales_ready"], 1)
            for m in range(HALF + 2, LOTS):
                norm_lot(m - (HALF + 2), m - (HALF + 2), lambda: next_mean(m))
            for m in range(HALF - 2, HALF):
                norm_lot(m, m)
            pool.wait_ge(S["scales_ready"], 2)
            for m in range(HALF + DVE_LOTS, LOTS):
                norm_lot(m, m - DVE_LOTS)

        @block.tensor
        def _(pe):
            def mm(o, lhsT, rhs, start=True, stop=True):
                return nc.tensor.matmul(o, lhsT, rhs, start=start, stop=stop)

            def turn(o, a):
                return nc.tensor.transpose(o, a, ident[:, :])

            def path_sum(done):
                mm(ps[0:1, SIDE_BANK, 0:STEPS], ones_bf[:, :], before[:, 0, :], stop=False)
                mm(ps[0:1, SIDE_BANK, 0:STEPS], ones_bf[0:TURNS - P, :], before[0:TURNS - P, 1, :],
                   start=False).then_inc(done, 1)

            def walk(q, between=None):
                side = int(q == GAT)
                base = WALKS_BEFORE[q] * STEPS

                def step(k, buf):
                    c = pe.value_load(chunk_at[0:1, side, ds(k, 1)], min_val=0, max_val=CHUNKS - 1)
                    pe.wait_ge(S["chunks_here"], c + (q * CHUNKS + 1))
                    if q == GAT:
                        pe.wait_ge(S["weights_ready"], k + 1)
                    else:
                        pe.wait_ge(S["onehot_ready"], k + (base + 1))
                    for j in range(J):
                        last = mm(ps[:, buf, 0:D + 1], onehot[:, buf, j, :],
                                  ring[:, ds((c & (RING - 1)) * J + j, 1), 0:D + 1]
                                  .rearrange("p o f -> p (o f)"),
                                  start=j == 0, stop=j == J - 1)
                    last.then_inc(S["steps_done"], 1)

                step(0, 0)
                counted = PLAIN_TURNS + COUNT_TURNS
                parts = ((0, counted), (counted, BLOCKS - counted)) if between else ((0, BLOCKS),)
                for start, turns in parts:
                    if start:
                        between()
                    with pe.Fori(0, turns) as i:
                        for n in (1, 2, 3):
                            step(3 * i + (3 * start + n), n % 3)

            def dense(n, turn_of, mix_of):
                def both(g, half):
                    turn_of(g, half)
                    mix_of(g - 1, 1 - half)

                def last(g, half):
                    if n in ("sage2", "gin1"):
                        pe.wait_ge(used[n], GROUPS - 2)
                    mix_of(g, half)
                grouped(pe, both, first=turn_of, last=last)

            def bank(which, half):
                return ps[:, which + half, :]

            def turn_sage(n):
                def f(g, half):
                    pe.wait_ge(fed[n], g + 1)
                    o = bank(TURN_BANK, half)
                    for i in range(2 * G):
                        last = turn(o[:, i * P:(i + 1) * P], fed_b[:, half, i, :])
                    last.then_inc(turned[n], 1)
                return f

            def mix_sage(n, layer):
                def f(g, half):
                    pe.wait_ge(copied[n], g + 1)
                    o = bank(MIX_BANK, half)
                    for i in range(G):
                        at = o[:, i * D:(i + 1) * D]
                        mm(at, ones[0:1, :], sage_bias[0:1, layer, :], stop=False)
                        mm(at, turned_b[:, half, i, :], wts[f"l{layer + 1}"][:, :], start=False, stop=False)
                        last = mm(at, turned_b[:, half, G + i, :], wts[f"r{layer + 1}"][:, :], start=False)
                    last.then_inc(mixed[n], 1)
                return f

            def turn_nodes(n):
                def f(g, half):
                    pe.wait_ge(fed[n], g + 1)
                    for i in range(G):
                        last = turn(bank(TURN_BANK, half)[:, i * P:(i + 1) * P], fed_b[:, half, i, :])
                    last.then_inc(turned[n], 1)
                return f

            def mix_gin(n, w):
                def f(g, half):
                    pe.wait_ge(copied[n], g + 1)
                    mm(bank(MIX_BANK, half)[:, 0:W], w[:, :],
                       turned_b[:, half, 0:G, :].rearrange("p i n -> p (i n)")).then_inc(mixed[n], 1)
                return f

            def mix_edge(g, half):
                pe.wait_ge(copied["edge"], g + 1)
                pe.wait_ge(used["edge"], g + 1)
                for i in range(G):
                    mm(bank(MIX_BANK, half)[:, i * W:i * W + D], turned_b[:, half, i, :], w_edge[:, 0:D])
                for i in range(G):
                    at = bank(OWN_BANK, half)[:, i * D:(i + 1) * D]
                    mm(at, ones[0:1, :], edge_bias[:, :], stop=False)
                    last = mm(at, turned_b[:, half, i, :], w_edge[:, D:2 * D], start=False)
                last.then_inc(mixed["edge"], 1)

            pe.wait_ge(S["ready_consts"], 1)
            pe.wait_ge(S["tabled"], 1)
            path_sum(S["tables_mm"])
            pe.wait_ge(S["tabled"], 2)

            def sum_counts():
                pe.wait_ge(S["consts_loaded"], 16 * CONSTS)
                mm(ps[:, SIDE_BANK - 1, 0:2], wts["at"][:, :], a_cols[:, :]).then_inc(S["wa_mm"], 1)
                pe.wait_ge(S["counted"], 1)
                mm(ps[:, SIDE_BANK, 0:BLOCKS], below[:, :], count[:, 0:BLOCKS])
                mm(ps[:, SIDE_BANK, P:P + BLOCKS], ones[:, :], count[:, 0:BLOCKS]).then_inc(S["counted_mm"], 1)
            walk(SAGE1, sum_counts)

            pe.wait_ge(S["degrees_ready"], 1)
            mm(ps[:, SIDE_BANK, 2 * P:2 * P + BLOCKS], below[:, :], deg[:, :])
            mm(ps[:, SIDE_BANK, 3 * P:3 * P + BLOCKS], ones[:, :], deg[:, :]).then_inc(S["counted_mm"], 1)
            dense("sage1", turn_sage("sage1"), mix_sage("sage1", 0))
            walk(SAGE2)
            dense("sage2", turn_sage("sage2"), mix_sage("sage2", 1))
            walk(GIN)
            dense("gin1", turn_nodes("gin1"), mix_gin("gin1", wts["g1"]))
            grouped(pe, mix_gin("gin2", wts["g2"]))

            def turn_back(g, half):
                pe.wait_ge(copied["gin3"], g + 1)
                for i in range(G):
                    last = turn(bank(MIX_BANK, half)[:, i * P:(i + 1) * P], turned_b[:, half, i, :])
                last.then_inc(mixed["gin3"], 1)
            grouped(pe, turn_back)
            dense("edge", turn_nodes("edge"), mix_edge)

            def rows_turn(c, r):
                pe.wait_ge(S["chunks_here"], c + (EDGE * CHUNKS + 1))
                for j in range(J):
                    last = turn(ps[:, 2 * (r % 2) + j // 4, (j % 4) * P:(j % 4 + 1) * P],
                                ring[:, r * J + j, 0:D])
                last.then_inc(S["rows_turned"], 1)

            def back_turn(c, r):
                pe.wait_ge(S["scanned"], c + 1)
                for j in range(J):
                    last = turn(ps[:, 4 + 2 * (r % 2) + j // 4, (j % 4) * P:(j % 4 + 1) * P],
                                maxT[:, r % 2, :].rearrange("f (p j) -> f j p", j=J)[:, j, :])
                last.then_inc(S["back_turned"], 1)

            def mix_gat(g, half):
                pe.wait_ge(copied["gat"], g + 1)
                for i in range(G):
                    last = mm(bank(MIX_BANK, half)[:, i * W:i * W + D + 2], turned_b[:, half, i, :], w_gat[:, :])
                last.then_inc(mixed["gat"], 1)

            pe.wait_ge(used["edge"], GROUPS + 1)
            rows_turn(0, 0)
            for r in range(1, RING):
                rows_turn(r, r)
                back_turn(r - 1, r - 1)
            with pe.Fori(1, LAPS) as lap:
                for r in range(RING):
                    rows_turn(lap * RING + r, r)
                    back_turn(lap * RING + r - 1, (r - 1) % RING)
            back_turn(CHUNKS - 1, RING - 1)

            dense("gat", turn_nodes("gat"), mix_gat)
            pe.wait_ge(used["gat"], GROUPS)
            turn(ps[0:BLOCKS, SIDE_BANK - 1, 0:P], inv[:, :]).then_inc(S["p_turned"], 1)
            pe.wait_ge(S["src_tabled"], 1)
            path_sum(S["src_tables_mm"])
            pe.wait_ge(S["src_tabled"], 2)
            walk(GAT)

        @block.scalar
        def _(act):
            chain = Tally(act, S["act_chain"])
            roots = [0]

            def root(what=None):
                roots[0] += 1
                act.wait_ge(S["sqrt_in"], roots[0])
                if what is None:
                    what = bn[:, 0, 1:2] if roots[0] == 2 else bn[:, 1, 1:2] if roots[0] == 3 else rstd[:, :]
                nc.scalar.activation(what, what, ACT.Sqrt).then_inc(S["sqrt_out"], 1)

            def copy_turned(n, width):
                def f(g, half):
                    act.wait_ge(turned[n], g + 1)
                    nc.scalar.copy(turned_b[:, half, 0:width, :].rearrange("p q n -> p (q n)"),
                                   ps[:, TURN_BANK + half, 0:width * P]).then_inc(copied[n], 1)
                return f

            def dense(first, use):
                def both(g, half):
                    first(g, half)
                    use(g - 1, 1 - half)
                grouped(act, both, first=first, last=use)

            def store_group(n, rows, src, cols):
                act.dma_start(rows.rearrange("(g b p) f -> g p b f", p=P, b=G)[ds(cols, 1), :, :, :]
                              .rearrange("o p b f -> p (o b) f"), src).then_inc(stored[n], 16)

            def use_sage1(g, half):
                act.wait_ge(mixed["sage1"], g + 1)
                to = acc[:, ds(g * G, G), 0:D]
                nc.scalar.activation(to, ps[:, MIX_BANK + half, 0:W].rearrange("p (i f) -> p i f", i=G),
                                     ACT.Relu).then_inc(used["sage1"], 1)
                act.wait_ge(used["sage1"], g + 1)
                store_group("sage1", h1_rows, to, g)

            assert 3 + 2 * X_PARTS < 3 * PLAIN_TURNS + 3 * COUNT_TURNS

            def bring(to, frm, s, chunks=0, steps=0):
                if steps:
                    act.wait_ge(S["steps_done"], steps)
                else:
                    assert chunks <= RING
                    act.wait_ge(S["chunks_here"], chunks)
                act.dma_start(to, frm).then_inc(S[s], 16)

            for i in range(RING):
                at = slice(i * LAPS, (i + 1) * LAPS)
                bring(as_chunks(raw_src)[:, at, :], by_chunk(A["src"])[:, at, :], "src_loaded", 1)
            def send(to, frm, ready, sent):
                act.wait_ge(S[ready], 1)
                act.dma_start(to, frm).then_inc(S[sent], 16)
            send(by_chunk(pair_dram), as_chunks(raw_key), "pair_ready", "pair_out")
            bring(raw_dst, A["dst_before"][1:EDGES + 1].rearrange("(p t) -> p t", p=P), "marks_loaded", RING)
            bring(raw_prev, A["dst_before"][0:EDGES].rearrange("(p t) -> p t", p=P), "marks_loaded", RING)
            for i in range(X_PARTS):
                at = slice(i * 2 * LOT, (i + 1) * 2 * LOT)
                bring(X[:, at, :], A["x"].rearrange("(b p) f -> p b f", p=P)[:, at, :], "consts_loaded",
                      steps=3 + 2 * i)
            send(starts_dram.rearrange("(p t) -> p t", p=P),
                 Y[:, COLS:COLS + COLS // 2].bitcast(bf16), "starts_ready", "starts_out")
            send(by_chunk(place_dram), as_chunks(place_i.bitcast(i32)), "place_ready", "place_out")

            dense(copy_turned("sage1", 2 * G), use_sage1)
            grouped(act, copy_turned("sage2", 2 * G))
            root()
            with act.Fori(0, LOTS) as m:
                act.wait_ge(S["normed"], m + 1)
                act.dma_start(x1_rows.rearrange("(m b p) f -> m p b f", b=LOT, p=P)[ds(m, 1), :, :, :]
                              .rearrange("o p b f -> p (o b) f"),
                              X[:, ds(m * LOT, LOT), :]).then_inc(S["x1_out"], 16)
            grouped(act, copy_turned("gin1", G))
            root()

            def normed_relu(n, layer):
                def f(g, half):
                    act.wait_ge(used[n], g + 1)
                    nc.scalar.activation(turned_b[:, half, 0:G, :].rearrange("p q n -> p (q n)"),
                                         Y[:, ds(g * W, W)], ACT.Relu, bias=bn[:, layer, 3:4],
                                         scale=bn[:, layer, 2:3]).then_inc(copied[n], 1)
                return f

            act.wait_ge(S["gin_ready"], 1)
            grouped(act, normed_relu("gin2", 0))
            root()
            act.wait_ge(S["gin_ready"], 2)
            grouped(act, normed_relu("gin3", 1))
            root()

            def use_edge(g, half):
                act.wait_ge(mixed["edge"], g + 1)
                to = acc[:, ds(g * G, G), 0:D]
                frm = ps[:, MIX_BANK + half, :].rearrange("p (i f) -> p i f", i=G)
                chain.link(nc.scalar.copy(to, frm[:, :, 0:D]))
                store_group("edge", z_rows, to, g)

            def looped_dense(first, use, per):
                first(0, 0)
                with act.Fori(0, (GROUPS - 1) // 2) as i:
                    chain.enter(i, 2 * per)
                    for half in (1, 0):
                        first(2 * i + 2 - half, half)
                        use(2 * i + 1 - half, 1 - half)
                    chain.leave((GROUPS - 1) // 2)
                use(GROUPS - 1, 0)

            looped_dense(copy_turned("edge", G), use_edge, 1)

            def rows_copy(c, r):
                act.wait_ge(S["rows_turned"], c + 1)
                nc.scalar.copy(rowsT[:, r % 2, :].rearrange("f (p j) -> f j p", j=J),
                               ps[:, 2 * (r % 2):2 * (r % 2) + 2, :].rearrange("f a (j p) -> f (a j) p", p=P)
                               ).then_inc(S["rows_copied"], 1)

            def back_copy(c, r):
                act.wait_ge(S["back_turned"], c + 1)
                a = 4 + 2 * (r % 2)
                nc.scalar.copy(ring[:, r * J:(r + 1) * J, 0:D],
                               ps[:, a:a + 2, :].rearrange("p a (j f) -> p (a j) f", f=D)
                               ).then_inc(S["back_copied"], 1)

            rows_copy(0, 0)
            for r in range(1, RING):
                rows_copy(r, r)
                back_copy(r - 1, r - 1)
            with act.Fori(1, LAPS) as lap:
                for r in range(RING):
                    rows_copy(lap * RING + r, r)
                    back_copy(lap * RING + r - 1, (r - 1) % RING)
            back_copy(CHUNKS - 1, RING - 1)
            root()

            def use_gat(g, half):
                act.wait_ge(mixed["gat"], g + 1)
                frm = ps[:, MIX_BANK + half, :].rearrange("p (i f) -> p i f", i=G)
                nc.scalar.copy(inv[:, ds(g * G, G)], frm[:, :, D]).then_inc(used["gat"], 1)
                chain.up(nc.scalar.copy(acc_wh[:, ds(g * G, G), 0:D], frm[:, :, 0:D]))
                chain.link(nc.scalar.copy(acc_wh[:, ds(g * G, G), D + 1:D + 2], frm[:, :, D + 1:D + 2]))
                store_group("gat", wh_rows, acc_wh[:, ds(g * G, G), :], g)

            looped_dense(copy_turned("gat", G), use_gat, 2)
            act.wait_ge(S["p_row"], 1)
            act.dma_start(p_dram.rearrange("(b p) -> b p", p=P), lot_a.rearrange("p b f -> p (b f)")[0:BLOCKS, 0:P]
                          ).then_inc(S["p_out"], 16)
            act.wait_ge(S["p_out"], 16)
            act.dma_start(Y[:, 0:NODES], p_dram.partition_broadcast(P)).then_inc(S["p_loaded"], 16)

            def weigh(k, n):
                act.wait_ge(S["scores_ready"], k + 1)
                chain.link(nc.scalar.activation(score[:, n % 3, :], score[:, n % 3, :], ACT.Exp, scale=-1.0))
                for j in range(J):
                    at = onehot[:, n % 3, j, :]
                    last = nc.scalar.mul(at, at, score[:, n % 3, j:j + 1])
                last.then_inc(S["weights_ready"], 1)
            weigh(0, 0)
            with act.Fori(0, BLOCKS // 2) as i:
                chain.enter(i, 6)
                for n in range(1, 7):
                    weigh(6 * i + n, n)
                chain.leave(BLOCKS // 2)
            def exp_lot(m, n):
                act.wait_ge(S["h_ready"], m + 1)
                chain.link(nc.scalar.activation(e_lot[n], h_lot[n], ACT.Relu, scale=-1.0))
                nc.scalar.activation(e_lot[n], e_lot[n], ACT.Exp, scale=-1.0).then_inc(S["e_ready"], 1)

            for half in range(2):
                at = half * HALF
                with act.Fori(0, HALF // 2) as i:
                    chain.enter(i, 2)
                    for n in range(2):
                        exp_lot(2 * i + (at + n), (at + n) % 2)
                    chain.leave(HALF // 2)
                exp_lot(at + HALF - 1, (at + HALF - 1) % 2)
                root(rstd[:, at * LOT:(at + HALF) * LOT])

        @block.vector
        def _(dve):
            v = nc.vector
            chain = Tally(dve, S["dve_chain"])
            up, link = chain.up, chain.link
            roots = [0]

            def path_tables(side, mask, tabled, mm_done):
                for a, n in ((0, P), (1, TURNS - P)):
                    if mask:
                        up(v.tensor_scalar(samp[0:n, a:a + 1], samp[0:n, a:a + 1], mask, BLOCK_SHIFT,
                                           ALU.bitwise_and, ALU.logical_shift_right))
                    else:
                        up(v.tensor_scalar(samp[0:n, a:a + 1], samp[0:n, a:a + 1], BLOCK_SHIFT, None,
                                           ALU.logical_shift_right))
                if mask:
                    link(v.tensor_scalar(srow[:, 0:TURNS], srow[:, 0:TURNS], mask, BLOCK_SHIFT,
                                         ALU.bitwise_and, ALU.logical_shift_right))
                else:
                    link(v.tensor_scalar(srow[:, 0:TURNS], srow[:, 0:TURNS], BLOCK_SHIFT, None,
                                         ALU.logical_shift_right))
                up(v.scalar_tensor_tensor(out=sampf[:, 0:1], in0=samp[:, 0:1], scalar=0.0, in1=part_f[:, :],
                                          op0=ALU.add, op1=ALU.add))
                up(v.scalar_tensor_tensor(out=sampf[0:TURNS - P, 1:2], in0=samp[0:TURNS - P, 1:2],
                                          scalar=float(P), in1=part_f[0:TURNS - P, :], op0=ALU.add, op1=ALU.add))
                link(v.scalar_tensor_tensor(out=steps_to[:, side, 0:TURNS], in0=srow[:, 0:TURNS], scalar=1.0,
                                            in1=iota_f[0:1, 0:TURNS], op0=ALU.add, op1=ALU.add))
                up(v.tensor_scalar(before[:, 0, :], iota_f[:, :], sampf[:, 0:1], None, ALU.is_gt))
                v.tensor_scalar(before[0:TURNS - P, 1, :], iota_f[0:TURNS - P, :], sampf[0:TURNS - P, 1:2],
                                None, ALU.is_gt).then_inc(tabled, 1)
                dve.wait_ge(mm_done, 1)
                v.tensor_copy(chunk_at[:, side, :], ps[0:1, SIDE_BANK, 0:STEPS]).then_inc(tabled, 1)
                dve.wait_ge(tabled, 2)

            def chunk_of(side, k):
                return dve.value_load(chunk_at[0:1, side, ds(k, 1)], min_val=0, max_val=CHUNKS - 1)

            def block_of(k, c):
                return (k - c).with_bounds(min_val=0, max_val=ACC_BLOCKS - 1)

            def one_hot(side, k, buf, c=None):
                c = chunk_of(side, k) if c is None else c
                return c, v.scalar_tensor_tensor(
                    out=onehot[:, buf, :, :], in0=wide(key[:, ds(c * J, J)], P),
                    scalar=first_node[:, ds(block_of(k, c), 1)],
                    in1=iota_f[:, 0:P].unsqueeze(1).to_broadcast([P, J, P]), op0=ALU.subtract, op1=ALU.is_equal)

            def add_step(q, k, buf, c=None):
                base = WALKS_BEFORE[q] * STEPS
                c = chunk_of(int(q == GAT), k) if c is None else c
                to = acc[:, ds(block_of(k, c), 1), :].rearrange("p o f -> p (o f)")
                dve.wait_ge(S["acc_done"], k + (base + WALKS_BEFORE[q] + 1))
                dve.wait_ge(S["steps_done"], k + (base + 1))
                v.tensor_tensor(to, to, ps[:, buf, 0:D + 1], ALU.add).then_inc(S["acc_done"], 1)

            def clear_acc():
                v.memset(acc[:, :, :], 0.0).then_inc(S["acc_done"], 1)

            def walk(q, parts=((BLOCKS, 1, None, 0, None),)):
                if q != SAGE1:
                    clear_acc()
                _, ins = one_hot(0, 0, 0)
                ins.then_inc(S["onehot_ready"], 1)
                start = 0
                for turns, triples, hook, per, after in parts:
                    with dve.Fori(0, turns) as i:
                        chain.enter(i, per)
                        c = chunk_of(0, 3 * triples * i + 3 * start)
                        for n in range(1, 3 * triples + 1):
                            k = 3 * triples * i + (3 * start + n)
                            c_next, ins = one_hot(0, k, n % 3)
                            ins.then_inc(S["onehot_ready"], 1)
                            add_step(q, k - 1, (n - 1) % 3, c)
                            c = c_next
                        if hook:
                            hook(i)
                        chain.leave(turns)
                    start += turns * triples
                    if after:
                        after()
                assert start == BLOCKS
                add_step(q, STEPS - 1, (STEPS - 1) % 3)
                dve.wait_ge(S["acc_done"], (WALKS_BEFORE[q] + 1) * (STEPS + 1))

            def walk_gat():
                def step(k, n, c, c_next_at, c_before=None):
                    buf = n % 3
                    _, ins = one_hot(1, k, buf, c)
                    up(ins)
                    b = block_of(k, c) if not isinstance(k, int) or k else 0
                    c_next = c_next_at and chunk_of(1, k + 1)
                    chain.done()
                    up(v.tensor_tensor(products, onehot[:, buf, :, :],
                                       Y[:, ds(b * P, P)].unsqueeze(1).to_broadcast([P, J, P]), ALU.mult))
                    if c_before is not None:
                        add_step(GAT, k - 2, (n - 2) % 3, c_before)
                    chain.done()
                    link(v.tensor_reduce(score[:, buf, :], products, mybir.AxisListType.X, ALU.add))
                    dve.wait_ge(S["chunks_here"], c + (GAT * CHUNKS + 1))
                    link(v.tensor_tensor(score[:, buf, :], score[:, buf, :],
                                         ring[:, ds((c & (RING - 1)) * J, J), D + 1], ALU.add))
                    v.scalar_tensor_tensor(out=score[:, buf, :], in0=score[:, buf, :], scalar=LRELU_SLOPE,
                                           in1=score[:, buf, :], op0=ALU.mult, op1=ALU.max
                                           ).then_inc(S["scores_ready"], 1)
                    return c_next

                def run(ks, offset):
                    cs = {ks[0] - 2: chunk_of(1, offset + ks[0] - 2), ks[0] - 1: chunk_of(1, offset + ks[0] - 1),
                          ks[0]: chunk_of(1, offset + ks[0])}
                    for k in ks:
                        cs[k + 1] = step(offset + k, k, cs[k], k != ks[-1], cs[k - 2])

                dve.wait_ge(S["p_loaded"], 16)
                c = step(0, 0, chunk_of(1, 0), True)
                dve.wait_ge(S["cols_out"], 16)
                step(1, 1, c, False)
                with dve.Fori(0, (STEPS - 7) // 6) as i:
                    chain.enter(i, 6 * 4)
                    run(range(2, 8), 6 * i)
                    chain.leave((STEPS - 7) // 6)
                run(range(6 * ((STEPS - 7) // 6) + 2, STEPS), 0)
                add_step(GAT, STEPS - 2, (STEPS - 2) % 3)
                add_step(GAT, STEPS - 1, (STEPS - 1) % 3)
                dve.wait_ge(S["acc_done"], 4 * (STEPS + 1))

            def norm_stats(at, n, first_block):
                settle(dve)
                for i in range(n):
                    up(v.bn_stats(lstat[:, i, :], at(i)))
                chain.done()
                settle(dve)
                for i in range(n):
                    up(v.bn_aggr(lmv[:, i, :], lstat[:, i, :]))
                chain.done()
                up(v.tensor_copy(mv[:, ds(first_block, n), :], lmv[:, 0:n, :]))

            def norm_scale(at=slice(0, BLOCKS)):
                chain.done()
                v.tensor_scalar(rstd[:, at], mv[:, at, 1], LN_EPS, None, ALU.add).then_inc(S["sqrt_in"], 1)
                roots[0] += 1
                dve.wait_ge(S["sqrt_out"], roots[0])
                link(v.reciprocal(rstd[:, at], rstd[:, at]))

            def norm_block(b, to=None):
                at = X[:, ds(b, 1), :].rearrange("p o f -> p (o f)")
                return v.tensor_scalar(at if to is None else to, at, mv[:, ds(b, 1), 0:1].rearrange("p o t -> p (o t)"),
                                       rstd[:, ds(b, 1)], ALU.subtract, ALU.mult)

            def norm_lots(first=0, n=LOTS):
                def less_mean(m):
                    at = ds(m * LOT + first * LOT, LOT)
                    up(v.tensor_tensor(X[:, at, :], X[:, at, :], wide(mv[:, at, 0], D), ALU.subtract))

                def scaled(m):
                    at = ds(m * LOT + first * LOT, LOT)
                    v.tensor_tensor(X[:, at, :], X[:, at, :], wide(rstd[:, at], D), ALU.mult).then_inc(S["normed"], 1)

                less_mean(0)
                with dve.Fori(1, n) as m:
                    chain.enter(m - 1, 1)
                    chain.done()
                    less_mean(m)
                    scaled(m - 1)
                    chain.leave(n - 1)
                chain.done()
                scaled(n - 1)

            def norm_groups(n, out_of):
                norm_scale()

                def make(g, half):
                    for i in range(G):
                        last = norm_block(g * G + i, fed_b[:, half, i, :])
                    return last

                def norm(g, half):
                    feed(n, make)(g, half)
                    for i in range(G):
                        norm_block(g * G + i)

                staged(dve, norm, out_of)

            def chained_groups(body, per):
                body(0, 0)
                with dve.Fori(0, (GROUPS - 1) // 2) as i:
                    chain.enter(i, 2 * per)
                    for half in (1, 0):
                        body(2 * i + 2 - half, half)
                    chain.leave((GROUPS - 1) // 2)

            def feed(n, make):
                def f(g, half):
                    if not isinstance(g, int) or g > 1:
                        dve.wait_ge(turned[n], g - 1)
                    make(g, half).then_inc(fed[n], 1)
                return f

            def mean(g, half, other):
                v.tensor_copy(fed_b[:, half, G:2 * G, :], other[:, ds(g * G, G), :])
                return v.tensor_tensor(fed_b[:, half, 0:G, :], acc[:, ds(g * G, G), 0:D],
                                       wide(inv[:, ds(g * G, G)], D), ALU.mult)

            def x_group(g):
                return X[:, ds(g * G, G), :]

            def mix_out(half, which=MIX_BANK):
                return ps[:, which + half, 0:W].rearrange("p (i f) -> p i f", i=G)

            dve.wait_ge(S["iotas"], 2)
            up(v.tensor_copy(iota_f[:, :], iota_i[:, :]))
            up(v.tensor_copy(part_f[:, :], part_i[:, :]))
            up(v.memset(ones[:, :], 1.0))
            up(v.memset(ones_bf[:, :], 1.0))
            up(v.memset(ring[:, :, D:ROW], 1.0))
            chain.done()
            up(v.tensor_scalar(first_node[:, :], iota_f[:, 0:ACC_BLOCKS], float(P), None, ALU.mult))
            up(v.tensor_scalar(below[:, :], iota_f[:, 0:P], part_f[:, :], None, ALU.is_gt))
            up(v.tensor_scalar(ident[:, :], iota_f[:, 0:P], part_f[:, :], None, ALU.is_equal))
            chain.done()
            clear_acc()
            dve.sem_inc(S["ready_consts"], 1)
            dve.wait_ge(S["samples_loaded"], 16 * 3)
            path_tables(0, 0, S["tabled"], S["tables_mm"])
            dve.wait_ge(S["keys_loaded"], 16 * RING)
            link(v.tensor_copy(key[:, :], raw_key))

            def count_bucket(h):
                link(v.tensor_scalar(mine, bucket, iota_f[:, ds(h, 1)], 0.0, ALU.is_equal, ALU.add,
                                   accum_out=count[:, ds(h, 1)]))

            def count_four(i):
                for n in range(4):
                    count_bucket(4 * i + n)

            def words_and_buckets():
                dve.wait_ge(S["src_loaded"], 16 * RING)
                up(v.tensor_scalar(place_i.bitcast(i32), raw_src, BLOCK_SHIFT, None, ALU.logical_shift_right))
                link(v.tensor_scalar(raw_key, raw_key, DST_SHIFT, None, ALU.logical_shift_left))
                up(v.tensor_copy(bucket, place_i.bitcast(i32)))
                v.tensor_tensor(raw_key, raw_key, raw_src, ALU.bitwise_or).then_inc(S["pair_ready"], 1)
                link(v.memset(place, 0.0))

            def other_constants():
                dve.wait_ge(S["marks_loaded"], 16 * 2)
                dve.wait_ge(S["pair_out"], 16)
                link(v.tensor_tensor(is_start, raw_dst, raw_prev, ALU.is_equal))
                link(v.tensor_scalar(is_start, is_start, 2.0, -1.0, ALU.mult, ALU.add))
                v.tensor_scalar(Y[:, COLS:COLS + COLS // 2].bitcast(bf16), is_start, BIG, None, ALU.mult
                                ).then_inc(S["starts_ready"], 1)
                dve.wait_ge(S["consts_loaded"], 16 * CONSTS)
                up(v.tensor_tensor(w_edge[:, D:2 * D], w_edge[:, D:2 * D], w_edge[:, 0:D], ALU.subtract))
                up(v.tensor_scalar(eps1[:, :], eps1[:, :], 1.0, None, ALU.add))
                dve.wait_ge(S["wa_mm"], 1)
                link(v.tensor_copy(w_gat[:, D:D + 2], ps[:, SIDE_BANK - 1, 0:2]))

            def bucket_starts():
                other_constants()
                dve.sem_inc(S["counted"], 1)
                dve.wait_ge(S["counted_mm"], 1)
                link(v.tensor_copy(offs[:, :], side[:, P:P + BLOCKS]))
                link(v.tensor_tensor_scan(out=count[:, 0:BLOCKS], data0=offs[:, :], data1=offs[:, :], initial=0.0,
                                          op0=ALU.add, op1=ALU.max))
                link(v.tensor_tensor(offs[:, :], count[:, 0:BLOCKS], offs[:, :], ALU.subtract))
                link(v.tensor_tensor(offs[:, :], offs[:, :], side[:, 0:BLOCKS], ALU.add))

            def rank_bucket(h):
                link(v.tensor_scalar(mine, bucket, iota_f[:, ds(h, 1)], None, ALU.is_equal))
                link(v.tensor_tensor_scan(out=rank, data0=mine, data1=mine, initial=offs[:, ds(h, 1)],
                                          op0=ALU.add, op1=ALU.max))
                settle(dve)
                link(v.copy_predicated(place, mine.bitcast(mybir.dt.int16), rank))

            def rank_three(i):
                for n in range(3):
                    rank_bucket(3 * i + n)

            def rank_last(i):
                for h in range(BLOCKS - LAST_RANKS, BLOCKS):
                    rank_bucket(h)

            def places():
                v.tensor_scalar(place_i.bitcast(i32), place, -1.0, None, ALU.add).then_inc(S["place_ready"], 1)

            side = ps[:, SIDE_BANK, :]
            rest = BLOCKS - (PLAIN_TURNS + COUNT_TURNS + 2 * RANK_TURNS + 1)
            walk(SAGE1, ((PLAIN_TURNS, 1, None, 0, words_and_buckets), (COUNT_TURNS, 1, count_four, 4, bucket_starts),
                         (RANK_TURNS, 2, rank_three, 9, None), (1, 1, rank_last, 3 * LAST_RANKS, places),
                         (rest, 1, None, 0, None)))
            link(v.tensor_copy(deg[:, :], acc[:, 0:BLOCKS, D]))
            up(v.tensor_scalar(inv[:, :], deg[:, :], 1.0, None, ALU.max))
            v.tensor_scalar(lone[:, :], deg[:, :], 1.0, None, ALU.min).then_inc(S["degrees_ready"], 1)
            dve.wait_ge(S["degrees_ready"], 1)
            link(v.reciprocal(inv[:, :], inv[:, :]))
            link(v.tensor_scalar(lone[:, :], lone[:, :], -1.0, 1.0, ALU.mult, ALU.add))
            staged(dve, feed("sage1", lambda g, half: mean(g, half, X)), lambda g, half: None)
            dve.wait_ge(S["counted_mm"], 2)
            link(v.tensor_copy(scan_b[:, :], side[:, 3 * P:3 * P + BLOCKS]))
            link(v.tensor_tensor_scan(out=rstd[:, :], data0=scan_b[:, :], data1=scan_b[:, :], initial=0.0,
                                      op0=ALU.add, op1=ALU.max))
            link(v.tensor_tensor(scan_b[:, :], rstd[:, :], scan_b[:, :], ALU.subtract))
            link(v.tensor_tensor(scan_b[:, :], scan_b[:, :], side[:, 2 * P:2 * P + BLOCKS], ALU.add))
            link(v.scalar_tensor_tensor(out=scan_b[:, :], in0=scan_b[:, :], scalar=-1.0, in1=deg[:, :],
                                        op0=ALU.add, op1=ALU.add))
            link(v.tensor_scalar(last_i[:, :], scan_b[:, :], 0.0, None, ALU.max))
            dve.wait_ge(stored["sage1"], 16 * GROUPS)
            walk(SAGE2)

            def sage2_out(g, half):
                dve.wait_ge(mixed["sage2"], g + 1)
                v.scalar_tensor_tensor(out=x_group(g), in0=mix_out(half), scalar=0.0, in1=x_group(g),
                                       op0=ALU.max, op1=ALU.add).then_inc(used["sage2"], 1)
                dve.wait_ge(used["sage2"], g + 1)
                norm_stats(lambda i: X[:, ds(g * G + i, 1), :].rearrange("p o f -> p (o f)"), G, g * G)

            sage2_feed = feed("sage2", lambda g, half: mean(g, half, Yn))

            dve.wait_ge(S["h1_loaded"], 16)
            staged(dve, sage2_feed, sage2_out, chain, 1 + 2 * G)
            norm_scale()
            norm_lots()

            walk(GIN)

            def gin_in(g, half):
                return v.scalar_tensor_tensor(out=fed_b[:, half, 0:G, :], in0=x_group(g), scalar=eps1[:, :],
                                              in1=acc[:, ds(g * G, G), 0:D], op0=ALU.mult, op1=ALU.add)

            def gin_stats(g):
                if isinstance(g, int) and g == GROUPS - 1:
                    up(v.bn_stats(stats[:, g, :], Y[:, g * W:N_NODES]))
                else:
                    up(v.bn_stats(stats[:, ds(g, 1), :].rearrange("p o t -> p (o t)"), Y[:, ds(g * W, W)]))

            def gin_out(n, layer):
                def f(g, half):
                    dve.wait_ge(mixed[n], g + 1)
                    ins = v.tensor_scalar(Y[:, ds(g * W, W)], ps[:, MIX_BANK + half, 0:W],
                                          vecs[:, 3 * layer:3 * layer + 1], None, ALU.add)
                    ins.then_inc(used[n], 1)
                    dve.wait_ge(used[n], g + (1 if n == "gin1" else 2))
                    settle(dve)
                    gin_stats(g)
                return f

            def gin_scale(layer):
                chain.done()
                link(v.bn_aggr(bn[:, layer, 0:2], stats[:, :, :].rearrange("p g t -> p (g t)")))
                v.tensor_scalar(bn[:, layer, 1:2], bn[:, layer, 1:2], BN_EPS, None, ALU.add).then_inc(S["sqrt_in"], 1)
                roots[0] += 1
                dve.wait_ge(S["sqrt_out"], roots[0])
                link(v.reciprocal(bn[:, layer, 2:3], bn[:, layer, 1:2]))
                link(v.tensor_tensor(bn[:, layer, 2:3], bn[:, layer, 2:3], vecs[:, 3 * layer + 1:3 * layer + 2],
                                     ALU.mult))
                link(v.tensor_tensor(bn[:, layer, 3:4], bn[:, layer, 0:1], bn[:, layer, 2:3], ALU.mult))
                v.tensor_tensor(bn[:, layer, 3:4], vecs[:, 3 * layer + 2:3 * layer + 3], bn[:, layer, 3:4],
                                ALU.subtract).then_inc(S["gin_ready"], 1)

            staged(dve, feed("gin1", gin_in), gin_out("gin1", 0), chain, 1)
            gin_scale(0)
            dve.sem_inc(used["gin2"], 1)
            gin_out("gin2", 1)(0, 0)
            with dve.Fori(0, (GROUPS - 1) // 2 - 1) as i:
                chain.enter(i, 2)
                for half in (1, 0):
                    gin_out("gin2", 1)(2 * i + 2 - half, half)
                chain.leave((GROUPS - 1) // 2 - 1)
            gin_out("gin2", 1)(GROUPS - 2, 1)
            gin_out("gin2", 1)(GROUPS - 1, 0)
            gin_scale(1)
            dve.sem_inc(used["gin3"], 1)

            def gin3_out(g, half):
                dve.wait_ge(mixed["gin3"], g + 1)
                v.tensor_tensor(x_group(g), x_group(g), mix_out(half), ALU.add).then_inc(used["gin3"], 1)
                dve.wait_ge(used["gin3"], g + 2)
                settle(dve)
                norm_stats(lambda i: X[:, ds(g * G + i, 1), :].rearrange("p o f -> p (o f)"), G, g * G)
            chained_groups(gin3_out, 2 * G + 1)

            dve.sem_inc(used["edge"], 1)

            def edge_own(g, half):
                dve.wait_ge(mixed["edge"], g + 1)
                v.tensor_copy(Yn[:, ds(g * G, G), :], mix_out(half, OWN_BANK)).then_inc(used["edge"], 1)
            norm_groups("edge", edge_own)

            def scan_max(c, r, lap, first=False):
                a = r % 2
                dve.wait_ge(starts_here[a], 16 * (2 * lap + r // 2 + 1))
                if not first:
                    dve.wait_ge(S["scanned"], c)
                    if not isinstance(c, int) or c >= 2:
                        dve.wait_ge(S["back_turned"], c - 1)
                dve.wait_ge(S["rows_copied"], c + 1)
                v.tensor_tensor_scan(out=maxT[:, a, :], data0=starts_b[:, a, :], data1=rowsT[:, a, :],
                                     initial=-BIG if first else maxT[:, 1 - a, J * P - 1:J * P],
                                     op0=ALU.min, op1=ALU.max).then_inc(S["scanned"], 1)

            for r in range(RING):
                scan_max(r, r, 0, first=r == 0)
            with dve.Fori(1, LAPS) as lap:
                for r in range(RING):
                    scan_max(lap * RING + r, r, lap)

            def pick(m, half):
                v.tensor_copy(pick_idx[:, half, :], last_i[:, ds(m * LOT, LOT)]).then_inc(S["pick_ready"], 1)

            def edge_out(m, half, turn):
                dve.wait_ge(picked[half], 16 * LOT * (turn + 1))
                xs = X[:, ds(m * LOT, LOT), :]
                up(v.memset(lot_c, 0.0))
                link(v.tensor_tensor(lot_ps, ring[:, half * J:half * J + LOT, 0:D], Yn[:, ds(m * LOT, LOT), :],
                                     ALU.add))
                link(v.scalar_tensor_tensor(out=lot_b, in0=lot_ps, scalar=0.0,
                                            in1=wide(lone[:, ds(m * LOT, LOT)], D),
                                            op0=ALU.mult, op1=ALU.is_equal))
                settle(dve)
                link(v.copy_predicated(lot_c, lot_b.bitcast(i32), lot_ps))
                link(v.tensor_tensor(xs, xs, lot_c, ALU.add))
                norm_stats(lambda i: X[:, ds(m * LOT + i, 1), :].rearrange("p o f -> p (o f)"), LOT, m * LOT)

            dve.wait_ge(S["back_copied"], CHUNKS)
            pick(0, 0)
            with dve.Fori(0, LOTS // 2 - 1) as i:
                chain.enter(i, 2 * (6 + 2 * LOT))
                pick(2 * i + 1, 1)
                edge_out(2 * i, 0, i)
                pick(2 * i + 2, 0)
                edge_out(2 * i + 1, 1, i)
                chain.leave(LOTS // 2 - 1)
            pick(LOTS - 1, 1)
            edge_out(LOTS - 2, 0, LOTS // 2 - 1)
            edge_out(LOTS - 1, 1, LOTS // 2 - 1)

            up(v.memset(acc_wh[:, :, D:D + 1], 1.0))
            norm_groups("gat", lambda g, half: None)

            dve.wait_ge(S["first_words"], 16)
            v.tensor_scalar(idx_ring[:, :, :], pair_ring[:, :, :], DST_SHIFT, None,
                            ALU.logical_shift_right).then_inc(S["first_idx_ready"], 1)
            up(v.memset(Y[:, NODES:ACC_BLOCKS * D], 0.0))
            dve.wait_ge(S["p_turned"], 1)
            v.tensor_copy(lot_a.rearrange("p b f -> p (b f)")[0:BLOCKS, 0:P], ps[0:BLOCKS, SIDE_BANK - 1, 0:P]
                          ).then_inc(S["p_row"], 1)
            dve.wait_ge(S["words_loaded"], 16)
            v.tensor_scalar(words_dst, words, DST_SHIFT, None, ALU.logical_shift_right).then_inc(S["words_ready"], 1)
            dve.wait_ge(S["words_ready"], 1)
            link(v.tensor_scalar(words, words, (1 << DST_SHIFT) - 1, None, ALU.bitwise_and))
            up(v.tensor_copy(key[:, :], words))
            dve.wait_ge(S["sorted_samples"], 16 * 3)
            path_tables(1, (1 << DST_SHIFT) - 1, S["src_tabled"], S["src_tables_mm"])
            chain.done()
            dve.wait_ge(stored["gat"], 16 * GROUPS)
            clear_acc()
            walk_gat()

            pad_at = acc[:, BLOCKS - 1, D:D + 1]
            link(v.scalar_tensor_tensor(out=pad_at, in0=part_f[:, :], scalar=float(N_NODES % P), in1=pad_at,
                                        op0=ALU.is_ge, op1=ALU.add))
            link(v.reciprocal(inv[:, :], acc[:, 0:BLOCKS, D]))
            dve.sem_inc(S["inverses_ready"], 1)
            up(v.tensor_scalar(deg[:, :], inv[:, :], 0.0, None, ALU.mult))

            def gat_out(m, n):
                xs = X[:, ds(m * LOT, LOT), :]
                dve.wait_ge(S["e_ready"], m + 1)
                link(v.scalar_tensor_tensor(out=h_lot[n], in0=h_lot[n], scalar=0.0, in1=e_lot[n],
                                            op0=ALU.max, op1=ALU.add))
                v.scalar_tensor_tensor(out=xs, in0=h_lot[n], scalar=-1.0, in1=xs, op0=ALU.add, op1=ALU.add
                                       ).then_inc(S["lot_out"], 1)
                dve.wait_ge(S["lot_out"], m + 1)
                norm_stats(lambda i: X[:, ds(m * LOT + i, 1), :].rearrange("p o f -> p (o f)"), LOT, m * LOT)

            chain.done()
            for half in range(2):
                at = half * HALF
                with dve.Fori(0, HALF // 2) as i:
                    chain.enter(i, 2 * (2 + 2 * LOT))
                    for n in range(2):
                        gat_out(2 * i + (at + n), (at + n) % 2)
                    chain.leave(HALF // 2)
                gat_out(at + HALF - 1, (at + HALF - 1) % 2)
                blocks = slice(at * LOT, (at + HALF) * LOT)
                norm_scale(blocks)
                link(v.tensor_tensor(rstd[:, blocks], rstd[:, blocks], deg[:, blocks], ALU.add))
                dve.sem_inc(S["scales_ready"], 1)
            norm_lots(HALF, DVE_LOTS)


def kernel(x, src, dst, L0_gnn_W1_l, L0_gnn_b1, L0_gnn_W1_r, L0_gnn_W2_l, L0_gnn_b2, L0_gnn_W2_r,
           L1_gnn_eps, L1_gnn_W1, L1_gnn_b1, L1_gnn_g1, L1_gnn_beta1, L1_gnn_W2, L1_gnn_b2, L1_gnn_g2,
           L1_gnn_beta2, L2_gnn_W, L2_gnn_b, L3_gnn_W, L3_gnn_a):
    import numpy as np
    import concourse.bacc as bacc
    from concourse.bass_utils import run_bass_kernel_spmd as run

    def flat(a):
        return np.ascontiguousarray(np.asarray(a))

    x, src, dst = flat(x), flat(src), flat(dst)
    pad = np.full(EDGES - N_EDGES, PAD_NODE, src.dtype)
    arrays = {
        "x": np.concatenate([x, np.zeros((NODES - N_NODES, D), x.dtype)]),
        "src": np.concatenate([src, pad]),
        "dst_before": np.concatenate([np.full(1, -1, dst.dtype), dst, pad]),
        "W1_l": flat(L0_gnn_W1_l), "W1_r": flat(L0_gnn_W1_r),
        "W2_l": flat(L0_gnn_W2_l), "W2_r": flat(L0_gnn_W2_r),
        "gin_W1t": flat(np.asarray(L1_gnn_W1).T), "gin_W2t": flat(np.asarray(L1_gnn_W2).T),
        "edge_Wt": flat(np.asarray(L2_gnn_W).T),
        "gat_W": flat(L3_gnn_W), "gat_Wt": flat(np.asarray(L3_gnn_W).T),
        "gat_a": flat(np.asarray(L3_gnn_a).reshape(2, D).T),
        "vecs": flat(np.stack([np.asarray(a) for a in (L1_gnn_b1, L1_gnn_g1, L1_gnn_beta1,
                                                       L1_gnn_b2, L1_gnn_g2, L1_gnn_beta2)], axis=1)),
        "biases": flat(np.stack([np.asarray(a) for a in (L0_gnn_b1, L0_gnn_b2, L2_gnn_b)])),
        "eps": flat(L1_gnn_eps),
    }
    nc = bacc.Bacc("TRN2", target_bir_lowering=False, num_devices=1)
    A = {n: nc.dram_tensor("in_" + n, a.shape, mybir.dt.from_np(a.dtype), kind="ExternalInput").ap()
         for n, a in arrays.items()}
    out = nc.dram_tensor("out", (N_NODES, D), mybir.dt.float32, kind="ExternalOutput").ap()
    gnn(nc, A, out)
    r = run(nc, [{"in_" + n: a for n, a in arrays.items()}], core_ids=[0])
    return r.results[0]["out"]
```
